# Optimizing a Trainium2 kernel written in Bass

```python
import numpy as np
import jax
import jax.numpy as jnp

def _softmax(x, axis=-1):
    return jax.nn.softmax(x, axis=axis)

def _gelu(x):
    return jax.nn.gelu(x, approximate=True)

def _silu(x):
    return jax.nn.silu(x)

def _sigmoid(x):
    return jax.nn.sigmoid(x)

def _layernorm(x, axis=-1, eps=1e-05):
    m = jnp.mean(x, axis=axis, keepdims=True)
    v = jnp.var(x, axis=axis, keepdims=True)
    return (x - m) / jnp.sqrt(v + eps)

def _scatter_add(tgt, idx, src, axis=0):
    return tgt.at[idx].add(src)

def _segment_sum(src, seg, n):
    return jax.ops.segment_sum(src, seg, n)
kernel_name = 'mk_gps_d1_gnn_r8_8a74f1'

def setup_inputs(seed: int=0):
    np.random.seed(seed)
    _w = jnp.asarray

    def _rec_inputs():
        import jax
        import jax.numpy as jnp
        _gk = jax.random.key(seed)
        x = -0.0003713 + 1 * jax.random.normal(jax.random.fold_in(_gk, 1), (6250, 256), jnp.float32)
        src = jax.random.randint(jax.random.fold_in(_gk, 2), (200000,), 0, 6250, jnp.int32)
        dst = jnp.minimum((6250 * jax.random.uniform(jax.random.fold_in(_gk, 3), (200000,)) ** 2.0).astype(jnp.int32), 49999)
        _o = jnp.argsort(dst, stable=True)
        src = src[_o]
        dst = dst[_o]
        return (x, src, dst)
    x, src, dst = _rec_inputs()

    def _L0_gnn_setup():
        import jax, jax.numpy as jnp
        import numpy as np
        N = 6250
        E = 100000
        IN_DIM = 256
        HID = 128
        HEADS = 2
        OUT_DIM = 256
        NEG_SLOPE = 0.2

        def gat_layer(x, W, a_l, a_r, b, src, dst, num_nodes):
            heads, d = a_l.shape
            z = (x @ W).reshape(num_nodes, heads, d)
            el = jnp.einsum('nhd,hd->nh', z, a_l)
            er = jnp.einsum('nhd,hd->nh', z, a_r)
            e = el[src] + er[dst]
            e = jnp.where(e > 0, e, NEG_SLOPE * e)
            m = jax.ops.segment_max(e, dst, num_segments=num_nodes)
            ex = jnp.exp(e - m[dst])
            s = jax.ops.segment_sum(ex, dst, num_segments=num_nodes)
            alpha = ex / s[dst]
            msg = z[src] * alpha[:, :, None]
            out = jax.ops.segment_sum(msg, dst, num_segments=num_nodes)
            return out + b[None, :, :]
        key = jax.random.key(seed)
        ks = jax.random.split(key, 12)
        sc1 = 1.0 / np.sqrt(IN_DIM)
        sc2 = 1.0 / np.sqrt(HEADS * HID)
        return {'node_feats': jax.random.normal(ks[0], (N, IN_DIM), dtype=jnp.float32), 'src': jax.random.randint(ks[1], (E,), 0, N, dtype=jnp.int32), 'dst': jax.random.randint(ks[2], (E,), 0, N, dtype=jnp.int32), 'W1': jax.random.normal(ks[3], (IN_DIM, HEADS * HID), dtype=jnp.float32) * sc1, 'al1': jax.random.normal(ks[4], (HEADS, HID), dtype=jnp.float32) * sc1, 'ar1': jax.random.normal(ks[5], (HEADS, HID), dtype=jnp.float32) * sc1, 'b1': jnp.zeros((HEADS, HID), dtype=jnp.float32), 'W2': jax.random.normal(ks[6], (HEADS * HID, OUT_DIM), dtype=jnp.float32) * sc2, 'al2': jax.random.normal(ks[7], (1, OUT_DIM), dtype=jnp.float32) * sc2, 'ar2': jax.random.normal(ks[8], (1, OUT_DIM), dtype=jnp.float32) * sc2, 'b2': jnp.zeros((1, OUT_DIM), dtype=jnp.float32)}
    _L0_gnn_all = _L0_gnn_setup()
    _L0_gnn_in = {k: v for k, v in _L0_gnn_all.items() if k in ('W1', 'al1', 'ar1', 'b1', 'W2', 'al2', 'ar2', 'b2')}
    del _L0_gnn_all

    def _L0_mix_setup():
        import jax, jax.numpy as jnp
        import numpy as np
        A, Bc, Cc = (0.5, 1.0, 1.0)
        H = 8
        EPS = 1e-12

        def _normalize(t):
            n = jnp.linalg.norm(t, axis=-1, keepdims=True)
            return t / jnp.maximum(n, EPS)
        key = jax.random.key(seed)
        ks = jax.random.split(key, 5)
        B, N, C = (8, 256, 256)
        D = C // H
        x = jax.random.normal(ks[0], (B, N, C), dtype=jnp.float32)
        Wqkv = jax.random.normal(ks[1], (3 * H * D, C), dtype=jnp.float32) * 0.02
        bqkv = jnp.zeros((3 * H * D,), dtype=jnp.float32)
        Wproj = jax.random.normal(ks[2], (C, H * D), dtype=jnp.float32) * 0.02
        bproj = jnp.zeros((C,), dtype=jnp.float32)
        temperature = jnp.ones((1, H, 1, 1), dtype=jnp.float32)
        return {'x': x, 'Wqkv': Wqkv, 'bqkv': bqkv, 'Wproj': Wproj, 'bproj': bproj, 'temperature': temperature}
    _L0_mix_all = _L0_mix_setup()
    _L0_mix_in = {k: v for k, v in _L0_mix_all.items() if k in ('Wqkv', 'bqkv', 'Wproj', 'bproj', 'temperature')}
    del _L0_mix_all

    def _L0_ffn_setup():
        import jax, jax.numpy as jnp
        import numpy as np
        BN_EPS = 0.001

        def _bn(h, g, b, m, v):
            return g * (h - m) * jax.lax.rsqrt(v + BN_EPS) + b
        key = jax.random.key(seed)
        ks = jax.random.split(key, 8)
        B, F, Df = (256, 64, 256)
        E, H, D = (8, 256, 256)
        s1 = 1.0 / np.sqrt(Df)
        s2 = 1.0 / np.sqrt(H)
        return {'x': jax.random.normal(ks[0], (B, F, Df), jnp.float32), 'Wr': jax.random.normal(ks[1], (Df, E), jnp.float32) * s1, 'br': jnp.zeros((E,), jnp.float32), 'W1': jax.random.normal(ks[2], (E, Df, H), jnp.float32) * s1, 'b1': jnp.zeros((E, H), jnp.float32), 'g1': jnp.ones((E, H), jnp.float32), 'be1': jnp.zeros((E, H), jnp.float32), 'm1': jnp.zeros((E, H), jnp.float32), 'v1': jnp.ones((E, H), jnp.float32), 'W2': jax.random.normal(ks[3], (E, H, H), jnp.float32) * s2, 'b2': jnp.zeros((E, H), jnp.float32), 'g2': jnp.ones((E, H), jnp.float32), 'be2': jnp.zeros((E, H), jnp.float32), 'm2': jnp.zeros((E, H), jnp.float32), 'v2': jnp.ones((E, H), jnp.float32), 'Wo': jax.random.normal(ks[4], (E, H, D), jnp.float32) * s2, 'bo': jnp.zeros((E, D), jnp.float32)}
    _L0_ffn_all = _L0_ffn_setup()
    _L0_ffn_in = {k: v for k, v in _L0_ffn_all.items() if k in ('Wr', 'br', 'W1', 'b1', 'g1', 'be1', 'm1', 'v1', 'W2', 'b2', 'g2', 'be2', 'm2', 'v2', 'Wo', 'bo')}
    del _L0_ffn_all
    return {'x': x, 'src': src, 'dst': dst, 'L0_gnn_W1': _L0_gnn_in['W1'], 'L0_gnn_al1': _L0_gnn_in['al1'], 'L0_gnn_ar1': _L0_gnn_in['ar1'], 'L0_gnn_b1': _L0_gnn_in['b1'], 'L0_gnn_W2': _L0_gnn_in['W2'], 'L0_gnn_al2': _L0_gnn_in['al2'], 'L0_gnn_ar2': _L0_gnn_in['ar2'], 'L0_gnn_b2': _L0_gnn_in['b2'], 'L0_mix_Wqkv': _L0_mix_in['Wqkv'], 'L0_mix_bqkv': _L0_mix_in['bqkv'], 'L0_mix_Wproj': _L0_mix_in['Wproj'], 'L0_mix_bproj': _L0_mix_in['bproj'], 'L0_mix_temperature': _L0_mix_in['temperature'], 'L0_ffn_Wr': _L0_ffn_in['Wr'], 'L0_ffn_br': _L0_ffn_in['br'], 'L0_ffn_W1': _L0_ffn_in['W1'], 'L0_ffn_b1': _L0_ffn_in['b1'], 'L0_ffn_g1': _L0_ffn_in['g1'], 'L0_ffn_be1': _L0_ffn_in['be1'], 'L0_ffn_m1': _L0_ffn_in['m1'], 'L0_ffn_v1': _L0_ffn_in['v1'], 'L0_ffn_W2': _L0_ffn_in['W2'], 'L0_ffn_b2': _L0_ffn_in['b2'], 'L0_ffn_g2': _L0_ffn_in['g2'], 'L0_ffn_be2': _L0_ffn_in['be2'], 'L0_ffn_m2': _L0_ffn_in['m2'], 'L0_ffn_v2': _L0_ffn_in['v2'], 'L0_ffn_Wo': _L0_ffn_in['Wo'], 'L0_ffn_bo': _L0_ffn_in['bo']}

def reference(x, src, dst, L0_gnn_W1, L0_gnn_al1, L0_gnn_ar1, L0_gnn_b1, L0_gnn_W2, L0_gnn_al2, L0_gnn_ar2, L0_gnn_b2, L0_mix_Wqkv, L0_mix_bqkv, L0_mix_Wproj, L0_mix_bproj, L0_mix_temperature, L0_ffn_Wr, L0_ffn_br, L0_ffn_W1, L0_ffn_b1, L0_ffn_g1, L0_ffn_be1, L0_ffn_m1, L0_ffn_v1, L0_ffn_W2, L0_ffn_b2, L0_ffn_g2, L0_ffn_be2, L0_ffn_m2, L0_ffn_v2, L0_ffn_Wo, L0_ffn_bo):
    import jax
    import jax.numpy as jnp

    def _L0_gnn_ref(node_feats, src, dst, W1, al1, ar1, b1, W2, al2, ar2, b2):
        import jax, jax.numpy as jnp
        import numpy as np
        N = 6250
        E = 100000
        IN_DIM = 256
        HID = 128
        HEADS = 2
        OUT_DIM = 256
        NEG_SLOPE = 0.2

        def gat_layer(x, W, a_l, a_r, b, src, dst, num_nodes):
            heads, d = a_l.shape
            z = (x @ W).reshape(num_nodes, heads, d)
            el = jnp.einsum('nhd,hd->nh', z, a_l)
            er = jnp.einsum('nhd,hd->nh', z, a_r)
            e = el[src] + er[dst]
            e = jnp.where(e > 0, e, NEG_SLOPE * e)
            m = jax.ops.segment_max(e, dst, num_segments=num_nodes)
            ex = jnp.exp(e - m[dst])
            s = jax.ops.segment_sum(ex, dst, num_segments=num_nodes)
            alpha = ex / s[dst]
            msg = z[src] * alpha[:, :, None]
            out = jax.ops.segment_sum(msg, dst, num_segments=num_nodes)
            return out + b[None, :, :]
        h = gat_layer(node_feats, W1, al1, ar1, b1, src, dst, N)
        h = jax.nn.relu(h.reshape(N, HEADS * HID))
        out = gat_layer(h, W2, al2, ar2, b2, src, dst, N)
        return out[:, 0, :]

    def _L0_mix_ref(x, Wqkv, bqkv, Wproj, bproj, temperature):
        import jax, jax.numpy as jnp
        import numpy as np
        A, Bc, Cc = (0.5, 1.0, 1.0)
        H = 8
        EPS = 1e-12

        def _normalize(t):
            n = jnp.linalg.norm(t, axis=-1, keepdims=True)
            return t / jnp.maximum(n, EPS)
        B, N, C = x.shape
        D = C // H
        scale = float(D) ** 0.25
        qkv = (x @ Wqkv.T + bqkv).reshape(B, N, 3, H, D)
        qkv = jnp.transpose(qkv, (2, 0, 3, 1, 4))
        q, k, v = (qkv[0], qkv[1], qkv[2])
        q = q * scale
        v1 = jnp.concatenate([jnp.ones((B, H, N, 1), dtype=v.dtype), v], axis=-1)
        qn = _normalize(q) * (scale * temperature)
        kn = _normalize(k) * scale
        vN = v1 / N
        kv_mod = jnp.einsum('bhni,bhnj,bhne->bhije', kn, kn, vN)
        kv = jnp.einsum('bhnd,bhne->bhde', kn, vN)
        vsum = jnp.sum(vN, axis=-2)[:, :, None, :]
        y = A * jnp.einsum('bhni,bhnj,bhije->bhne', qn, qn, kv_mod) + scale ** 2 * Bc * jnp.einsum('bhnd,bhde->bhne', qn, kv) + scale ** 4 * Cc * vsum
        y_norm, y = (y[..., :1], y[..., 1:])
        y = y / y_norm
        out = jnp.transpose(y, (0, 2, 1, 3)).reshape(B, N, H * D)
        return out @ Wproj.T + bproj

    def _L0_ffn_ref(x, Wr, br, W1, b1, g1, be1, m1, v1, W2, b2, g2, be2, m2, v2, Wo, bo):
        import jax, jax.numpy as jnp
        import numpy as np
        BN_EPS = 0.001

        def _bn(h, g, b, m, v):
            return g * (h - m) * jax.lax.rsqrt(v + BN_EPS) + b
        feat = jnp.mean(x, axis=0)
        w = jax.nn.softmax(feat @ Wr + br, axis=-1)
        h = jnp.einsum('bfd,edh->bfeh', x, W1) + b1
        h = jax.nn.relu(_bn(h, g1, be1, m1, v1))
        h = jnp.einsum('bfeh,ehk->bfek', h, W2) + b2
        h = jax.nn.relu(_bn(h, g2, be2, m2, v2))
        y = jnp.einsum('bfeh,ehd->bfed', h, Wo) + bo
        return jnp.einsum('bfed,fe->bfd', y, w)
    xn = _layernorm(x, axis=-1)
    x = x + _L0_gnn_ref(xn, src, dst, L0_gnn_W1, L0_gnn_al1, L0_gnn_ar1, L0_gnn_b1, L0_gnn_W2, L0_gnn_al2, L0_gnn_ar2, L0_gnn_b2) + _L0_mix_ref(xn[None], L0_mix_Wqkv, L0_mix_bqkv, L0_mix_Wproj, L0_mix_bproj, L0_mix_temperature)[0]
    x = x + _L0_ffn_ref(_layernorm(x, axis=-1)[None], L0_ffn_Wr, L0_ffn_br, L0_ffn_W1, L0_ffn_b1, L0_ffn_g1, L0_ffn_be1, L0_ffn_m1, L0_ffn_v1, L0_ffn_W2, L0_ffn_b2, L0_ffn_g2, L0_ffn_be2, L0_ffn_m2, L0_ffn_v2, L0_ffn_Wo, L0_ffn_bo)[0]
    return x

_drawn_inputs = setup_inputs


def setup_inputs(seed=0):
    import zlib

    import numpy as np

    out = dict(_drawn_inputs(seed))
    spreads = {'L0_gnn_b1': (0.0, 0.1),
     'L0_gnn_b2': (0.0, 0.1),
     'L0_mix_bqkv': (0.0, 0.269),
     'L0_mix_bproj': (0.0, 0.1),
     'L0_mix_temperature': (1.0, 0.6),
     'L0_ffn_br': (0.0, 0.1),
     'L0_ffn_b1': (0.0, 0.325),
     'L0_ffn_g1': (1.0, 0.2),
     'L0_ffn_be1': (0.0, 0.336),
     'L0_ffn_m1': (0.0, 0.326),
     'L0_ffn_v1': (1.0, 0.6),
     'L0_ffn_b2': (0.0, 0.1),
     'L0_ffn_g2': (1.0, 0.2),
     'L0_ffn_be2': (0.0, 0.1),
     'L0_ffn_m2': (0.0, 0.1),
     'L0_ffn_v2': (1.0, 0.555),
     'L0_ffn_bo': (0.0, 0.1)}
    factors = {'L0_gnn_ar1': 25.831, 'L0_gnn_al2': 8.0, 'L0_gnn_ar2': 38.145, 'L0_mix_Wqkv': 28.725}
    for name, (base, spread) in spreads.items():
        noise = np.random.default_rng([zlib.crc32(name.encode()), seed]).standard_normal(out[name].shape)
        drawn = base * np.exp(spread * noise) if base else spread * noise
        out[name] = jnp.asarray(drawn.astype(out[name].dtype))
    for name, factor in factors.items():
        out[name] = (out[name] * factor).astype(out[name].dtype)
    return out
```

```python
from contextlib import ExitStack, contextmanager

import concourse.bass as bass
from concourse import mybir

ALU = mybir.AluOpType
ACT = mybir.ActivationFunctionType
F32 = mybir.dt.float32
BF16 = mybir.dt.bfloat16
I32 = mybir.dt.int32
AX_X = mybir.AxisListType.X

P = 128
N, C = 6250, 256
E = 200000
NT = 50
FULL = N // P
REST = N - FULL * P
PAIRS = NT // 2
HM, DM = 8, 32
MAIN = 16 * DM
QUADS = HM * MAIN // P
FEAT = HM * MAIN + 2 * HM * DM
CH = FEAT // P
V1 = DM + 1
COLS = 1664
JT = COLS // P
ET = (E + P - 1) // P
ETP = COLS
NBLK = (N + P - 1) // P
STEPS = ET + NBLK
UA = 8
AIT = (ET + UA - 1) // UA
UB = 4
BIT = (STEPS + UB - 1) // UB
NX = 8
EPS_LN, EPS_BN, EPS_NORM = 1e-5, 1e-3, 1e-12
SC = float(DM) ** 0.25
BIG = 1.0e30


class Count:

    def __init__(self, eng, sem):
        self.eng, self.sem, self.total, self.n, self.reg = eng, sem, 0, 0, 0

    def inc(self, ins):
        ins.then_inc(self.sem, 1)
        self.n += 1

    def wait(self):
        self.eng.wait_ge(self.sem, self.reg + (self.total + self.n))

    def link(self, ins):
        self.inc(ins)
        self.wait()

    def enter(self, i, per_round):
        self.total, self.n, self.per, self.reg = self.total + self.n, 0, per_round, i * per_round

    def leave(self, rounds):
        assert self.n == self.per, (self.n, self.per)
        self.total, self.n, self.reg = self.total + rounds * self.per, 0, 0


@contextmanager
def phase_semaphores(nc):
    held = []

    def sem(name):
        held.append(nc.alloc_semaphore(name))
        return held[-1]

    yield sem
    nc.clear_and_free_semaphores(held)
    nc.all_engine_barrier()


def bcast(ap, count):
    return bass.AP(ap.tensor, ap.offset, [list(d) for d in ap.ap] + [[0, count]])



def build(nc, x, src, dst, W1, al1, ar1, b1, W2, al2, ar2, b2, Wqkv, bqkv, Wproj, bproj, temp,
          Wr, br, fW1, fb1, fg1, fbe1, fm1, fv1, fW2, fb2, fg2, fbe2, fm2, fv2, fWo, fbo, out):
    ctx = ExitStack()
    with ctx:
        def sb(name, shape, dt=F32, at=None):
            return (at or ctx).enter_context(nc.sbuf_tensor(name, shape, dt))

        def pb(name, shape, at, dt=F32):
            return at.enter_context(nc.psum_tensor(name, shape, dt))

        def sem(name):
            return ctx.enter_context(nc.semaphore(name))

        def dram(name, shape, dt):
            return nc.dram_tensor(name, shape, dt, kind="Internal").ap()

        s_gate = {e: sem(f"gate_{e}") for e in ("pool", "act", "dve", "pe", "sp")}

        def gated(eng, name, s, value):
            eng.wait_ge(s, value)
            eng.sem_inc(s_gate[name], 1)

        ztab = dram("ztab", (NT * P, C), F32)

        X = sb("X", [P, NT, C])
        ident = sb("ident", [P, P])
        iota = sb("iota", [P, P])
        elr = sb("elr", [P, NT, 4])

        constants(nc, ctx, sb, pb, sem, ident, iota, X, x)
        project_and_mix(nc, sb, pb, sem, gated, ident, X, elr, ztab,
                        W1, al1, ar1, b2, Wqkv, bqkv, Wproj, bproj, temp)
        attention_layers(nc, sb, pb, sem, dram, gated, ident, iota, X, elr, ztab, src, dst, b1, W2, al2, ar2)
        experts(nc, sb, pb, sem, gated, ident, X, out, Wr, br, fW1, fb1, fg1, fbe1, fm1, fv1,
                fW2, fb2, fg2, fbe2, fm2, fv2, fWo, fbo)


def constants(nc, ctx, sb, pb, sem, ident, iota, X, x):
    s_pad, s_x, s_id = sem("s_pad"), sem("s_x"), sem("s_id")
    tmp = ctx.enter_context(nc.sbuf_tensor("iota_i", [P, P], I32))
    with nc.Block() as block:
        @block.sync
        def _(sp):
            sp.dma_start(X[:, 0:FULL, :], x[0:FULL * P, :].rearrange("(k p) c -> p k c", p=P)).then_inc(s_x, 16)
            sp.wait_ge(s_pad, 1)
            sp.dma_start(X[0:REST, FULL, :], x[FULL * P:N, :]).then_inc(s_x, 16)
            sp.wait_ge(s_x, 32)

        @block.gpsimd
        def _(pool):
            pool.memset(X[:, FULL:NT, :], 0.0).then_inc(s_pad, 1)
            pool.memset(ident[:, :], 0.0).then_inc(s_id, 1)
            pool.iota(tmp[:, :], pattern=[[1, P]], base=0, channel_multiplier=0).then_inc(s_id, 1)
            pool.wait_ge(s_id, 2)
            pool.affine_select(out=ident[:, :], in_=ident[:, :], compare_op=ALU.not_equal, fill=1.0,
                               base=0, pattern=[[-1, P]], channel_multiplier=1).then_inc(s_id, 1)
            pool.tensor_copy(iota[:, :], tmp[:, :]).then_inc(s_id, 1)
            pool.wait_ge(s_id, 4)


def layer_norm(nc, sem, name, X, XN, sq, sm, rs):
    s_dve, s_var, s_root = sem(name + "_dve"), sem(name + "_var"), sem(name + "_root")
    with nc.Block() as block:
        @block.vector
        def _(dve):
            ch = Count(dve, s_dve)
            centre_and_square(dve, ch, X, XN, sq, sm, rs)
            dve.sem_inc(s_var, 1)
            dve.wait_ge(s_root, 1)
            ch.link(dve.reciprocal(rs[:, :], sm[:, :]))
            dve.sem_inc(s_var, 1)

        @block.scalar
        def _(act):
            act.wait_ge(s_var, 1)
            act.activation(sm[:, :], rs[:, :], ACT.Sqrt).then_inc(s_root, 1)


def centre_and_square(dve, ch, X, XN, sq, sm, rs):
    ch.link(dve.tensor_reduce(sm[:, :], X[:, :, :], AX_X, ALU.add))
    ch.link(dve.tensor_scalar(sm[:, :], sm[:, :], 1.0 / C, None, ALU.mult))
    ch.link(dve.tensor_tensor(XN[:, :, :], X[:, :, :], bcast(sm[:, :], C), ALU.subtract))
    for c in range(NT // 10):
        part = XN[:, 10 * c:10 * c + 10, :]
        ch.link(dve.tensor_tensor(sq[:, :, :], part, part, ALU.mult))
        ch.link(dve.tensor_reduce(rs[:, 10 * c:10 * c + 10], sq[:, :, :], AX_X, ALU.add))
    ch.link(dve.tensor_scalar(rs[:, :], rs[:, :], 1.0 / C, EPS_LN, ALU.mult, ALU.add))


def project_and_mix(nc, sb, pb, sem, gated, ident, X, elr, ztab, W1, al1, ar1, b2, Wqkv, bqkv, Wproj, bproj, temp):
    ctx = ExitStack()
    with ctx:
        sem = ctx.enter_context(phase_semaphores(nc))
        t = lambda name, shape, dt=F32: sb(name, shape, dt, at=ctx)
        QN = t("QN", [P, NT, C])
        KVS = t("KVS", [P, QUADS, V1])
        KV4 = t("KV4", [P, 4, 4 * V1])
        VS = t("VS", [P, HM * V1])
        wproj = t("wproj", [P, 2, C])
        bsum = t("bsum", [P, C])
        w8 = t("w8", [P, 2])
        head_of = t("head_of", [P, 4])
        c1 = ExitStack()
        with c1:
            t = lambda name, shape, dt=F32: sb(name, shape, dt, at=c1)
            wz = t("wz", [P, 2, C + 4])
            wqkv = t("wqkv", [P, 2, 3 * C])
            wnat = t("wnat", [P, 8, C])
            avec = t("avec", [P, 2, C])
            prod = t("prod", [P, C])
            bq = t("bq", [P, 3 * C])
            tmpb = t("tmpb", [P, 2, C])
            tempb = t("tempb", [P, HM])
            fac = t("fac", [P, 2, HM])
            sq2 = t("sq2", [P, 2, HM])
            mask = t("mask", [P, NT])
            sq = t("sq", [P, 10, C])
            sm = t("sm", [P, NT])
            rs = t("rs", [P, NT])
            xs = t("xs", [P, 2, C])
            xT = t("xT", [P, 2, 2, P])
            zs = t("zs", [P, 2, C])
            qkv = t("qkv", [P, 3 * C])
            sqk = t("sqk", [P, 2 * C])
            nrm = t("nrm", [P, 2, HM])
            rt = t("rt", [P, 2 * HM])
            kn = t("kn", [P, HM, 2 * DM])
            v1 = t("v1", [P, 2, HM, V1])
            KF = t("KF", [P, 2, FEAT])
            ones = t("ones", [P, P])
            zero = t("zero", [P, 512])
            pKV = [pb(f"pKV{n}", [P, 512], c1) for n in range(4)]
            pT = pb("pT", [P, 2, P], c1)
            pZ = pb("pZ", [P, 512], c1)
            pQ = pb("pQ", [P, 1024], c1)
            s_w, s_nw, s_cst = sem("p_w"), sem("p_natural"), sem("p_const")
            s_wt, s_wc = sem("p_wT"), sem("p_wT_copied")
            s_dve, s_xs, s_t, s_xt = sem("p_dve"), sem("p_xs"), sem("p_T"), sem("p_xT")
            s_n2, s_rt, s_z, s_q, s_zc, s_elr, s_qv, s_kf, s_kv, s_init = [sem("p_" + n) for n in (
                "norm2", "norm", "z", "qkv", "z_copied", "elr", "qkv_read", "features", "kv", "init")]
            s_zd = [sem(f"p_z_stored{u}") for u in range(2)]

            def kv_place(ch):
                if ch < QUADS:
                    n, c = (ch // 15, (ch % 15) * V1) if ch < 30 else (2, (ch - 30) * V1)
                    return pKV[n][:, c:c + V1]
                g = ch - QUADS
                n, c = (2, 2 * V1 + g * 4 * V1) if g < 3 else (3, 0)
                return pKV[n][:, c:c + 4 * V1]
            VSUM = pKV[3][:, 4 * V1:4 * V1 + HM * V1]

            layer_norm(nc, sem, "ln1", X, QN, sq, sm, rs)
            with nc.Block() as block:
                @block.sync
                def _(sp):
                    sp.dma_start(wz[:, :, 0:C], W1.rearrange("(a p) n -> p a n", p=P)).then_inc(s_w, 16)
                    sp.dma_start(avec[:, 0, :], al1.rearrange("h d -> (h d)").partition_broadcast(P)).then_inc(s_w, 16)
                    sp.dma_start(avec[:, 1, :], ar1.rearrange("h d -> (h d)").partition_broadcast(P)).then_inc(s_w, 16)
                    sp.dma_start(bq[:, :], bqkv.partition_broadcast(P)).then_inc(s_w, 16)
                    sp.dma_start(tmpb[:, 0, :], bproj.partition_broadcast(P)).then_inc(s_w, 16)
                    sp.dma_start(tmpb[:, 1, :], b2.rearrange("h d -> (h d)").partition_broadcast(P)).then_inc(s_w, 16)
                    sp.dma_start(tempb[:, :], temp.rearrange("a h b c -> (a h b c)").partition_broadcast(P)).then_inc(s_w, 16)
                    sp.dma_start(wnat[:, 0:6, :], Wqkv.rearrange("(a p) c -> p a c", p=P)).then_inc(s_nw, 16)
                    sp.dma_start(wnat[:, 6:8, :], Wproj.rearrange("(a p) c -> p a c", p=P)).then_inc(s_nw, 16)
                    sp.wait_ge(s_w, 7 * 16)
                    sp.wait_ge(s_nw, 32)

                    with sp.Fori(0, PAIRS) as i:
                        for u in range(2):
                            sp.wait_ge(s_zc, i * 2 + (u + 1))
                            sp.dma_start(ztab[bass.ds(i * (2 * P) + u * P, P), :], zs[:, u, :]).then_inc(s_zd[u], 16)
                    for u in range(2):
                        sp.wait_ge(s_zd[u], 16 + PAIRS * 16)

                @block.gpsimd
                def _(pool):
                    pool.memset(ones[:, :], 1.0).then_inc(s_cst, 1)
                    pool.memset(zero[:, :], 0.0).then_inc(s_cst, 1)
                    pool.memset(mask[:, :], 1.0 / N).then_inc(s_cst, 1)
                    pool.memset(w8[:, 0:1], 1.0).then_inc(s_cst, 1)
                    pool.wait_ge(s_cst, 4)
                    pool.memset(w8[0:DM, 0:1], 0.5).then_inc(s_cst, 1)
                    pool.wait_ge(s_cst, 5)
                    pool.affine_select(out=mask[:, :], in_=mask[:, :], compare_op=ALU.is_gt, fill=0.0,
                                       base=N, pattern=[[-P, NT]], channel_multiplier=-1).then_inc(s_cst, 1)
                    pool.memset(head_of[:, :], 0.0).then_inc(s_cst, 1)
                    pool.wait_ge(s_cst, 7)
                    for h in range(4):
                        pool.memset(head_of[DM * h:DM * h + DM, h:h + 1], 1.0).then_inc(s_cst, 1)
                    pool.wait_ge(s_cst, 11)

                @block.vector
                def _(dve):
                    ch = Count(dve, s_dve)
                    dve.wait_ge(s_w, 7 * 16)
                    for c in range(2):
                        for side in range(2):
                            ch.link(dve.tensor_tensor(prod[:, :], wz[:, c, 0:C], avec[:, side, :], ALU.mult))
                            ch.link(dve.tensor_reduce(wz[:, c, C + 2 * side:C + 2 * side + 2],
                                                      prod[:, :].rearrange("p (h d) -> p h d", h=2), AX_X, ALU.add))
                    ch.link(dve.tensor_tensor(bsum[:, :], tmpb[:, 0, :], tmpb[:, 1, :], ALU.add))
                    ch.link(dve.tensor_scalar(fac[:, 0, :], tempb[:, :], SC * SC, None, ALU.mult))
                    ch.link(dve.memset(fac[:, 1, :], SC))
                    ch.link(dve.memset(sq2[:, 0, :], SC * SC))
                    ch.link(dve.memset(sq2[:, 1, :], 1.0))
                    for n in range(8):
                        dve.wait_ge(s_wt, n + 1)
                        to = wqkv[:, :, n * P:n * P + P] if n < 6 else wproj[:, :, (n - 6) * P:(n - 5) * P]
                        dve.tensor_copy(to, pT[:, :, :]).then_inc(s_wc, 1)
                    dve.wait_ge(s_cst, 11)

                    with dve.Fori(0, PAIRS) as i:
                        ch.enter(i, 2 * 17)
                        for u in range(2):
                            k = i * 2 + u
                            dve.wait_ge(s_t, i * 2 + (u + 1))
                            ch.link(dve.tensor_scalar(xs[:, u, :], QN[:, bass.ds(k, 1), :].rearrange("p a c -> p (a c)"),
                                                      rs[:, bass.ds(k, 1)], None, ALU.mult))
                            dve.sem_inc(s_xs, 1)
                            dve.wait_ge(s_zc, i * 2 + (u + 1))
                            ch.link(dve.tensor_scalar(elr[:, bass.ds(k, 1), :].rearrange("p a c -> p (a c)"),
                                                      pZ[:, C:C + 4], 1.0, None, ALU.mult))
                            dve.sem_inc(s_elr, 1)
                            dve.wait_ge(s_q, i * 2 + (u + 1))
                            ch.link(dve.tensor_tensor(qkv[:, :], pQ[:, 0:3 * C], bq[:, :], ALU.add))
                            dve.sem_inc(s_qv, 1)
                            ch.link(dve.tensor_tensor(sqk[:, :], qkv[:, 0:2 * C], qkv[:, 0:2 * C], ALU.mult))
                            flat = nrm[:, :, :].rearrange("p a h -> p (a h)")
                            ch.link(dve.tensor_reduce(flat, sqk[:, :].rearrange("p (g d) -> p g d", d=DM), AX_X, ALU.add))
                            ch.link(dve.tensor_tensor(nrm[:, :, :], nrm[:, :, :], sq2[:, :, :], ALU.mult))
                            ch.link(dve.tensor_scalar(flat, flat, EPS_NORM ** 2, None, ALU.max))
                            dve.sem_inc(s_n2, 1)
                            dve.wait_ge(s_rt, i * 2 + (u + 1))
                            ch.link(dve.reciprocal(flat, rt[:, :]))
                            ch.link(dve.tensor_tensor(nrm[:, :, :], nrm[:, :, :], fac[:, :, :], ALU.mult))
                            ch.inc(dve.tensor_tensor(QN[:, bass.ds(k, 1), :].rearrange("p a (h d) -> p (a h) d", h=HM),
                                                     qkv[:, 0:C].rearrange("p (h d) -> p h d", h=HM),
                                                     bcast(nrm[:, 0, :], DM), ALU.mult))
                            for half in range(2):
                                ch.inc(dve.tensor_tensor(kn[:, :, DM * half:DM * half + DM],
                                                         qkv[:, C:2 * C].rearrange("p (h d) -> p h d", h=HM),
                                                         bcast(nrm[:, 1, :], DM), ALU.mult))
                            dve.wait_ge(s_kv, i * 2 + (u + 1))
                            ch.inc(dve.tensor_scalar(v1[:, u, :, 1:V1], qkv[:, 2 * C:3 * C].rearrange("p (h d) -> p h d", h=HM),
                                                     mask[:, bass.ds(k, 1)], None, ALU.mult))
                            ch.link(dve.tensor_scalar(v1[:, u, :, 0:1], bcast(ones[:, 0:HM], 1),
                                                      mask[:, bass.ds(k, 1)], None, ALU.mult))
                            ch.link(features(dve, KF[:, u, :], kn, ch))
                            dve.sem_inc(s_kf, 1)
                        ch.leave(PAIRS)
                    dve.wait_ge(s_kv, NT + 2)
                    for c in range(QUADS):
                        w = w8[:, 0:1] if c % 4 == 0 else 1.0
                        ch.inc(dve.tensor_scalar(KVS[:, c, :], kv_place(c), w, None, ALU.mult))
                    for g in range(4):
                        w = 0.5 if g < 2 else SC * SC
                        ch.inc(dve.scalar_tensor_tensor(out=KV4[:, g, :].rearrange("p (h e) -> p h e", h=4),
                                                        in0=kv_place(QUADS + g).rearrange("p (h e) -> p h e", h=4),
                                                        scalar=w, in1=bcast(head_of[:, :], V1),
                                                        op0=ALU.mult, op1=ALU.mult))
                    ch.inc(dve.tensor_scalar(VS[:, :], VSUM, SC ** 4, None, ALU.mult))
                    gated(dve, "dve", s_dve, ch.total + ch.n)

                @block.tensor
                def _(pe):
                    pe.wait_ge(s_nw, 32)
                    for n in range(8):
                        if n:
                            pe.wait_ge(s_wc, n)
                        for c in range(2):
                            mm = pe.transpose(pT[:, c, :], wnat[:, n, c * P:c * P + P], ident[:, :])
                        mm.then_inc(s_wt, 1)
                    pe.wait_ge(s_wc, 8)
                    pe.wait_ge(s_cst, 5)
                    for n in range(4):
                        mm = pe.matmul(pKV[n][:, :], zero[:, 0:P], zero[:, :], start=True, stop=False,
                                       skip_group_check=True)
                    mm.then_inc(s_init, 1)
                    pe.wait_ge(s_init, 1)
                    pe.sem_inc(s_kv, 2)
                    pe.sem_inc(s_t, 2)

                    def key_side(i, u):
                        pe.wait_ge(s_kf, i * 2 + (u + 1))
                        for c in range(CH):
                            if c < QUADS:
                                rhs = v1[:, u, c // 4, :]
                            else:
                                rhs = v1[:, u, 4 * (c % 2):4 * (c % 2) + 4, :].rearrange("p h e -> p (h e)")
                            pe.matmul(kv_place(c), KF[:, u, c * P:(c + 1) * P], rhs, start=False, stop=False,
                                      skip_group_check=True)
                        pe.matmul(VSUM, ones[:, :], v1[:, u, :, :].rearrange("p h e -> p (h e)"),
                                  start=False, stop=False, skip_group_check=True).then_inc(s_kv, 1)

                    with pe.Fori(0, PAIRS) as i:
                        for u in range(2):
                            pe.wait_ge(s_xs, i * 2 + (u + 1))
                            for c in range(2):
                                mm = pe.transpose(pT[:, c, :], xs[:, u, c * P:c * P + P], ident[:, :])
                            mm.then_inc(s_t, 1)
                            pe.wait_ge(s_xt, i * 2 + (u + 1))
                            if u:
                                pe.wait_ge(s_zc, i * 2 + 1)
                                gated(pe, "pe", s_elr, i * 2 + 1)
                            for c in range(2):
                                mm = pe.matmul(pZ[:, 0:C + 4], xT[:, u, c, :], wz[:, c, :], start=c == 0, stop=c == 1)
                            mm.then_inc(s_z, 1)
                            if u:
                                pe.wait_ge(s_qv, i * 2 + 1)
                            for a, b in ((0, 512), (512, 768)):
                                for c in range(2):
                                    mm = pe.matmul(pQ[:, a:b], xT[:, u, c, :], wqkv[:, c, a:b], start=c == 0, stop=c == 1)
                            mm.then_inc(s_q, 1)
                            if u:
                                key_side(i, 0)
                        key_side(i, 1)
                        gated(pe, "pe", s_zc, i * 2 + 2)
                        gated(pe, "pe", s_elr, i * 2 + 2)
                        gated(pe, "pe", s_qv, i * 2 + 2)

                @block.scalar
                def _(act):
                    for u in range(2):
                        act.sem_inc(s_zd[u], 16)
                    with act.Fori(0, PAIRS) as i:
                        for u in range(2):
                            act.wait_ge(s_t, i * 2 + (2 + u + 1))
                            act.copy(xT[:, u, :, :], pT[:, :, :]).then_inc(s_xt, 1)
                            act.wait_ge(s_z, i * 2 + (u + 1))
                            gated(act, "act", s_zd[u], i * 16 + 16)
                            act.copy(zs[:, u, :], pZ[:, 0:C]).then_inc(s_zc, 1)
                            act.wait_ge(s_n2, i * 2 + (u + 1))
                            act.activation(rt[:, :], nrm[:, :, :].rearrange("p a h -> p (a h)"), ACT.Sqrt).then_inc(s_rt, 1)
        c1.close()
        query_side(nc, sb, pb, sem, gated, ident, X, QN, KVS, KV4, VS, wproj, bsum)


def features(eng, out, kn, ch):
    base = kn[:, :, :]
    part = list(base.ap[0])
    same = bass.AP(base.tensor, base.offset, [part, [2 * DM, HM], [0, 16], [1, DM]])
    window = bass.AP(base.tensor, base.offset, [part, [2 * DM, HM], [1, 16], [1, DM]])
    main = out[:, 0:HM * MAIN].rearrange("p (h d i) -> p h d i", h=HM, d=16)
    ch.inc(eng.tensor_tensor(main, same, window, ALU.mult))
    rest = out[:, HM * MAIN:HM * MAIN + HM * DM].rearrange("p (h i) -> p h i", h=HM)
    ch.inc(eng.tensor_tensor(rest, kn[:, :, 0:DM], kn[:, :, 16:16 + DM], ALU.mult))
    return eng.tensor_copy(out[:, HM * MAIN + HM * DM:FEAT].rearrange("p (h i) -> p h i", h=HM), kn[:, :, 0:DM])


def query_side(nc, sb, pb, sem, gated, ident, X, QN, KVS, KV4, VS, wproj, bsum):
    ctx = ExitStack()
    with ctx:
        sem = ctx.enter_context(phase_semaphores(nc))
        t = lambda name, shape: sb(name, shape, F32, at=ctx)
        q2 = t("q2", [P, HM, 2 * DM])
        QF = t("QF", [P, 2, FEAT])
        QT = t("QT", [P, 2, CH, P])
        rec = t("rec", [P, 2, HM])
        yo = t("yo", [P, 2, C])
        yT = t("yT", [P, 2, 2, P])
        ot = t("ot", [P, C])
        pT = [pb(f"qT{n}", [P, 4, P], ctx) for n in range(3)]
        pY = [pb(f"qY{n}", [P, HM, V1], ctx) for n in range(2)]
        pYT = [pb(f"qYT{n}", [P, 2, P], ctx) for n in range(2)]
        pO = pb("qO", [P, C], ctx)
        s_dve, s_f, s_t, s_tc, s_y, s_yo, s_yt, s_yc, s_o, s_or = [sem("q_" + n) for n in (
            "dve", "features", "T", "T_copied", "y", "y_divided", "yT", "yT_copied", "projected", "projection_read")]
        G = CH // 4
        with nc.Block() as block:
            @block.vector
            def _(dve):
                ch = Count(dve, s_dve)
                with dve.Fori(0, PAIRS) as i:
                    ch.enter(i, 2 * 9)
                    for u in range(2):
                        row = QN[:, bass.ds(i * 2 + u, 1), :].rearrange("p a (h d) -> p (a h) d", h=HM)
                        for half in range(2):
                            ch.inc(dve.tensor_scalar(q2[:, :, DM * half:DM * half + DM], row, 1.0, None, ALU.mult))
                        ch.wait()
                        gated(dve, "dve", s_t, i * (2 * G) + (G * u + G))
                        ch.link(features(dve, QF[:, u, :], q2, ch))
                        dve.sem_inc(s_f, 1)
                    for u in range(2):
                        dve.wait_ge(s_y, i * 2 + (u + 1))
                        ch.link(dve.reciprocal(rec[:, u, :], pY[u][:, :, 0:1].rearrange("p h e -> p (h e)")))
                        ch.link(dve.tensor_tensor(yo[:, u, :].rearrange("p (h d) -> p h d", h=HM), pY[u][:, :, 1:V1],
                                                  bcast(rec[:, u, :], DM), ALU.mult))
                        dve.sem_inc(s_yo, 1)
                    for u in range(2):
                        xk = X[:, bass.ds(i * 2 + u, 1), :].rearrange("p a c -> p (a c)")
                        dve.wait_ge(s_o, i * 2 + (u + 1))
                        ch.link(dve.tensor_tensor(ot[:, :], pO[:, :], bsum[:, :], ALU.add))
                        dve.sem_inc(s_or, 1)
                        ch.link(dve.tensor_tensor(xk, xk, ot[:, :], ALU.add))
                ch.leave(PAIRS)

            @block.tensor
            def _(pe):
                pe.sem_inc(s_t, 2 * G)
                pe.sem_inc(s_or, 1)
                pe.sem_inc(s_tc, 3)
                with pe.Fori(0, PAIRS) as i:
                    for u in range(2):
                        pe.wait_ge(s_f, i * 2 + (u + 1))
                        for g in range(G):
                            pe.wait_ge(s_tc, i * (2 * G) + (u * G + g + 1))
                            for c in range(4 * g, 4 * g + 4):
                                mm = pe.transpose(pT[(u * G + g) % 3][:, c % 4, :], QF[:, u, c * P:(c + 1) * P], ident[:, :])
                            mm.then_inc(s_t, 1)
                    for u in range(2):
                        pe.wait_ge(s_tc, i * (2 * G) + (3 + u * G + G))
                        flat = pY[u][:, :, :].rearrange("p h e -> p (h e)")
                        pe.matmul(flat, ident[:, :], VS[:, :], start=True, stop=False, skip_group_check=True)
                        for c in range(CH):
                            if c < QUADS:
                                h, nh, rhs = c // 4, 1, KVS[:, c, :]
                            else:
                                h, nh, rhs = 4 * (c % 2), 4, KV4[:, c - QUADS, :]
                            mm = pe.matmul(flat[:, h * V1:(h + nh) * V1], QT[:, u, c, :], rhs, start=False,
                                           stop=c == CH - 1, skip_group_check=True)
                        mm.then_inc(s_y, 1)
                    for u in range(2):
                        pe.wait_ge(s_yo, i * 2 + (u + 1))
                        for c in range(2):
                            mm = pe.transpose(pYT[u][:, c, :], yo[:, u, c * P:c * P + P], ident[:, :])
                        mm.then_inc(s_yt, 1)
                    for u in range(2):
                        pe.wait_ge(s_yc, i * 2 + (u + 1))
                        gated(pe, "pe", s_or, i * 2 + (u + 1))
                        for c in range(2):
                            mm = pe.matmul(pO[:, :], yT[:, u, c, :], wproj[:, c, :], start=c == 0, stop=c == 1)
                        mm.then_inc(s_o, 1)

            @block.scalar
            def _(act):
                with act.Fori(0, PAIRS) as i:
                    for u in range(2):
                        for g in range(G):
                            act.wait_ge(s_t, i * (2 * G) + (2 * G + u * G + g + 1))
                            act.copy(QT[:, u, 4 * g:4 * g + 4, :], pT[(u * G + g) % 3][:, :, :]).then_inc(s_tc, 1)
                    for u in range(2):
                        act.wait_ge(s_yt, i * 2 + (u + 1))
                        act.copy(yT[:, u, :, :], pYT[u][:, :, :]).then_inc(s_yc, 1)


def to_tiles(pe, mm_sem, rd_sem, base, pt, ident, src):
    for j in range(JT):
        if base + j:
            pe.wait_ge(rd_sem, base + j)
        pe.transpose(pt[:, :], src[:, j * P:j * P + P], ident[:, :]).then_inc(mm_sem, 1)


def prepare_edges(nc, sb, pb, sem, ident, src, dst, D, T):
    ctx = ExitStack()
    with ctx:
        sem = ctx.enter_context(phase_semaphores(nc))
        t = lambda name, shape, dt=F32: sb(name, shape, dt, at=ctx)
        si, di = t("e_src", [P, COLS], I32), t("e_dst", [P, COLS], I32)
        wi, wf, wb = t("e_int", [P, COLS], I32), t("e_f32", [P, COLS]), t("e_b16", [P, COLS], BF16)
        wb2 = t("e_b16b", [P, COLS], BF16)
        sf, df = t("e_srcf", [P, COLS]), t("e_dstf", [P, COLS])
        lo2 = t("e_lo2", [P, COLS])
        dx = t("e_dx", [P, COLS + 2])
        keyB = t("e_keyB", [P, COLS])
        ends = t("e_ends", [1, 2])
        tile_i, tile_f = t("e_ti", [P, JT], I32), t("e_tf", [P, JT])
        step_i, step_f = t("e_si", [P, JT], I32), t("e_sf", [P, JT])
        key, tf, bf, b128 = t("e_key", [P, JT]), t("e_t", [P, JT]), t("e_b", [P, JT]), t("e_b128", [P, JT])
        brow_f, brow_i = t("e_brf", [JT, P]), t("e_bri", [JT, P], I32)
        pt = pb("e_pt", [P, P], ctx)
        s_pad, s_ld, s_w, s_b, s_dve, s_io, s_k, s_kb, s_mm, s_rd, s_br = [sem("e_" + n) for n in (
            "pad", "loaded", "written", "windowed", "dve", "iota", "keys_ready", "keys", "T", "T_read", "brow")]
        rows = E // COLS
        left = E - rows * COLS
        with nc.Block() as block:
            @block.gpsimd
            def _(pool):
                pool.memset(si[:, :], 0).then_inc(s_pad, 1)
                pool.memset(di[:, :], N - 1).then_inc(s_pad, 1)
                pool.iota(tile_i[:, :], pattern=[[1, JT]], base=0, channel_multiplier=JT).then_inc(s_io, 1)
                pool.iota(step_i[:, :], pattern=[[P, JT]], base=0, channel_multiplier=1).then_inc(s_io, 1)
                pool.wait_ge(s_io, 2)

            @block.sync
            def _(sp):
                sp.wait_ge(s_pad, 2)
                for a, b in ((src, si), (dst, di)):
                    sp.dma_start(b[0:rows, :], a[0:rows * COLS].rearrange("(p c) -> p c", c=COLS)).then_inc(s_ld, 16)
                    sp.dma_start(b[rows:rows + 1, 0:left], a[rows * COLS:E].rearrange("(a c) -> a c", a=1)).then_inc(s_ld, 16)
                sp.wait_ge(s_k, 1)
                for a, b in ((D["src_hi"], wb), (D["dst_hi"], wb2), (D["src"], sf), (D["dst"], df)):
                    sp.dma_start(a.rearrange("(p c) -> p c", c=COLS), b[:, :]).then_inc(s_w, 16)
                sp.dma_start(D["window"][1:1 + P * COLS].rearrange("(p c) -> p c", c=COLS), df[:, :]).then_inc(s_w, 16)
                sp.dma_start(D["window"][0:1].rearrange("(a c) -> a c", a=1), ends[:, 0:1]).then_inc(s_w, 16)
                sp.dma_start(D["window"][1 + P * COLS:2 + P * COLS].rearrange("(a c) -> a c", a=1), ends[:, 1:2]).then_inc(s_w, 16)
                sp.dma_start(D["keys"].rearrange("(p c) -> p c", c=JT), key[:, :]).then_inc(s_w, 16)
                sp.wait_ge(s_w, 8 * 16)
                w = D["window"]
                sp.dma_start(dx[:, :], bass.AP(w.tensor, 0, [[COLS, P], [1, COLS + 2]])).then_inc(s_b, 16)
                sp.dma_start(keyB[:, :], D["keys"].partition_broadcast(P)).then_inc(s_kb, 16)
                sp.wait_ge(s_br, 1)
                sp.dma_start(D["block_of"].rearrange("(p c) -> p c", c=P), brow_i[:, :]).then_inc(s_b, 16)
                sp.wait_ge(s_b, 32)
                sp.dma_start(T["block_of"][:, :], D["block_of"].rearrange("(a c) -> a c", a=1)).then_inc(s_b, 16)
                sp.wait_ge(s_b, 48)
                sp.wait_ge(s_kb, 16)

            @block.vector
            def _(dve):
                ch = Count(dve, s_dve)
                dve.wait_ge(s_ld, 64)
                dve.wait_ge(s_io, 2)
                ch.inc(dve.tensor_copy(sf[:, :], si[:, :]))
                ch.inc(dve.tensor_copy(df[:, :], di[:, :]))
                ch.inc(dve.tensor_copy(tile_f[:, :], tile_i[:, :]))
                ch.inc(dve.tensor_copy(step_f[:, :], step_i[:, :]))
                ch.inc(dve.memset(ends[:, 0:1], -1.0))
                ch.inc(dve.memset(ends[:, 1:2], 2.0e6))
                ch.link(dve.tensor_scalar(wi[:, :], si[:, :], P - 1, None, ALU.bitwise_and))
                ch.inc(dve.tensor_copy(wf[:, :], wi[:, :]))
                ch.link(dve.tensor_scalar(si[:, :], si[:, :], 7, None, ALU.arith_shift_right))
                ch.link(dve.tensor_copy(wb[:, :], si[:, :]))
                ch.link(dve.tensor_scalar(wi[:, :], di[:, :], P - 1, None, ALU.bitwise_and))
                ch.inc(dve.tensor_copy(lo2[:, :], wi[:, :]))
                ch.link(dve.tensor_scalar(di[:, :], di[:, :], 7, None, ALU.arith_shift_right))
                ch.link(dve.tensor_copy(wb2[:, :], di[:, :]))
                ch.link(dve.tensor_copy(key[:, :], di[:, P - 1:COLS:P]))
                ch.link(dve.tensor_tensor(key[:, :], key[:, :], tile_f[:, :], ALU.add))
                ch.link(dve.tensor_copy(wi[:, :], T["edge_no"][:, :]))
                ch.link(dve.tensor_copy(keyB[:, :], wi[:, :]))
                ch.link(dve.tensor_scalar(keyB[:, :], keyB[:, :], E - 0.5, 1.0e6, ALU.is_gt, ALU.mult))
                ch.link(dve.tensor_tensor(df[:, :], df[:, :], keyB[:, :], ALU.add))
                dve.sem_inc(s_k, 1)
                for n, to in ((0, T["src_lo"]), (1, T["dst_lo"])):
                    for j in range(JT):
                        dve.wait_ge(s_mm, n * JT + j + 1)
                        dve.tensor_copy(to[:, j:COLS:JT], pt[:, :]).then_inc(s_rd, 1)
                dve.wait_ge(s_b, 16)
                for a, b, c in ((T["starts"], 0, 1), (T["ends"], 2, 1)):
                    ch.link(dve.tensor_tensor(a[:, :], dx[:, b:b + COLS], dx[:, c:c + COLS], ALU.not_equal))
                    ch.link(dve.tensor_scalar(a[:, :], a[:, :], -BIG, None, ALU.mult))
                for a, n in ((T["starts"], 0), (T["ends"], 1)):
                    ch.link(dve.tensor_reduce(T["chain"][:, n:n + 1], a[:, :], AX_X, ALU.add))
                dve.wait_ge(s_kb, 16)
                for j in range(JT):
                    ch.link(dve.tensor_scalar(wf[:, :], keyB[:, :], step_f[:, j:j + 1], 0.0, ALU.is_lt, ALU.add,
                                              accum_out=tf[:, j:j + 1]))
                ch.link(dve.tensor_copy(T["tile_of"][:, :], tf[:, :]))
                ch.link(dve.tensor_tensor(bf[:, :], step_f[:, :], tf[:, :], ALU.subtract))
                ch.link(dve.tensor_scalar(T["first_node"][:, :], bf[:, :], float(P), None, ALU.mult))
                dve.sem_inc(s_k, 1)
                dve.wait_ge(s_mm, 2 * JT + 1)
                ch.link(dve.tensor_copy(brow_i[:, :], pt[0:JT, :]))
                dve.sem_inc(s_br, 1)

            @block.tensor
            def _(pe):
                pe.wait_ge(s_k, 1)
                to_tiles(pe, s_mm, s_rd, 0, pt, ident, wf)
                to_tiles(pe, s_mm, s_rd, JT, pt, ident, lo2)
                pe.wait_ge(s_k, 2)
                pe.wait_ge(s_rd, 2 * JT)
                pe.transpose(pt[0:JT, :], bf[:, :], ident[:, :]).then_inc(s_mm, 1)

        g = ExitStack()
        with g:
            G = [sb(f"e_g{n}", [P, 2, P], F32, at=g) for n in range(2)]
            pp = pb("e_pp", [P, 2, P], g)
            s_g = [sem(f"e_rows{n}") for n in range(2)]
            s_l, s_m, s_r = sem("e_local"), sem("e_rowT"), sem("e_rowT_read")
            s_dve = sem("e_dve2")
            with nc.Block() as block:
                @block.gpsimd
                def _(pool):
                    for j in range(JT):
                        if j >= 2:
                            pool.wait_ge(s_m, j - 1)
                        off = bass.IndirectOffsetOnAxis(ap=T["tile_of"][:, j:j + 1], axis=0)
                        for a, name in enumerate(("src", "dst")):
                            pool.indirect_dma_start(G[j % 2][:, a, :], None, D[name].rearrange("(t e) -> t e", e=P),
                                                    off).then_inc(s_g[j % 2], 16)

                @block.vector
                def _(dve):
                    for j in range(JT):
                        dve.wait_ge(s_g[j % 2], 32 * (j // 2 + 1))
                        dve.tensor_scalar(G[j % 2][:, 1, :], G[j % 2][:, 1, :], T["first_node"][:, j:j + 1], None,
                                          ALU.subtract).then_inc(s_l, 1)
                        dve.wait_ge(s_m, j + 1)
                        dve.tensor_copy(T["src_of"][:, j * P:j * P + P], pp[:, 0, :]).then_inc(s_r, 1)
                        dve.tensor_copy(T["dst_of"][:, j * P:j * P + P], pp[:, 1, :]).then_inc(s_r, 1)

                @block.tensor
                def _(pe):
                    for j in range(JT):
                        pe.wait_ge(s_l, j + 1)
                        if j:
                            pe.wait_ge(s_r, 2 * j)
                        for a in range(2):
                            mm = pe.transpose(pp[:, a, :], G[j % 2][:, a, :], ident[:, :])
                        mm.then_inc(s_m, 1)


def edge_softmax(nc, sb, pb, sem, gated, ident, iota, elr, er_col, D, T, H, L):
    ctx = ExitStack()
    with ctx:
        sem = ctx.enter_context(phase_semaphores(nc))
        t = lambda name, shape, dt=F32: sb(f"{name}{L}", shape, dt, at=ctx)
        S = lambda *names: [sem(f"{n}{L}") for n in names]
        val = [t(f"l_val{s}", [P, ETP, H]) for s in range(2)]
        vP = [[t(f"l_P{s}{h}", [P, COLS]) for h in range(H)] for s in range(2)]
        c1 = ExitStack()
        with c1:
            t1 = lambda name, shape, dt=F32: sb(f"{name}{L}", shape, dt, at=c1)
            parts = t1("l_parts", [NT, 2, 3, H * P], BF16)
            whole = t1("l_whole", [NT, 2, H * P])
            back = t1("l_back", [NT, H * P])
            bcs = t1("l_hi", [NT, 2, 2, UA * P], BF16)
            pick = t1("l_pick", [NT, 2, 2, UA * P], BF16)
            own_i = t1("l_own_i", [NT, 1], I32)
            own = t1("l_own", [NT, 1])
            junk = t1("l_junk", [P, 2, UA, H, P])
            got = t1("l_got", [P, 2, UA, H])
            banks = [pb(f"l_b{n}{L}", [P, 512], c1) for n in range(UA)]
            s_t, s_dve, s_own, s_hi0, s_hi1, s_pk, s_mm, s_rd = S("l_T", "l_dve", "l_own", "l_hi0", "l_hi1", "l_pick", "l_mm", "l_read")
            s_hi = [s_hi0, s_hi1]
            with nc.Block() as block:
                @block.gpsimd
                def _(pool):
                    pool.iota(own_i[:, :], pattern=[[0, 1]], base=0, channel_multiplier=1).then_inc(s_own, 1)
                    pool.wait_ge(s_own, 1)
                    pool.tensor_copy(own[:, :], own_i[:, :]).then_inc(s_own, 1)

                @block.sync
                def _(sp):
                    with sp.Fori(0, (AIT + 1) // 2) as i:
                        for u in range(2):
                            gated(sp, "sp", s_pk, i * 4 + 2 * (u + 1))
                            for s, name in enumerate(("src_hi", "dst_hi")):
                                row = D[name][bass.ds(i * (2 * UA * P) + u * UA * P, UA * P)]
                                sp.dma_start(bcs[:, u, s, :], row.partition_broadcast(NT)).then_inc(s_hi[u], 16)

                @block.tensor
                def _(pe):
                    for s in range(2):
                        for h in range(H):
                            mm = pe.transpose(banks[s][0:NT, h * P:h * P + P], elr[:, :, s * er_col + h], ident[:, :])
                    mm.then_inc(s_t, 1)
                    pe.wait_ge(s_rd, 1)
                    with pe.Fori(0, (AIT + 1) // 2) as i:
                        for u in range(2):
                            pe.wait_ge(s_pk, i * 4 + (4 + 2 * u + 2))
                            for s in range(2):
                                for q in range(UA):
                                    pe.wait_ge(s_rd, i * (4 * UA) + (1 + 2 * UA * u + s * UA + q + 1))
                                    for part in range(3):
                                        mm = pe.matmul(banks[q][:, 0:H * P], pick[:, u, s, q * P:q * P + P],
                                                       parts[:, s, part, :], start=part == 0, stop=part == 2)
                                    mm.then_inc(s_mm, 1)

                @block.vector
                def _(dve):
                    ch = Count(dve, s_dve)
                    dve.wait_ge(s_own, 2)
                    dve.wait_ge(s_t, 1)
                    for s in range(2):
                        ch.link(dve.tensor_copy(whole[:, s, :], banks[s][0:NT, 0:H * P]))
                        for part in range(3):
                            ch.link(dve.tensor_copy(parts[:, s, part, :], whole[:, s, :]))
                            if part < 2:
                                ch.link(dve.tensor_copy(back[:, :], parts[:, s, part, :]))
                                ch.link(dve.tensor_tensor(whole[:, s, :], whole[:, s, :], back[:, :], ALU.subtract))
                    dve.sem_inc(s_rd, 1)
                    dve.sem_inc(s_rd, UA)
                    dve.sem_inc(s_pk, 4)
                    with dve.Fori(0, (AIT + 1) // 2) as i:
                        ch.enter(i, 2 * 2)
                        for u in range(2):
                            dve.wait_ge(s_hi[u], i * 32 + 32)
                            for s in range(2):
                                dve.tensor_scalar(pick[:, u, s, :], bcs[:, u, s, :], own[:, 0:1], None,
                                                  ALU.is_equal).then_inc(s_pk, 1)
                            for s, lo in enumerate((T["src_lo"], T["dst_lo"])):
                                for q in range(UA):
                                    col = i * (2 * UA) + (u * UA + q)
                                    dve.wait_ge(s_mm, i * (4 * UA) + (2 * UA * u + s * UA + q + 1))
                                    for h in range(H):
                                        ins = dve.scalar_tensor_tensor(
                                            out=junk[:, s, q, h, :], in0=iota[:, :], scalar=lo[:, bass.ds(col, 1)],
                                            in1=banks[q][:, h * P:h * P + P], op0=ALU.is_equal, op1=ALU.mult,
                                            accum_out=got[:, s, q, h:h + 1])
                                    ins.then_inc(s_rd, 1)
                            gated(dve, "dve", s_rd, i * (4 * UA) + (1 + UA + 2 * UA * (u + 1)))
                            for s in range(2):
                                to = val[s][:, bass.ds(i * (2 * UA) + u * UA, UA), :].rearrange("p t h -> p (t h)")
                                ch.inc(dve.tensor_scalar(to, got[:, s, :, :].rearrange("p t h -> p (t h)"), 1.0, None, ALU.mult))
                            ch.wait()
                        ch.leave((AIT + 1) // 2)

        c2 = ExitStack()
        with c2:
            t2 = lambda name, shape, dt=F32: sb(f"{name}{L}", shape, dt, at=c2)
            F, M, W = t2("m_F", [P, COLS]), t2("m_M", [P, COLS]), t2("m_W", [P, COLS])
            rows_ = t2("m_rows", [1, 4, P + 2])
            carry = t2("m_carry", [P, 2])
            pt = [pb(f"m_pt{n}{L}", [P, P], c2) for n in range(2)]
            pr = pb(f"m_pr{L}", [1, 2, P], c2)
            pc = pb(f"m_pc{L}", [P, 2], c2)
            s_dve, s_mm, s_rd, s_row, s_mr, s_ex, s_exd = S("m_dve", "m_T", "m_T_read", "m_row", "m_mr", "m_e", "m_stored")
            n_t = (AIT + 1) // 2 * 2 * UA
            with nc.Block() as block:
                @block.tensor
                def _(pe):
                    n = 0
                    for s in range(2):
                        for h in range(H):
                            for j in range(JT):
                                if n >= 2:
                                    pe.wait_ge(s_rd, n - 1)
                                pe.transpose(pt[n % 2][:, :], val[s][:, j:COLS:JT, h], ident[:, :]).then_inc(s_mm, 1)
                                n += 1
                    for h in range(H):
                        for d in range(2):
                            r = 2 * (2 * h + d)
                            pe.wait_ge(s_row, r + 1)
                            pe.transpose(pr[:, 0, :], carry[:, 0:1], ident[:, :])
                            pe.transpose(pr[:, 1, :], T["chain"][:, d:d + 1], ident[:, :]).then_inc(s_mr, 1)
                            pe.wait_ge(s_row, r + 2)
                            pe.transpose(pc[:, 0:1], rows_[:, 3, d:d + P], ident[0:1, 0:1]).then_inc(s_mr, 1)

                @block.vector
                def _(dve):
                    ch = Count(dve, s_dve)
                    n = 0
                    for s in range(2):
                        for h in range(H):
                            for j in range(JT):
                                dve.wait_ge(s_mm, n + 1)
                                dve.tensor_copy(vP[s][h][:, j * P:j * P + P], pt[n % 2][:, :]).then_inc(s_rd, 1)
                                n += 1
                    dve.wait_ge(s_rd, n)

                    def turn(ap, d, n):
                        return ap if d == 0 else bass.AP(ap.tensor, ap.offset + n - 1, [list(ap.ap[0]), [-1, n]])

                    for h in range(H):
                        for d, mark, v, o in ((0, T["starts"], vP[0][h], F), (1, T["ends"], F, M)):
                            r = 2 * (2 * h + d)
                            scan = lambda init: dve.tensor_tensor_scan(
                                turn(o[:, :], d, COLS), turn(mark[:, :], d, COLS), turn(v[:, :], d, COLS), init, ALU.add, ALU.max)
                            ch.link(scan(-BIG))
                            last = COLS - 1 if d == 0 else 0
                            ch.link(dve.tensor_copy(carry[:, 0:1], o[:, last:last + 1]))
                            dve.sem_inc(s_row, 1)
                            dve.wait_ge(s_mr, r + 1)
                            ch.inc(dve.tensor_copy(rows_[:, 0, 0:P], pr[:, 0, :]))
                            ch.inc(dve.tensor_copy(rows_[:, 1, 0:P], pr[:, 1, :]))
                            ch.link(dve.memset(rows_[:, 3, :], -BIG))
                            ch.link(dve.tensor_tensor_scan(turn(rows_[:, 3, 1:P + 1], d, P), turn(rows_[:, 1, 0:P], d, P),
                                                           turn(rows_[:, 0, 0:P], d, P), -BIG, ALU.add, ALU.max))
                            if d:
                                ch.link(dve.tensor_copy(rows_[:, 2, 0:P], rows_[:, 3, 1:P + 1]))
                                ch.link(dve.memset(rows_[:, 3, :], -BIG))
                                ch.link(dve.tensor_copy(rows_[:, 3, 1:P], rows_[:, 2, 1:P]))
                            dve.sem_inc(s_row, 1)
                            dve.wait_ge(s_mr, r + 2)
                            ch.link(dve.tensor_copy(carry[:, 1:2], pc[:, 0:1]))
                            ch.link(scan(carry[:, 1:2]))
                        el, er = vP[0][h], vP[1][h]
                        ch.link(dve.tensor_tensor(W[:, :], el[:, :], er[:, :], ALU.add))
                        ch.inc(dve.scalar_tensor_tensor(out=W[:, :], in0=W[:, :], scalar=0.2, in1=W[:, :], op0=ALU.mult, op1=ALU.max))
                        ch.link(dve.tensor_tensor(M[:, :], M[:, :], er[:, :], ALU.add))
                        ch.link(dve.scalar_tensor_tensor(out=M[:, :], in0=M[:, :], scalar=0.2, in1=M[:, :], op0=ALU.mult, op1=ALU.max))
                        ch.link(dve.tensor_tensor(el[:, :], W[:, :], M[:, :], ALU.subtract))
                        dve.sem_inc(s_ex, 1)

                @block.scalar
                def _(act):
                    for h in range(H):
                        act.wait_ge(s_ex, h + 1)
                        act.activation(vP[0][h][:, :], vP[0][h][:, :], ACT.Exp).then_inc(s_exd, 1)
                        act.wait_ge(s_exd, h * 17 + 1)
                        act.dma_start(D["ex"][h].rearrange("(p c) -> p c", c=COLS), vP[0][h][:, :]).then_inc(s_exd, 16)
                        act.wait_ge(s_exd, h * 17 + 17)

        c3 = ExitStack()
        with c3:
            G = [sb(f"x_g{n}{L}", [P, H, P], F32, at=c3) for n in range(2)]
            pp = pb(f"x_p{L}", [P, H, P], c3)
            s_g = S("x_rows0", "x_rows1")
            s_m, s_r = S("x_T", "x_T_read")
            with nc.Block() as block:
                @block.gpsimd
                def _(pool):
                    for j in range(JT):
                        if j >= 2:
                            pool.wait_ge(s_m, j - 1)
                        off = bass.IndirectOffsetOnAxis(ap=T["tile_of"][:, j:j + 1], axis=0)
                        for h in range(H):
                            pool.indirect_dma_start(G[j % 2][:, h, :], None, D["ex"][h].rearrange("(t e) -> t e", e=P),
                                                    off).then_inc(s_g[j % 2], 16)

                @block.tensor
                def _(pe):
                    for j in range(JT):
                        pe.wait_ge(s_g[j % 2], 16 * H * (j // 2 + 1))
                        if j:
                            pe.wait_ge(s_r, j)
                        for h in range(H):
                            mm = pe.transpose(pp[:, h, :], G[j % 2][:, h, :], ident[:, :])
                        mm.then_inc(s_m, 1)

                @block.vector
                def _(dve):
                    for j in range(JT):
                        dve.wait_ge(s_m, j + 1)
                        dve.tensor_copy(T["ex"][:, j * P:j * P + P, 0:H].rearrange("p e h -> p h e"),
                                        pp[:, :, :]).then_inc(s_r, 1)


R8 = 8


def gather_and_sum(nc, sb, pb, sem, gated, iota, ztab, acc, T, H, L):
    ctx = ExitStack()
    with ctx:
        sem = ctx.enter_context(phase_semaphores(nc))
        G = [sb(f"g_row{n}{L}", [P, C], F32, at=ctx) for n in range(R8)]
        GS = sb(f"g_scaled{L}", [P, R8, C], F32, at=ctx)
        OH = sb(f"g_onehot{L}", [P, R8, P], F32, at=ctx)
        idx = sb(f"g_idx{L}", [P, 2, 4], I32, at=ctx)
        ps = [pb(f"g_ps{n}{L}", [P, C + H], ctx) for n in range(R8)]
        S = lambda *names: [sem(f"{n}{L}") for n in names]
        s_row = [sem(f"g_landed{n}{L}") for n in range(R8)]
        s_idx, s_used, s_gs, s_oh, s_mm, s_add, s_z = S("g_idx", "g_used", "g_scaled", "g_onehot", "g_mm", "g_added", "g_zero")
        TURNS = (STEPS + R8 - 1) // R8
        w = C // H
        with nc.Block() as block:
            @block.gpsimd
            def _(pool):
                with pool.Fori(0, TURNS) as i:
                    for half in range(2):
                        gated(pool, "pool", s_used, i * R8 + (4 * half + 4))
                        pool.tensor_copy(idx[:, half, :], T["src_of"][:, bass.ds(i * R8 + 4 * half, 4)]).then_inc(s_idx, 1)
                        gated(pool, "pool", s_idx, i * 2 + (half + 1))
                        for q in range(4):
                            n = 4 * half + q
                            pool.indirect_dma_start(G[n][:, :], None, ztab, bass.IndirectOffsetOnAxis(
                                ap=idx[:, half, q:q + 1], axis=0)).then_inc(s_row[n], 16)

            @block.scalar
            def _(act):
                act.sem_inc(s_used, R8)
                with act.Fori(0, TURNS) as i:
                    for n in range(R8):
                        gated(act, "act", s_mm, i * R8 + (n + 1))
                        gated(act, "act", s_row[n], i * 16 + 16)
                        for h in range(H):
                            ins = act.activation(GS[:, n, h * w:h * w + w], G[n][:, h * w:h * w + w], ACT.Copy,
                                                 scale=T["ex"][:, bass.ds(i * R8 + n, 1), h])
                        ins.then_inc(s_gs, 1)
                        gated(act, "act", s_gs, i * R8 + (n + 1))
                        act.sem_inc(s_used, 1)

            @block.tensor
            def _(pe):
                pe.sem_inc(s_mm, R8)
                with pe.Fori(0, TURNS) as i:
                    for n in range(R8):
                        pe.wait_ge(s_oh, i * R8 + (n + 1))
                        gated(pe, "pe", s_add, i * R8 + (n + 1))
                        gated(pe, "pe", s_gs, i * R8 + (n + 1))
                        pe.matmul(ps[n][:, 0:C], OH[:, n, :], GS[:, n, :], start=True, stop=True)
                        pe.matmul(ps[n][:, C:C + H], OH[:, n, :],
                                  T["ex"][:, bass.ds(i * R8 + n, 1), 0:H].rearrange("p a h -> p (a h)"),
                                  start=True, stop=True).then_inc(s_mm, 1)

            @block.vector
            def _(dve):
                dve.memset(acc[:, :, :], 0.0).then_inc(s_z, 1)
                dve.sem_inc(s_add, R8)

                def one_hot(turn, half, need):
                    for n in range(4 * half, 4 * half + 4):
                        dve.wait_ge(s_mm, need + (n + 1))
                        dve.tensor_scalar(OH[:, n, :], iota[:, :], T["dst_of"][:, bass.ds(turn + n, 1)], None,
                                          ALU.is_equal).then_inc(s_oh, 1)

                for n in range(4):
                    dve.wait_ge(s_mm, n + 1)
                    dve.tensor_scalar(OH[:, n, :], iota[:, :], T["dst_of"][:, n:n + 1], None,
                                      ALU.is_equal).then_inc(s_oh, 1)
                dve.wait_ge(s_z, 1)
                with dve.Fori(0, TURNS) as i:
                    for half in range(2):
                        one_hot(i * R8 + R8 * half, 1 - half, i * R8 + R8 * half)
                        for n in range(4 * half, 4 * half + 4):
                            b = dve.value_load(T["block_of"][0:1, bass.ds(i * R8 + n, 1)], min_val=0, max_val=NT - 1)
                            to = acc[:, bass.ds(b, 1), :].rearrange("p a c -> p (a c)")
                            dve.wait_ge(s_mm, i * R8 + (R8 + n + 1))
                            gated(dve, "dve", s_add, i * R8 + (R8 + n))
                            dve.tensor_tensor(to, to, ps[n][:, :], ALU.add).then_inc(s_add, 1)


def divide_by_sum(nc, sem, acc, small, H, L, bias=None, X=None):
    s_dve = sem(f"d_dve{L}")
    w = C // H
    with nc.Block() as block:
        @block.vector
        def _(dve):
            ch = Count(dve, s_dve)
            ch.link(dve.tensor_scalar(small[:, :, 0:H], acc[:, :, C:C + H], 1.0e-30, None, ALU.max))
            ch.link(dve.reciprocal(small[:, :, 0:H], small[:, :, 0:H]))
            for h in range(H):
                part = acc[:, :, h * w:h * w + w]
                ch.link(dve.tensor_tensor(part, part, bcast(small[:, :, h], w), ALU.mult))
            body = acc[:, :, 0:C]
            if bias is not None:
                b = bias[:, :]
                ch.link(dve.tensor_tensor(body, body, bass.AP(b.tensor, b.offset, [list(b.ap[0]), [0, NT], [1, C]]), ALU.add))
                ch.link(dve.tensor_scalar(body, body, 0.0, None, ALU.max))
            else:
                ch.link(dve.tensor_tensor(X[:, :, :], X[:, :, :], body, ALU.add))


def second_projection(nc, sb, pb, sem, gated, ident, acc, elr, ztab, W2, al2, ar2):
    ctx = ExitStack()
    with ctx:
        sem = ctx.enter_context(phase_semaphores(nc))
        t = lambda name, shape: sb(name, shape, F32, at=ctx)
        wz, avec, prod = t("z_w", [P, 2, C + 2]), t("z_a", [P, 2, C]), t("z_prod", [P, C])
        xs, xT, zs = t("z_xs", [P, 2, C]), t("z_xT", [P, 2, 2, P]), t("z_zs", [P, 2, C])
        pT = [pb(f"z_pT{n}", [P, 2, P], ctx) for n in range(2)]
        pZ = [pb(f"z_pZ{n}", [P, C + 2], ctx) for n in range(2)]
        s_w, s_dve, s_xs, s_t, s_xt, s_z, s_zc, s_e = [sem("z_" + n) for n in (
            "w", "dve", "xs", "T", "xT", "mm", "copied", "elr")]
        s_zd = [sem(f"z_stored{u}") for u in range(2)]
        with nc.Block() as block:
            @block.sync
            def _(sp):
                sp.dma_start(wz[:, :, 0:C], W2.rearrange("(a p) n -> p a n", p=P)).then_inc(s_w, 16)
                sp.dma_start(avec[:, 0, :], al2.rearrange("h d -> (h d)").partition_broadcast(P)).then_inc(s_w, 16)
                sp.dma_start(avec[:, 1, :], ar2.rearrange("h d -> (h d)").partition_broadcast(P)).then_inc(s_w, 16)
                with sp.Fori(0, PAIRS) as i:
                    for u in range(2):
                        sp.wait_ge(s_zc, i * 2 + (u + 1))
                        sp.dma_start(ztab[bass.ds(i * (2 * P) + u * P, P), :], zs[:, u, :]).then_inc(s_zd[u], 16)
                for u in range(2):
                    sp.wait_ge(s_zd[u], 16 + PAIRS * 16)

            @block.vector
            def _(dve):
                ch = Count(dve, s_dve)
                dve.wait_ge(s_w, 48)
                for c in range(2):
                    for side in range(2):
                        ch.link(dve.tensor_tensor(prod[:, :], wz[:, c, 0:C], avec[:, side, :], ALU.mult))
                        ch.link(dve.tensor_reduce(wz[:, c, C + side:C + side + 1], prod[:, :], AX_X, ALU.add))
                with dve.Fori(0, PAIRS) as i:
                    for u in range(2):
                        dve.wait_ge(s_t, i * 2 + (u + 1))
                        dve.tensor_scalar(xs[:, u, :], acc[:, bass.ds(i * 2 + u, 1), 0:C].rearrange("p a c -> p (a c)"),
                                          1.0, None, ALU.mult).then_inc(s_xs, 1)
                    for u in range(2):
                        dve.wait_ge(s_zc, i * 2 + (u + 1))
                        dve.tensor_scalar(elr[:, bass.ds(i * 2 + u, 1), 0:2].rearrange("p a c -> p (a c)"),
                                          pZ[u][:, C:C + 2], 1.0, None, ALU.mult).then_inc(s_e, 1)

            @block.tensor
            def _(pe):
                pe.sem_inc(s_t, 2)
                pe.sem_inc(s_e, 2)
                pe.wait_ge(s_dve, 8)
                with pe.Fori(0, PAIRS) as i:
                    for u in range(2):
                        pe.wait_ge(s_xs, i * 2 + (u + 1))
                        for c in range(2):
                            mm = pe.transpose(pT[u][:, c, :], xs[:, u, c * P:c * P + P], ident[:, :])
                        mm.then_inc(s_t, 1)
                    for u in range(2):
                        pe.wait_ge(s_xt, i * 2 + (u + 1))
                        gated(pe, "pe", s_e, i * 2 + (u + 1))
                        for c in range(2):
                            mm = pe.matmul(pZ[u][:, :], xT[:, u, c, :], wz[:, c, :], start=c == 0, stop=c == 1)
                        mm.then_inc(s_z, 1)

            @block.scalar
            def _(act):
                for u in range(2):
                    act.sem_inc(s_zd[u], 16)
                with act.Fori(0, PAIRS) as i:
                    for u in range(2):
                        act.wait_ge(s_t, i * 2 + (2 + u + 1))
                        act.copy(xT[:, u, :, :], pT[u][:, :, :]).then_inc(s_xt, 1)
                    for u in range(2):
                        act.wait_ge(s_z, i * 2 + (u + 1))
                        gated(act, "act", s_zd[u], i * 16 + 16)
                        act.copy(zs[:, u, :], pZ[u][:, 0:C]).then_inc(s_zc, 1)


def attention_layers(nc, sb, pb, sem, dram, gated, ident, iota, X, elr, ztab, src, dst, b1, W2, al2, ar2):
    ctx = ExitStack()
    with ctx:
        sem = ctx.enter_context(phase_semaphores(nc))
        t = lambda name, shape, dt=F32: sb(name, shape, dt, at=ctx)
        D = {"src_hi": dram("src_hi", (P * COLS,), BF16), "dst_hi": dram("dst_hi", (P * COLS,), BF16),
             "src": dram("src_f", (P * COLS,), F32), "dst": dram("dst_f", (P * COLS,), F32),
             "window": dram("window", (P * COLS + 2,), F32), "keys": dram("keys", (COLS,), F32),
             "block_of": dram("block_of_d", (COLS,), I32),
             "ex": [dram(f"ex{h}", (P * COLS,), F32) for h in range(2)]}
        T = {"src_lo": t("src_lo", [P, COLS]), "dst_lo": t("dst_lo", [P, COLS]),
             "starts": t("starts", [P, COLS]), "ends": t("ends", [P, COLS]), "chain": t("chain", [P, 2]),
             "tile_of": t("tile_of", [P, JT], I32), "first_node": t("first_node", [P, JT]),
             "src_of": t("src_of", [P, COLS], I32), "dst_of": t("dst_of", [P, COLS]),
             "block_of": t("block_of", [1, COLS], I32), "ex": t("ex", [P, COLS, 2])}
        bias = t("gat_bias", [P, C])
        small = t("small", [P, NT, 2])
        c0 = ExitStack()
        with c0:
            T["edge_no"] = sb("edge_no", [P, COLS], I32, at=c0)
            s_i, s_b = sem("i_edge"), sem("i_bias")
            with nc.Block() as block:
                @block.gpsimd
                def _(pool):
                    pool.iota(T["edge_no"][:, :], pattern=[[1, COLS]], base=0, channel_multiplier=COLS).then_inc(s_i, 1)
                    pool.wait_ge(s_i, 1)

                @block.sync
                def _(sp):
                    sp.dma_start(bias[:, :], b1.rearrange("h d -> (h d)").partition_broadcast(P)).then_inc(s_b, 16)
                    sp.wait_ge(s_b, 16)
            prepare_edges(nc, sb, pb, sem, ident, src, dst, D, T)
        edge_softmax(nc, sb, pb, sem, gated, ident, iota, elr, 2, D, T, 2, "a")
        c1 = ExitStack()
        with c1:
            acc = sb("acc_a", [P, NT, C + 2], F32, at=c1)
            gather_and_sum(nc, sb, pb, sem, gated, iota, ztab, acc, T, 2, "a")
            divide_by_sum(nc, sem, acc, small, 2, "a", bias=bias)
            second_projection(nc, sb, pb, sem, gated, ident, acc, elr, ztab, W2, al2, ar2)
        edge_softmax(nc, sb, pb, sem, gated, ident, iota, elr, 1, D, T, 1, "b")
        c1 = ExitStack()
        with c1:
            acc = sb("acc_b", [P, NT, C + 1], F32, at=c1)
            gather_and_sum(nc, sb, pb, sem, gated, iota, ztab, acc, T, 1, "b")
            divide_by_sum(nc, sem, acc, small, 1, "b", X=X)


def experts(nc, sb, pb, sem, gated, ident, X, out, Wr, br, fW1, fb1, fg1, fbe1, fm1, fv1,
            fW2, fb2, fg2, fbe2, fm2, fv2, fWo, fbo):
    ctx = ExitStack()
    with ctx:
        sem = ctx.enter_context(phase_semaphores(nc))
        t = lambda name, shape, dt=F32: sb(name, shape, dt, at=ctx)
        XN = t("f_xn", [P, NT, C])
        rs = t("f_rs", [P, NT])
        c1 = ExitStack()
        with c1:
            sq, sm = sb("f_sq", [P, 10, C], F32, at=c1), sb("f_sm", [P, NT], F32, at=c1)
            layer_norm(nc, sem, "ln2", X, XN, sq, sm, rs)
        w1, w2, wo = [t(n, [P, NX, 2, C]) for n in ("f_w1", "f_w2", "f_wo")]
        wr = t("f_wr", [P, 2, NX])
        brb = t("f_br", [P, NX])
        bo = t("f_bo", [NX, C])
        pn = t("f_pn", [80, 2, P])
        par = t("f_par", [P, 2, 5, 16])
        root = t("f_root", [P, 2, 16])
        mul, add = t("f_mul", [P, 2, 16]), t("f_add", [P, 2, 16])
        xs = t("f_xs", [P, 2, C])
        xT = t("f_xT", [P, 2, 2 * P])
        h1, h2 = t("f_h1", [P, 2, 2, 2 * P]), t("f_h2", [P, 2, 2, 2 * P])
        lg, wt, m2 = t("f_lg", [P, 2, NX]), t("f_wt", [P, 2, NX]), t("f_m2", [P, 2])
        wT = t("f_wT", [NX, 2, P])
        pH1 = [pb(f"f_pH1{n}", [P, 2, 2 * P], ctx) for n in range(2)]
        pH2 = [pb(f"f_pH2{n}", [P, 2, 2 * P], ctx) for n in range(2)]
        pY = [pb(f"f_pY{n}", [P, 2, C], ctx) for n in range(2)]
        pT = pb("f_pT", [P, 2, 2 * P], ctx)
        pR = pb("f_pR", [P, 512], ctx)
        names = ("loaded par parT par_read dve root bn xs T xT logits wlog exp weights wT wT_copied bo_sum bo_read "
                 "h1 a1 h2 a2 y y_read").split()
        (s_ld, s_par, s_pt, s_pr, s_dve, s_root, s_bn, s_xs, s_t, s_xt, s_lg, s_wl, s_ex, s_w, s_wT, s_wc, s_b, s_br,
         s_h1, s_a1, s_h2, s_a2, s_y, s_yr) = [sem("f_" + n) for n in names]
        s_done, s_out = sem("f_done"), sem("f_out")
        with nc.Block() as block:
            @block.sync
            def _(sp):
                for n, stack in enumerate(((fb1, fg1, fbe1, fm1, fv1), (fb2, fg2, fbe2, fm2, fv2))):
                    for a, p in enumerate(stack):
                        sp.dma_start(pn[16 * a:16 * a + 16, n, :], p.rearrange("e (c p) -> (e c) p", p=P)).then_inc(s_par, 16)
                sp.dma_start(wr[:, :, :], Wr.rearrange("(a p) e -> p a e", p=P)).then_inc(s_ld, 16)
                sp.dma_start(brb[:, :], br.partition_broadcast(P)).then_inc(s_ld, 16)
                sp.dma_start(bo[:, :], fbo).then_inc(s_ld, 16)
                for to, w in ((w1, fW1), (w2, fW2), (wo, fWo)):
                    for e in range(NX):
                        sp.dma_start(to[:, e, :, :], w[e].rearrange("(a p) n -> p a n", p=P)).then_inc(s_ld, 16)
                with sp.Fori(0, PAIRS - 1) as i:
                    sp.wait_ge(s_done, i + 1)
                    rows = out[bass.ds(i * (2 * P), 2 * P), :].rearrange("(k p) c -> p k c", p=P)
                    sp.dma_start(rows, X[:, bass.ds(i * 2, 2), :]).then_inc(s_out, 16)
                sp.wait_ge(s_done, PAIRS)
                sp.dma_start(out[FULL * P:N, :], X[0:REST, FULL, :]).then_inc(s_out, 16)
                sp.wait_ge(s_out, PAIRS * 16)

            @block.vector
            def _(dve):
                ch = Count(dve, s_dve)
                for n in range(2):
                    dve.wait_ge(s_pt, n + 1)
                    dve.tensor_copy(par[:, n, :, :].rearrange("p a b -> p (a b)"), pR[:, 0:80]).then_inc(s_pr, 1)
                dve.wait_ge(s_pr, 2)
                ch.link(dve.tensor_scalar(root[:, :, :], par[:, :, 4, :], EPS_BN, None, ALU.add))
                dve.sem_inc(s_bn, 1)
                dve.wait_ge(s_root, 1)
                ch.link(dve.reciprocal(root[:, :, :], root[:, :, :]))
                ch.link(dve.tensor_tensor(mul[:, :, :], par[:, :, 1, :], root[:, :, :], ALU.mult))
                ch.link(dve.tensor_tensor(add[:, :, :], par[:, :, 0, :], par[:, :, 3, :], ALU.subtract))
                ch.link(dve.tensor_tensor(add[:, :, :], add[:, :, :], mul[:, :, :], ALU.mult))
                ch.link(dve.tensor_tensor(add[:, :, :], add[:, :, :], par[:, :, 2, :], ALU.add))
                dve.sem_inc(s_bn, 1)
                dve.wait_ge(s_ld, 27 * 16)
                with dve.Fori(0, PAIRS) as i:
                    ch.enter(i, 2 + 6 + 1 + 2 * NX)
                    for u in range(2):
                        ch.link(dve.tensor_scalar(xs[:, u, :], XN[:, bass.ds(i * 2 + u, 1), :].rearrange("p a c -> p (a c)"),
                                                  rs[:, bass.ds(i * 2 + u, 1)], None, ALU.mult))
                    dve.sem_inc(s_xs, 1)
                    dve.wait_ge(s_lg, i + 1)
                    b = brb[:, :]
                    ch.link(dve.tensor_tensor(lg[:, :, :], pR[:, 0:2 * NX].rearrange("p (u e) -> p u e", u=2),
                                              bass.AP(b.tensor, b.offset, [list(b.ap[0]), [0, 2], [1, NX]]), ALU.add))
                    ch.link(dve.tensor_reduce(m2[:, :], lg[:, :, :], AX_X, ALU.max))
                    ch.link(dve.tensor_tensor(lg[:, :, :], lg[:, :, :], bcast(m2[:, :], NX), ALU.subtract))
                    dve.sem_inc(s_wl, 1)
                    dve.wait_ge(s_ex, i + 1)
                    ch.link(dve.tensor_reduce(m2[:, :], lg[:, :, :], AX_X, ALU.add))
                    ch.link(dve.reciprocal(m2[:, :], m2[:, :]))
                    ch.link(dve.tensor_tensor(wt[:, :, :], lg[:, :, :], bcast(m2[:, :], NX), ALU.mult))
                    dve.sem_inc(s_w, 1)
                    both = X[:, bass.ds(i * 2, 2), :]
                    dve.wait_ge(s_b, i + 1)
                    ch.link(dve.tensor_tensor(both, both, pT[:, :, :], ALU.add))
                    dve.sem_inc(s_br, 1)
                    for e in range(NX):
                        dve.wait_ge(s_y, i * NX + (e + 3))
                        for u in range(2):
                            xk = X[:, bass.ds(i * 2 + u, 1), :].rearrange("p a c -> p (a c)")
                            ch.inc(dve.scalar_tensor_tensor(out=xk, in0=pY[e % 2][:, u, :], scalar=wt[:, u, e:e + 1], in1=xk,
                                                            op0=ALU.mult, op1=ALU.add))
                        ch.wait()
                        dve.sem_inc(s_yr, 1)
                    dve.sem_inc(s_done, 1)
                ch.leave(PAIRS)

            @block.scalar
            def _(act):
                act.wait_ge(s_bn, 1)
                act.activation(root[:, :, :], root[:, :, :], ACT.Sqrt).then_inc(s_root, 1)
                act.wait_ge(s_bn, 2)
                act.sem_inc(s_a1, 2)
                act.sem_inc(s_a2, 2)

                def relu(i, e, p, h, layer, ready, slot, done):
                    act.wait_ge(ready, i * NX + (e + 1 + 2 * layer))
                    gated(act, "act", slot, i * NX + (e + 1))
                    for c in range(2):
                        k = 2 * e + c
                        ins = act.activation(h[:, e % 2, c, :], p[e % 2][:, c, :], ACT.Relu, bias=add[:, layer, k:k + 1],
                                             scale=mul[:, layer, k:k + 1])
                    ins.then_inc(done, 1)

                with act.Fori(0, PAIRS) as i:
                    act.wait_ge(s_t, i + 1)
                    act.copy(xT[:, :, :], pT[:, :, :]).then_inc(s_xt, 1)
                    act.wait_ge(s_wl, i + 1)
                    act.activation(lg[:, :, :], lg[:, :, :], ACT.Exp).then_inc(s_ex, 1)
                    act.wait_ge(s_wT, i + 1)
                    act.copy(wT[:, :, :].rearrange("p u n -> p (u n)"), pR[0:NX, 256:512]).then_inc(s_wc, 1)
                    for e in range(NX + 1):
                        if e < NX:
                            relu(i, e, pH1, h1, 0, s_h1, s_h2, s_a1)
                        if e:
                            relu(i, e - 1, pH2, h2, 1, s_h2, s_y, s_a2)

            @block.tensor
            def _(pe):
                pe.wait_ge(s_par, 160)
                for n in range(2):
                    if n:
                        pe.wait_ge(s_pr, n)
                    pe.transpose(pR[:, 0:80], pn[:, n, :], ident[0:80, 0:80]).then_inc(s_pt, 1)
                pe.wait_ge(s_ld, 27 * 16)
                pe.wait_ge(s_pr, 2)
                pe.sem_inc(s_h2, 2)
                pe.sem_inc(s_y, 2)
                pe.sem_inc(s_yr, 2)

                def layer(i, e, w, h_of, p, waits, done):
                    for s, v in waits:
                        gated(pe, "pe", s, v)
                    for m in range(2):
                        for c in range(2):
                            mm = pe.matmul(p[e % 2][:, m, :], w[:, e, c, m * P:m * P + P], h_of(c), start=c == 0, stop=c == 1)
                    mm.then_inc(done, 1)

                with pe.Fori(0, PAIRS) as i:
                    gated(pe, "pe", s_xs, i + 1)
                    for c in range(2):
                        for u in range(2):
                            mm = pe.transpose(pT[:, c, u * P:u * P + P], xs[:, u, c * P:c * P + P], ident[:, :])
                    mm.then_inc(s_t, 1)
                    gated(pe, "pe", s_xt, i + 1)
                    for u in range(2):
                        for c in range(2):
                            mm = pe.matmul(pR[:, u * NX:u * NX + NX], xT[:, c, u * P:u * P + P], wr[:, c, :],
                                           start=c == 0, stop=c == 1)
                    mm.then_inc(s_lg, 1)
                    for e in range(NX + 2):
                        if e < NX:
                            layer(i, e, w1, lambda c: xT[:, c, :], pH1, [(s_a1, i * NX + (e + 1))], s_h1)
                        if e == 1:
                            gated(pe, "pe", s_w, i + 1)
                            for u in range(2):
                                mm = pe.transpose(pR[0:NX, 256 + u * P:256 + u * P + P], wt[:, u, :], ident[:, :])
                            mm.then_inc(s_wT, 1)
                        if 1 <= e <= NX:
                            layer(i, e - 1, w2, lambda c: h1[:, (e - 1) % 2, c, :], pH2,
                                  [(s_a1, i * NX + (e + 2)), (s_a2, i * NX + e)], s_h2)
                        if e == 1:
                            gated(pe, "pe", s_wc, i + 1)
                            for u in range(2):
                                mm = pe.matmul(pT[:, u, :], wT[:, u, :], bo[:, :], start=True, stop=True)
                            mm.then_inc(s_b, 1)
                        if e >= 2:
                            f = e - 2
                            gated(pe, "pe", s_a2, i * NX + (f + 3))
                            gated(pe, "pe", s_yr, i * NX + (f + 1))
                            for u in range(2):
                                for c in range(2):
                                    mm = pe.matmul(pY[f % 2][:, u, :], h2[:, f % 2, c, u * P:u * P + P], wo[:, f, c, :],
                                                   start=c == 0, stop=c == 1)
                            mm.then_inc(s_y, 1)
                    gated(pe, "pe", s_br, i + 1)


_INS = ['x', 'src', 'dst', 'L0_gnn_W1', 'L0_gnn_al1', 'L0_gnn_ar1', 'L0_gnn_b1', 'L0_gnn_W2', 'L0_gnn_al2', 'L0_gnn_ar2', 'L0_gnn_b2', 'L0_mix_Wqkv', 'L0_mix_bqkv', 'L0_mix_Wproj', 'L0_mix_bproj', 'L0_mix_temperature', 'L0_ffn_Wr', 'L0_ffn_br', 'L0_ffn_W1', 'L0_ffn_b1', 'L0_ffn_g1', 'L0_ffn_be1', 'L0_ffn_m1', 'L0_ffn_v1', 'L0_ffn_W2', 'L0_ffn_b2', 'L0_ffn_g2', 'L0_ffn_be2', 'L0_ffn_m2', 'L0_ffn_v2', 'L0_ffn_Wo', 'L0_ffn_bo']


def kernel(**inputs):
    import numpy as _np
    import concourse.bacc as _bacc
    from concourse import mybir as _mybir
    from concourse.bass_utils import run_bass_kernel_spmd as _run

    nc = _bacc.Bacc("TRN2", target_bir_lowering=False, num_devices=1)
    arrays, args = {}, []
    for name in _INS:
        a = _np.ascontiguousarray(inputs[name])
        arrays[f"in_{name}_dram"] = a
        args.append(nc.dram_tensor(f"in_{name}_dram", a.shape, _mybir.dt.from_np(a.dtype), kind="ExternalInput").ap())
    args.append(nc.dram_tensor("out_dram", (N, C), F32, kind="ExternalOutput").ap())
    build(nc, *args)
    r = _run(nc, [arrays], core_ids=[0])
    return r.results[0]["out_dram"]
```

```python
from contextlib import ExitStack, contextmanager

import concourse.bass as bass
from concourse import mybir

ALU = mybir.AluOpType
ACT = mybir.ActivationFunctionType
F32 = mybir.dt.float32
BF16 = mybir.dt.bfloat16
I32 = mybir.dt.int32
AX_X = mybir.AxisListType.X

P = 128
N, C = 6250, 256
E = 200000
NT = 50
FULL = N // P
REST = N - FULL * P
PAIRS = NT // 2
HM, DM = 8, 32
MAIN = 16 * DM
QUADS = HM * MAIN // P
FEAT = HM * MAIN + 2 * HM * DM
CH = FEAT // P
V1 = DM + 1
COLS = 1664
JT = COLS // P
ET = (E + P - 1) // P
ETP = COLS
NBLK = (N + P - 1) // P
STEPS = ET + NBLK
UA = 16
AIT = (ET + 2 * UA - 1) // (2 * UA)
NX = 8
EPS_LN, EPS_BN, EPS_NORM = 1e-5, 1e-3, 1e-12
SC = float(DM) ** 0.25
BIG = 1.0e30


class Count:

    def __init__(self, eng, sem):
        self.eng, self.sem, self.total, self.n, self.reg = eng, sem, 0, 0, 0

    def inc(self, ins):
        ins.then_inc(self.sem, 1)
        self.n += 1

    def wait(self):
        self.eng.wait_ge(self.sem, self.reg + (self.total + self.n))

    def link(self, ins):
        self.inc(ins)
        self.wait()

    def enter(self, i, per_round):
        self.total, self.n, self.per, self.reg = self.total + self.n, 0, per_round, i * per_round

    def leave(self, rounds):
        assert self.n == self.per, (self.n, self.per)
        self.total, self.n, self.reg = self.total + rounds * self.per, 0, 0


@contextmanager
def phase_semaphores(nc):
    held = []

    def sem(name):
        held.append(nc.alloc_semaphore(name))
        return held[-1]

    yield sem
    nc.clear_and_free_semaphores(held)
    nc.all_engine_barrier()


def bcast(ap, count):
    return bass.AP(ap.tensor, ap.offset, [list(d) for d in ap.ap] + [[0, count]])



def build(nc, x, src, dst, W1, al1, ar1, b1, W2, al2, ar2, b2, Wqkv, bqkv, Wproj, bproj, temp,
          Wr, br, fW1, fb1, fg1, fbe1, fm1, fv1, fW2, fb2, fg2, fbe2, fm2, fv2, fWo, fbo, out):
    ctx = ExitStack()
    with ctx:
        def sb(name, shape, dt=F32, at=None):
            return (at or ctx).enter_context(nc.sbuf_tensor(name, shape, dt))

        def pb(name, shape, at, dt=F32):
            return at.enter_context(nc.psum_tensor(name, shape, dt))

        def sem(name):
            return ctx.enter_context(nc.semaphore(name))

        def dram(name, shape, dt):
            return nc.dram_tensor(name, shape, dt, kind="Internal").ap()

        s_gate = {e: sem(f"gate_{e}") for e in ("pool", "act", "dve", "pe", "sp")}

        def gated(eng, name, s, value):
            eng.wait_ge(s, value)
            eng.sem_inc(s_gate[name], 1)

        ztab = dram("ztab", (NT * P, C), F32)

        X = sb("X", [P, NT, C])
        ident = sb("ident", [P, P])
        iota = sb("iota", [P, P])
        elr = sb("elr", [P, NT, 4])

        constants(nc, ctx, sb, pb, sem, ident, iota, X, x)
        project_and_mix(nc, sb, pb, sem, gated, ident, X, elr, ztab,
                        W1, al1, ar1, b2, Wqkv, bqkv, Wproj, bproj, temp)
        attention_layers(nc, sb, pb, sem, dram, gated, ident, iota, X, elr, ztab, src, dst, b1, W2, al2, ar2)
        experts(nc, sb, pb, sem, gated, ident, X, out, Wr, br, fW1, fb1, fg1, fbe1, fm1, fv1,
                fW2, fb2, fg2, fbe2, fm2, fv2, fWo, fbo)


def constants(nc, ctx, sb, pb, sem, ident, iota, X, x):
    s_pad, s_x, s_id = sem("s_pad"), sem("s_x"), sem("s_id")
    tmp = ctx.enter_context(nc.sbuf_tensor("iota_i", [P, P], I32))
    with nc.Block() as block:
        @block.sync
        def _(sp):
            sp.dma_start(X[:, 0:FULL, :], x[0:FULL * P, :].rearrange("(k p) c -> p k c", p=P)).then_inc(s_x, 16)
            sp.wait_ge(s_pad, 1)
            sp.dma_start(X[0:REST, FULL, :], x[FULL * P:N, :]).then_inc(s_x, 16)
            sp.wait_ge(s_x, 32)

        @block.gpsimd
        def _(pool):
            pool.memset(X[:, FULL:NT, :], 0.0).then_inc(s_pad, 1)
            pool.memset(ident[:, :], 0.0).then_inc(s_id, 1)
            pool.iota(tmp[:, :], pattern=[[1, P]], base=0, channel_multiplier=0).then_inc(s_id, 1)
            pool.wait_ge(s_id, 2)
            pool.affine_select(out=ident[:, :], in_=ident[:, :], compare_op=ALU.not_equal, fill=1.0,
                               base=0, pattern=[[-1, P]], channel_multiplier=1).then_inc(s_id, 1)
            pool.tensor_copy(iota[:, :], tmp[:, :]).then_inc(s_id, 1)
            pool.wait_ge(s_id, 4)


def layer_norm(nc, sem, name, X, XN, sq, sm, rs):
    s_dve, s_var, s_root = sem(name + "_dve"), sem(name + "_var"), sem(name + "_root")
    with nc.Block() as block:
        @block.vector
        def _(dve):
            ch = Count(dve, s_dve)
            centre_and_square(dve, ch, X, XN, sq, sm, rs)
            dve.sem_inc(s_var, 1)
            dve.wait_ge(s_root, 1)
            ch.link(dve.reciprocal(rs[:, :], sm[:, :]))
            dve.sem_inc(s_var, 1)

        @block.scalar
        def _(act):
            act.wait_ge(s_var, 1)
            act.activation(sm[:, :], rs[:, :], ACT.Sqrt).then_inc(s_root, 1)


def centre_and_square(dve, ch, X, XN, sq, sm, rs):
    ch.link(dve.tensor_reduce(sm[:, :], X[:, :, :], AX_X, ALU.add))
    ch.link(dve.tensor_scalar(sm[:, :], sm[:, :], 1.0 / C, None, ALU.mult))
    ch.link(dve.tensor_tensor(XN[:, :, :], X[:, :, :], bcast(sm[:, :], C), ALU.subtract))
    for c in range(NT // 10):
        part = XN[:, 10 * c:10 * c + 10, :]
        ch.link(dve.tensor_tensor(sq[:, :, :], part, part, ALU.mult))
        ch.link(dve.tensor_reduce(rs[:, 10 * c:10 * c + 10], sq[:, :, :], AX_X, ALU.add))
    ch.link(dve.tensor_scalar(rs[:, :], rs[:, :], 1.0 / C, EPS_LN, ALU.mult, ALU.add))


def project_and_mix(nc, sb, pb, sem, gated, ident, X, elr, ztab, W1, al1, ar1, b2, Wqkv, bqkv, Wproj, bproj, temp):
    ctx = ExitStack()
    with ctx:
        sem = ctx.enter_context(phase_semaphores(nc))
        t = lambda name, shape, dt=F32: sb(name, shape, dt, at=ctx)
        QN = t("QN", [P, NT, C])
        KVS = t("KVS", [P, QUADS, V1])
        KV4 = t("KV4", [P, 4, 4 * V1])
        VS = t("VS", [P, HM * V1])
        wproj = t("wproj", [P, 2, C])
        bsum = t("bsum", [P, C])
        w8 = t("w8", [P, 2])
        head_of = t("head_of", [P, 4])
        c1 = ExitStack()
        with c1:
            t = lambda name, shape, dt=F32: sb(name, shape, dt, at=c1)
            wz = t("wz", [P, 2, C + 4])
            wqkv = t("wqkv", [P, 2, 3 * C])
            wnat = t("wnat", [P, 8, C])
            avec = t("avec", [P, 2, C])
            prod = t("prod", [P, C])
            bq = t("bq", [P, 3 * C])
            tmpb = t("tmpb", [P, 2, C])
            tempb = t("tempb", [P, HM])
            fac = t("fac", [P, 2, HM])
            sq2 = t("sq2", [P, 2, HM])
            mask = t("mask", [P, NT])
            sq = t("sq", [P, 10, C])
            sm = t("sm", [P, NT])
            rs = t("rs", [P, NT])
            xs = t("xs", [P, 2, C])
            xT = t("xT", [P, 2, 2, P])
            zs = t("zs", [P, 2, C])
            qkv = t("qkv", [P, 3 * C])
            sqk = t("sqk", [P, 2 * C])
            nrm = t("nrm", [P, 2, HM])
            rt = t("rt", [P, 2 * HM])
            kn = t("kn", [P, 2, HM, 2 * DM])
            v1 = t("v1", [P, 2, HM, V1])
            KF = t("KF", [P, 2, FEAT])
            ones = t("ones", [P, P])
            zero = t("zero", [P, 512])
            pKV = [pb(f"pKV{n}", [P, 512], c1) for n in range(4)]
            pT = pb("pT", [P, 2, P], c1)
            pZ = pb("pZ", [P, 512], c1)
            pQ = pb("pQ", [P, 1024], c1)
            s_w, s_nw, s_cst = sem("p_w"), sem("p_natural"), sem("p_const")
            s_wt, s_wc = sem("p_wT"), sem("p_wT_copied")
            s_dve, s_xs, s_t, s_xt = sem("p_dve"), sem("p_xs"), sem("p_T"), sem("p_xT")
            s_kl, s_sq, s_kn, s_kn2, s_v, s_n2, s_rt, s_z, s_q, s_zc, s_elr, s_qv, s_kf, s_kv, s_init = [sem("p_" + n) for n in (
                "linear", "squares", "keys", "keys_doubled", "values", "norm2", "norm", "z", "qkv", "z_copied", "elr", "qkv_read", "features", "kv", "init")]
            s_zd = [sem(f"p_z_stored{u}") for u in range(2)]

            def kv_place(ch):
                if ch < QUADS:
                    n, c = (ch // 15, (ch % 15) * V1) if ch < 30 else (2, (ch - 30) * V1)
                    return pKV[n][:, c:c + V1]
                g = ch - QUADS
                n, c = (2, 2 * V1 + g * 4 * V1) if g < 3 else (3, 0)
                return pKV[n][:, c:c + 4 * V1]
            VSUM = pKV[3][:, 4 * V1:4 * V1 + HM * V1]

            layer_norm(nc, sem, "ln1", X, QN, sq, sm, rs)
            with nc.Block() as block:
                @block.sync
                def _(sp):
                    sp.dma_start(wz[:, :, 0:C], W1.rearrange("(a p) n -> p a n", p=P)).then_inc(s_w, 16)
                    sp.dma_start(avec[:, 0, :], al1.rearrange("h d -> (h d)").partition_broadcast(P)).then_inc(s_w, 16)
                    sp.dma_start(avec[:, 1, :], ar1.rearrange("h d -> (h d)").partition_broadcast(P)).then_inc(s_w, 16)
                    sp.dma_start(bq[:, :], bqkv.partition_broadcast(P)).then_inc(s_w, 16)
                    sp.dma_start(tmpb[:, 0, :], bproj.partition_broadcast(P)).then_inc(s_w, 16)
                    sp.dma_start(tmpb[:, 1, :], b2.rearrange("h d -> (h d)").partition_broadcast(P)).then_inc(s_w, 16)
                    sp.dma_start(tempb[:, :], temp.rearrange("a h b c -> (a h b c)").partition_broadcast(P)).then_inc(s_w, 16)
                    sp.dma_start(wnat[:, 0:6, :], Wqkv.rearrange("(a p) c -> p a c", p=P)).then_inc(s_nw, 16)
                    sp.dma_start(wnat[:, 6:8, :], Wproj.rearrange("(a p) c -> p a c", p=P)).then_inc(s_nw, 16)
                    sp.wait_ge(s_w, 7 * 16)
                    sp.wait_ge(s_nw, 32)

                    with sp.Fori(0, PAIRS) as i:
                        for u in range(2):
                            sp.wait_ge(s_zc, i * 2 + (u + 1))
                            sp.dma_start(ztab[bass.ds(i * (2 * P) + u * P, P), :], zs[:, u, :]).then_inc(s_zd[u], 16)
                    for u in range(2):
                        sp.wait_ge(s_zd[u], 16 + PAIRS * 16)

                @block.gpsimd
                def _(pool):
                    pool.memset(ones[:, :], 1.0).then_inc(s_cst, 1)
                    pool.memset(zero[:, :], 0.0).then_inc(s_cst, 1)
                    pool.memset(mask[:, :], 1.0 / N).then_inc(s_cst, 1)
                    pool.memset(w8[:, 0:1], 1.0).then_inc(s_cst, 1)
                    pool.wait_ge(s_cst, 4)
                    pool.memset(w8[0:DM, 0:1], 0.5).then_inc(s_cst, 1)
                    pool.wait_ge(s_cst, 5)
                    pool.affine_select(out=mask[:, :], in_=mask[:, :], compare_op=ALU.is_gt, fill=0.0,
                                       base=N, pattern=[[-P, NT]], channel_multiplier=-1).then_inc(s_cst, 1)
                    pool.memset(head_of[:, :], 0.0).then_inc(s_cst, 1)
                    pool.wait_ge(s_cst, 7)
                    for h in range(4):
                        pool.memset(head_of[DM * h:DM * h + DM, h:h + 1], 1.0).then_inc(s_cst, 1)
                    pool.wait_ge(s_cst, 11)

                @block.vector
                def _(dve):
                    ch = Count(dve, s_dve)
                    dve.wait_ge(s_w, 7 * 16)
                    for c in range(2):
                        for side in range(2):
                            ch.link(dve.tensor_tensor(prod[:, :], wz[:, c, 0:C], avec[:, side, :], ALU.mult))
                            ch.link(dve.tensor_reduce(wz[:, c, C + 2 * side:C + 2 * side + 2],
                                                      prod[:, :].rearrange("p (h d) -> p h d", h=2), AX_X, ALU.add))
                    ch.link(dve.tensor_tensor(bsum[:, :], tmpb[:, 0, :], tmpb[:, 1, :], ALU.add))
                    ch.link(dve.tensor_scalar(fac[:, 0, :], tempb[:, :], SC * SC, None, ALU.mult))
                    ch.link(dve.memset(fac[:, 1, :], SC))
                    ch.link(dve.memset(sq2[:, 0, :], SC * SC))
                    ch.link(dve.memset(sq2[:, 1, :], 1.0))
                    for n in range(8):
                        dve.wait_ge(s_wt, n + 1)
                        to = wqkv[:, :, n * P:n * P + P] if n < 6 else wproj[:, :, (n - 6) * P:(n - 5) * P]
                        dve.tensor_copy(to, pT[:, :, :]).then_inc(s_wc, 1)
                    dve.wait_ge(s_cst, 11)


                    def products(j, u):
                        dve.wait_ge(s_kn2, j + 1)
                        gated(dve, "dve", s_kv, j + 1)
                        features(dve, KF[:, u, :], kn[:, u, :, :]).then_inc(s_kf, 1)

                    def front(j, u):
                        dve.wait_ge(s_zc, j + 1)
                        dve.tensor_scalar(elr[:, bass.ds(j, 1), :].rearrange("p a c -> p (a c)"),
                                          pZ[:, C:C + 4], 1.0, None, ALU.mult).then_inc(s_elr, 1)
                        dve.wait_ge(s_q, j + 1)
                        dve.tensor_tensor(qkv[:, :], pQ[:, 0:3 * C], bq[:, :], ALU.add).then_inc(s_qv, 1)

                    def norms(j):
                        flat = nrm[:, :, :].rearrange("p a h -> p (a h)")
                        dve.wait_ge(s_sq, j + 1)
                        ch.link(dve.tensor_reduce(flat, sqk[:, :].rearrange("p (g d) -> p g d", d=DM), AX_X, ALU.add))
                        ch.link(dve.tensor_tensor(nrm[:, :, :], nrm[:, :, :], sq2[:, :, :], ALU.mult))
                        dve.tensor_scalar(flat, flat, EPS_NORM ** 2, None, ALU.max).then_inc(s_n2, 1)

                    def rest(j, u):
                        dve.tensor_tensor(KF[:, u, HM * MAIN:HM * MAIN + HM * DM].rearrange("p (h i) -> p h i", h=HM),
                                          kn[:, u, :, 0:DM], kn[:, u, :, 16:16 + DM], ALU.mult).then_inc(s_kf, 1)

                    def scaled(j, u):
                        flat = nrm[:, :, :].rearrange("p a h -> p (a h)")
                        dve.wait_ge(s_rt, j + 1)
                        ch.link(dve.reciprocal(flat, rt[:, :]))
                        ch.link(dve.tensor_tensor(nrm[:, :, :], nrm[:, :, :], fac[:, :, :], ALU.mult))
                        gated(dve, "dve", s_kf, j * 2 + 2)
                        gated(dve, "dve", s_kl, j + 1)
                        dve.tensor_tensor(kn[:, u, :, 0:DM], qkv[:, C:2 * C].rearrange("p (h d) -> p h d", h=HM),
                                          bcast(nrm[:, 1, :], DM), ALU.mult).then_inc(s_kn, 1)
                        ch.inc(dve.tensor_tensor(QN[:, bass.ds(j, 1), :].rearrange("p a (h d) -> p (a h) d", h=HM),
                                                 qkv[:, 0:C].rearrange("p (h d) -> p h d", h=HM),
                                                 bcast(nrm[:, 0, :], DM), ALU.mult))
                        gated(dve, "dve", s_kv, j + 1)
                        ch.inc(dve.tensor_scalar(v1[:, u, :, 1:V1], qkv[:, 2 * C:3 * C].rearrange("p (h d) -> p h d", h=HM),
                                                 mask[:, bass.ds(j, 1)], None, ALU.mult))
                        ch.link(dve.tensor_scalar(v1[:, u, :, 0:1], bcast(ones[:, 0:HM], 1),
                                                  mask[:, bass.ds(j, 1)], None, ALU.mult))
                        dve.sem_inc(s_v, 1)

                    def tile(j, u, back=True):
                        front(j, u)
                        if back:
                            products(j + (-1), 1 - u)
                        norms(j)
                        if back:
                            rest(j + (-1), 1 - u)
                        scaled(j, u)

                    tile(0, 0, back=False)
                    tile(1, 1)
                    with dve.Fori(0, PAIRS - 1) as i:
                        ch.enter(i, 2 * 7)
                        tile(i * 2 + 2, 0)
                        tile(i * 2 + 3, 1)
                        ch.leave(PAIRS - 1)
                    products(NT - 1, 1)
                    rest(NT - 1, 1)
                    dve.wait_ge(s_kv, NT + 2)
                    for c in range(QUADS):
                        w = w8[:, 0:1] if c % 4 == 0 else 1.0
                        ch.inc(dve.tensor_scalar(KVS[:, c, :], kv_place(c), w, None, ALU.mult))
                    for g in range(4):
                        w = 0.5 if g < 2 else SC * SC
                        ch.inc(dve.scalar_tensor_tensor(out=KV4[:, g, :].rearrange("p (h e) -> p h e", h=4),
                                                        in0=kv_place(QUADS + g).rearrange("p (h e) -> p h e", h=4),
                                                        scalar=w, in1=bcast(head_of[:, :], V1),
                                                        op0=ALU.mult, op1=ALU.mult))
                    ch.inc(dve.tensor_scalar(VS[:, :], VSUM, SC ** 4, None, ALU.mult))
                    gated(dve, "dve", s_dve, ch.total + ch.n)

                @block.tensor
                def _(pe):
                    pe.wait_ge(s_nw, 32)
                    for n in range(8):
                        if n:
                            pe.wait_ge(s_wc, n)
                        for c in range(2):
                            mm = pe.transpose(pT[:, c, :], wnat[:, n, c * P:c * P + P], ident[:, :])
                        mm.then_inc(s_wt, 1)
                    pe.wait_ge(s_wc, 8)
                    pe.wait_ge(s_cst, 5)
                    for n in range(4):
                        mm = pe.matmul(pKV[n][:, :], zero[:, 0:P], zero[:, :], start=True, stop=False,
                                       skip_group_check=True)
                    mm.then_inc(s_init, 1)
                    pe.wait_ge(s_init, 1)
                    pe.sem_inc(s_kv, 2)
                    pe.sem_inc(s_t, 2)

                    def key_side(j, u):
                        gated(pe, "pe", s_kf, j * 2 + 6)
                        gated(pe, "pe", s_kl, j + 3)
                        gated(pe, "pe", s_v, j + 1)
                        for c in range(CH):
                            if c < QUADS:
                                rhs = v1[:, u, c // 4, :]
                            else:
                                rhs = v1[:, u, 4 * (c % 2):4 * (c % 2) + 4, :].rearrange("p h e -> p (h e)")
                            pe.matmul(kv_place(c), KF[:, u, c * P:(c + 1) * P], rhs, start=False, stop=False,
                                      skip_group_check=True)
                        pe.matmul(VSUM, ones[:, :], v1[:, u, :, :].rearrange("p h e -> p (h e)"),
                                  start=False, stop=False, skip_group_check=True).then_inc(s_kv, 1)

                    def project(j, u):
                        pe.wait_ge(s_xs, j + 1)
                        for c in range(2):
                            mm = pe.transpose(pT[:, c, :], xs[:, u, c * P:c * P + P], ident[:, :])
                        mm.then_inc(s_t, 1)
                        gated(pe, "pe", s_xt, j + 1)
                        gated(pe, "pe", s_elr, j + 1)
                        for c in range(2):
                            mm = pe.matmul(pZ[:, 0:C + 4], xT[:, u, c, :], wz[:, c, :], start=c == 0, stop=c == 1)
                        mm.then_inc(s_z, 1)
                        pe.wait_ge(s_qv, j + 1)
                        for a, b in ((0, 512), (512, 768)):
                            for c in range(2):
                                mm = pe.matmul(pQ[:, a:b], xT[:, u, c, :], wqkv[:, c, a:b], start=c == 0, stop=c == 1)
                        mm.then_inc(s_q, 1)

                    pe.sem_inc(s_elr, 1)
                    pe.sem_inc(s_qv, 1)
                    pe.sem_inc(s_kf, 4)
                    pe.sem_inc(s_kl, 2)
                    project(0, 0)
                    project(1, 1)
                    with pe.Fori(0, PAIRS - 1) as i:
                        for u in range(2):
                            project(i * 2 + (2 + u), u)
                            key_side(i * 2 + u, u)
                    key_side(NT - 2, 0)
                    key_side(NT - 1, 1)

                @block.scalar
                def _(act):
                    for u in range(2):
                        act.sem_inc(s_zd[u], 16)

                    def normalised(j, u):
                        gated(act, "act", s_t, j + 1)
                        act.activation(xs[:, u, :], QN[:, bass.ds(j, 1), :].rearrange("p a c -> p (a c)"), ACT.Copy,
                                       scale=rs[:, bass.ds(j, 1)]).then_inc(s_xs, 1)

                    def transposed(j, u):
                        act.wait_ge(s_t, j + 3)
                        act.copy(xT[:, u, :, :], pT[:, :, :]).then_inc(s_xt, 1)

                    def z_out(j, pair, u):
                        act.wait_ge(s_z, j + 1)
                        gated(act, "act", s_zd[u], pair * 16 + 16)
                        act.copy(zs[:, u, :], pZ[:, 0:C]).then_inc(s_zc, 1)

                    def squares(j):
                        act.wait_ge(s_qv, j + 2)
                        act.activation(sqk[:, :], qkv[:, 0:2 * C], ACT.Square).then_inc(s_sq, 1)

                    def root(j):
                        act.wait_ge(s_n2, j + 1)
                        act.activation(rt[:, :], nrm[:, :, :].rearrange("p a h -> p (a h)"), ACT.Sqrt).then_inc(s_rt, 1)

                    def copies(j, u):
                        act.wait_ge(s_kn, j + 1)
                        act.copy(kn[:, u, :, DM:2 * DM], kn[:, u, :, 0:DM]).then_inc(s_kn2, 1)
                        gated(act, "act", s_kv, j + 1)
                        act.copy(KF[:, u, HM * MAIN + HM * DM:FEAT].rearrange("p (h i) -> p h i", h=HM),
                                 kn[:, u, :, 0:DM]).then_inc(s_kl, 1)

                    def tile(j, pair, u, ahead=2):
                        squares(j)
                        if ahead >= 1:
                            transposed(j + 1, 1 - u)
                        root(j)
                        if ahead >= 1:
                            z_out(j + 1, pair + u, 1 - u)
                        copies(j, u)
                        if ahead >= 2:
                            normalised(j + 2, u)

                    normalised(0, 0)
                    transposed(0, 0)
                    z_out(0, 0, 0)
                    normalised(1, 1)
                    with act.Fori(0, PAIRS - 1) as i:
                        for u in range(2):
                            tile(i * 2 + u, i, u)
                    tile(NT - 2, PAIRS - 1, 0, ahead=1)
                    tile(NT - 1, PAIRS - 1, 1, ahead=0)
        c1.close()
        query_side(nc, sb, pb, sem, gated, ident, X, QN, KVS, KV4, VS, wproj, bsum)


def features(eng, out, kn):
    part = list(kn.ap[0])
    same = bass.AP(kn.tensor, kn.offset, [part, [2 * DM, HM], [0, 16], [1, DM]])
    window = bass.AP(kn.tensor, kn.offset, [part, [2 * DM, HM], [1, 16], [1, DM]])
    main = out[:, 0:HM * MAIN].rearrange("p (h d i) -> p h d i", h=HM, d=16)
    return eng.tensor_tensor(main, same, window, ALU.mult)


def query_side(nc, sb, pb, sem, gated, ident, X, QN, KVS, KV4, VS, wproj, bsum):
    ctx = ExitStack()
    with ctx:
        sem = ctx.enter_context(phase_semaphores(nc))
        t = lambda name, shape: sb(name, shape, F32, at=ctx)
        q2 = t("q2", [P, 2, HM, 2 * DM])
        QF = t("QF", [P, 2, FEAT])
        QT = t("QT", [P, 2, CH, P])
        rec = t("rec", [P, HM])
        yo = t("yo", [P, 2, C])
        yT = t("yT", [P, 2, P])
        ot = t("ot", [P, C])
        pT = [pb(f"qT{n}", [P, 4, P], ctx) for n in range(3)]
        pY = [pb(f"qY{n}", [P, HM, V1], ctx) for n in range(2)]
        pYT = pb("qYT", [P, 2, P], ctx)
        pO = pb("qO", [P, C], ctx)
        s_dve, s_f, s_l, s_q2, s_t, s_tc, s_y, s_yo, s_yt, s_yc, s_o, s_or = [sem("q_" + n) for n in (
            "dve", "products", "linear", "doubled", "T", "T_copied", "y", "y_divided", "yT", "yT_copied", "projected",
            "projection_read")]
        G = CH // 4
        with nc.Block() as block:
            @block.vector
            def _(dve):
                ch = Count(dve, s_dve)

                def query_features(j, u):
                    dve.wait_ge(s_q2, j + 1)
                    gated(dve, "dve", s_t, j * G + G)
                    ch.link(features(dve, QF[:, u, :], q2[:, u, :, :]))
                    ch.link(dve.tensor_tensor(QF[:, u, HM * MAIN:HM * MAIN + HM * DM].rearrange("p (h i) -> p h i", h=HM),
                                              q2[:, u, :, 0:DM], q2[:, u, :, 16:16 + DM], ALU.mult))
                    dve.sem_inc(s_f, 1)

                def divide(j, u):
                    dve.wait_ge(s_y, j + 1)
                    ch.link(dve.reciprocal(rec[:, :], pY[u][:, :, 0:1].rearrange("p h e -> p (h e)")))
                    ch.link(dve.tensor_tensor(yo[:, u, :].rearrange("p (h d) -> p h d", h=HM), pY[u][:, :, 1:V1],
                                              bcast(rec[:, :], DM), ALU.mult))
                    dve.sem_inc(s_yo, 1)

                def add_to_stream(j):
                    xk = X[:, bass.ds(j, 1), :].rearrange("p a c -> p (a c)")
                    dve.wait_ge(s_o, j + 1)
                    ch.link(dve.tensor_tensor(ot[:, :], pO[:, :], bsum[:, :], ALU.add))
                    dve.sem_inc(s_or, 1)
                    ch.link(dve.tensor_tensor(xk, xk, ot[:, :], ALU.add))

                def tile(j, u):
                    query_features(j, u)
                    divide(j + (-2), u)
                    add_to_stream(j + (-3))

                query_features(0, 0)
                query_features(1, 1)
                query_features(2, 0)
                divide(0, 0)
                tile(3, 1)
                with dve.Fori(0, PAIRS - 2) as i:
                    ch.enter(i, 2 * 6)
                    for u in range(2):
                        tile(i * 2 + (4 + u), u)
                    ch.leave(PAIRS - 2)
                divide(NT - 2, 0)
                add_to_stream(NT - 3)
                divide(NT - 1, 1)
                add_to_stream(NT - 2)
                add_to_stream(NT - 1)

            @block.tensor
            def _(pe):
                pe.sem_inc(s_t, 2 * G)
                pe.sem_inc(s_or, 1)
                pe.sem_inc(s_tc, 3)

                def turn(j, g, u):
                    pe.wait_ge(s_tc, j * G + (g + 1))
                    for c in range(4 * g, 4 * g + 4):
                        mm = pe.transpose(pT[g % 3][:, c % 4, :], QF[:, u, c * P:(c + 1) * P], ident[:, :])
                    mm.then_inc(s_t, 1)

                def y_chunk(j, g, u):
                    flat = pY[u][:, :, :].rearrange("p h e -> p (h e)")
                    if g == 0:
                        pe.wait_ge(s_tc, j * G + (G + 3))
                        pe.matmul(flat, ident[:, :], VS[:, :], start=True, stop=False, skip_group_check=True)
                    for c in range(4 * g, 4 * g + 4):
                        if c < QUADS:
                            h, nh, rhs = c // 4, 1, KVS[:, c, :]
                        else:
                            h, nh, rhs = 4 * (c % 2), 4, KV4[:, c - QUADS, :]
                        mm = pe.matmul(flat[:, h * V1:(h + nh) * V1], QT[:, u, c, :], rhs, start=False,
                                       stop=c == CH - 1, skip_group_check=True)
                    if g == G - 1:
                        mm.then_inc(s_y, 1)

                def project(j, u):
                    pe.wait_ge(s_yo, j + 1)
                    for c in range(2):
                        mm = pe.transpose(pYT[:, c, :], yo[:, u, c * P:c * P + P], ident[:, :])
                    mm.then_inc(s_yt, 1)

                def project_out(j):
                    pe.wait_ge(s_yc, j + 1)
                    gated(pe, "pe", s_or, j + 1)
                    for c in range(2):
                        mm = pe.matmul(pO[:, :], yT[:, c, :], wproj[:, c, :], start=c == 0, stop=c == 1)
                    mm.then_inc(s_o, 1)

                def tile(j, u, turns=True, ys=True, out=True):
                    if turns:
                        gated(pe, "pe", s_f, j + 3)
                        gated(pe, "pe", s_l, j + 1)
                    for g in range(G):
                        if turns:
                            turn(j, g, u)
                        if ys:
                            y_chunk(j + (-1), g, 1 - u)
                        if out and g == 2:
                            project(j + (-2), u)
                        if out and g == 5:
                            project_out(j + (-2))

                tile(0, 0, ys=False, out=False)
                tile(1, 1, out=False)
                with pe.Fori(0, PAIRS - 1) as i:
                    for u in range(2):
                        tile(i * 2 + (2 + u), u)
                tile(NT, 0, turns=False)
                tile(NT + 1, 1, turns=False, ys=False)

            @block.scalar
            def _(act):
                def doubled(j, u):
                    row = QN[:, bass.ds(j, 1), :].rearrange("p a (h d) -> p (a h) d", h=HM)
                    gated(act, "act", s_f, j + 1)
                    for half in range(2):
                        ins = act.copy(q2[:, u, :, DM * half:DM * half + DM], row)
                    ins.then_inc(s_q2, 1)
                    gated(act, "act", s_q2, j + 1)
                    gated(act, "act", s_t, j * G + G)
                    act.copy(QF[:, u, HM * MAIN + HM * DM:FEAT].rearrange("p (h i) -> p h i", h=HM),
                             q2[:, u, :, 0:DM]).then_inc(s_l, 1)

                def yT_out(j):
                    act.wait_ge(s_yt, j + 1)
                    act.copy(yT[:, :, :], pYT[:, :, :]).then_inc(s_yc, 1)

                def tile(j, u, ahead=True, out=True):
                    for g in range(G):
                        act.wait_ge(s_t, j * G + (2 * G + g + 1))
                        act.copy(QT[:, u, 4 * g:4 * g + 4, :], pT[g % 3][:, :, :]).then_inc(s_tc, 1)
                        if out and g == 3:
                            yT_out(j + (-2))
                    if ahead:
                        doubled(j + 2, u)

                act.sem_inc(s_f, 2)
                doubled(0, 0)
                doubled(1, 1)
                tile(0, 0, out=False)
                tile(1, 1, out=False)
                with act.Fori(0, PAIRS - 2) as i:
                    for u in range(2):
                        tile(i * 2 + (2 + u), u)
                tile(NT - 2, 0, ahead=False)
                tile(NT - 1, 1, ahead=False)
                yT_out(NT - 2)
                yT_out(NT - 1)


def to_tiles(pe, mm_sem, rd_sem, base, pt, ident, src):
    for j in range(JT):
        if base + j:
            pe.wait_ge(rd_sem, base + j)
        pe.transpose(pt[:, :], src[:, j * P:j * P + P], ident[:, :]).then_inc(mm_sem, 1)


def prepare_edges(nc, sb, pb, sem, ident, src, dst, D, T):
    ctx = ExitStack()
    with ctx:
        sem = ctx.enter_context(phase_semaphores(nc))
        t = lambda name, shape, dt=F32: sb(name, shape, dt, at=ctx)
        si, di = t("e_src", [P, COLS], I32), t("e_dst", [P, COLS], I32)
        wi, wf, wb = t("e_int", [P, COLS], I32), t("e_f32", [P, COLS]), t("e_b16", [P, COLS], BF16)
        sf, df = t("e_srcf", [P, COLS]), t("e_dstf", [P, COLS])
        zero = t("e_zero", [P, COLS])
        last = t("e_last", [P, JT])
        lastB = t("e_lastB", [P, COLS])
        dx = t("e_dx", [P, COLS + 2])
        keyB = t("e_keyB", [P, COLS])
        ends = t("e_ends", [1, 2])
        tile_i, tile_f = t("e_ti", [P, JT], I32), t("e_tf", [P, JT])
        step_i, step_f = t("e_si", [P, JT], I32), t("e_sf", [P, JT])
        before = t("e_before", [P, NT])
        less, equal, pos = t("e_less", [P, NT]), t("e_equal", [P, NT]), t("e_pos", [P, NT])
        key, tf, bf, b128 = t("e_key", [P, JT]), t("e_t", [P, JT]), t("e_b", [P, JT]), t("e_b128", [P, JT])
        brow_f, brow_i = t("e_brf", [JT, P]), t("e_bri", [JT, P], I32)
        pt = pb("e_pt", [P, P], ctx)
        s_pad, s_ld, s_w, s_b, s_dve, s_io, s_k, s_kb, s_mm, s_rd, s_br = [sem("e_" + n) for n in (
            "pad", "loaded", "written", "windowed", "dve", "iota", "keys_ready", "keys", "T", "T_read", "brow")]
        rows = E // COLS
        left = E - rows * COLS
        with nc.Block() as block:
            @block.gpsimd
            def _(pool):
                pool.memset(si[:, :], 0).then_inc(s_pad, 1)
                pool.memset(di[:, :], N - 1).then_inc(s_pad, 1)
                pool.iota(tile_i[:, :], pattern=[[1, JT]], base=0, channel_multiplier=JT).then_inc(s_io, 1)
                pool.iota(step_i[:, :], pattern=[[P, JT]], base=0, channel_multiplier=1).then_inc(s_io, 1)
                pool.wait_ge(s_io, 2)

            @block.sync
            def _(sp):
                sp.wait_ge(s_pad, 2)
                for a, b in ((src, si), (dst, di)):
                    sp.dma_start(b[0:rows, :], a[0:rows * COLS].rearrange("(p c) -> p c", c=COLS)).then_inc(s_ld, 16)
                    sp.dma_start(b[rows:rows + 1, 0:left], a[rows * COLS:E].rearrange("(a c) -> a c", a=1)).then_inc(s_ld, 16)
                sp.wait_ge(s_k, 1)
                for a, b in ((D["src_lo"], wb), (D["src"], sf), (D["dst"], df)):
                    sp.dma_start(a.rearrange("(p c) -> p c", c=COLS), b[:, :]).then_inc(s_w, 16)
                sp.dma_start(D["window"][1:1 + P * COLS].rearrange("(p c) -> p c", c=COLS), df[:, :]).then_inc(s_w, 16)
                sp.dma_start(D["window"][0:1].rearrange("(a c) -> a c", a=1), ends[:, 0:1]).then_inc(s_w, 16)
                sp.dma_start(D["window"][1 + P * COLS:2 + P * COLS].rearrange("(a c) -> a c", a=1), ends[:, 1:2]).then_inc(s_w, 16)
                sp.dma_start(D["keys"].rearrange("(p c) -> p c", c=JT), key[:, :]).then_inc(s_w, 16)
                sp.dma_start(D["last"].rearrange("(p c) -> p c", c=JT), last[:, :]).then_inc(s_w, 16)
                sp.dma_start(D["er1"].rearrange("(p c) h -> p (c h)", c=COLS), zero[:, :]).then_inc(s_w, 16)
                for h in range(2):
                    half = D["er2"][h * P * COLS // 2:(h + 1) * P * COLS // 2, :]
                    sp.dma_start(half.rearrange("(p c) h -> p (c h)", c=COLS // 2), zero[:, :]).then_inc(s_w, 16)
                sp.wait_ge(s_w, 11 * 16)
                w = D["window"]
                sp.dma_start(dx[:, :], bass.AP(w.tensor, 0, [[COLS, P], [1, COLS + 2]])).then_inc(s_b, 16)
                sp.dma_start(keyB[:, :], D["keys"].partition_broadcast(P)).then_inc(s_kb, 16)
                sp.dma_start(lastB[:, :], D["last"].partition_broadcast(P)).then_inc(s_kb, 16)
                sp.wait_ge(s_br, 1)
                sp.dma_start(D["block_of"].rearrange("(p c) -> p c", c=P), brow_i[:, :]).then_inc(s_b, 16)
                sp.wait_ge(s_b, 32)
                sp.dma_start(T["block_of"][:, :], D["block_of"].rearrange("(a c) -> a c", a=1)).then_inc(s_b, 16)
                sp.wait_ge(s_b, 48)
                sp.wait_ge(s_kb, 32)

            @block.vector
            def _(dve):
                ch = Count(dve, s_dve)
                dve.wait_ge(s_ld, 64)
                dve.wait_ge(s_io, 2)
                ch.inc(dve.tensor_copy(sf[:, :], si[:, :]))
                ch.inc(dve.tensor_copy(df[:, :], di[:, :]))
                ch.inc(dve.tensor_copy(tile_f[:, :], tile_i[:, :]))
                ch.inc(dve.tensor_copy(step_f[:, :], step_i[:, :]))
                ch.inc(dve.memset(ends[:, 0:1], -1.0))
                ch.inc(dve.memset(ends[:, 1:2], 2.0e6))
                ch.link(dve.tensor_scalar(wi[:, :], si[:, :], P - 1, None, ALU.bitwise_and))
                ch.inc(dve.tensor_copy(wb[:, :], wi[:, :]))
                ch.link(dve.tensor_scalar(si[:, :], si[:, :], 7, None, ALU.arith_shift_right))
                ch.link(dve.tensor_copy(wf[:, :], si[:, :]))
                ch.inc(dve.memset(zero[:, :], 0.0))
                ch.inc(dve.tensor_copy(last[:, :], di[:, P - 1:COLS:P]))
                ch.link(dve.tensor_copy(T["first_dst"][:, :], di[:, 0:1]))
                ch.link(dve.tensor_scalar(di[:, :], di[:, :], 7, None, ALU.arith_shift_right))
                ch.link(dve.tensor_copy(key[:, :], di[:, P - 1:COLS:P]))
                ch.link(dve.tensor_tensor(key[:, :], key[:, :], tile_f[:, :], ALU.add))
                ch.link(dve.tensor_copy(wi[:, :], T["edge_no"][:, :]))
                ch.link(dve.tensor_copy(keyB[:, :], wi[:, :]))
                ch.link(dve.tensor_scalar(keyB[:, :], keyB[:, :], E - 0.5, 1.0e6, ALU.is_gt, ALU.mult))
                ch.link(dve.tensor_tensor(df[:, :], df[:, :], keyB[:, :], ALU.add))
                dve.sem_inc(s_k, 1)
                for j in range(JT):
                    dve.wait_ge(s_mm, j + 1)
                    dve.tensor_copy(T["src_hi"][:, j:COLS:JT], pt[:, :]).then_inc(s_rd, 1)
                dve.wait_ge(s_b, 16)
                ch.link(dve.tensor_tensor(T["same"][:, :], dx[:, 0:COLS], dx[:, 1:1 + COLS], ALU.is_equal))
                for a, b, c in ((T["starts"], 0, 1), (T["ends"], 2, 1)):
                    ch.link(dve.tensor_tensor(a[:, :], dx[:, b:b + COLS], dx[:, c:c + COLS], ALU.not_equal))
                    ch.link(dve.tensor_scalar(a[:, :], a[:, :], -BIG, None, ALU.mult))
                for a, n in ((T["starts"], 0), (T["ends"], 1)):
                    ch.link(dve.tensor_reduce(T["chain"][:, n:n + 1], a[:, :], AX_X, ALU.add))
                dve.wait_ge(s_kb, 32)
                for j in range(JT):
                    ch.link(dve.tensor_scalar(wf[:, :], keyB[:, :], step_f[:, j:j + 1], 0.0, ALU.is_lt, ALU.add,
                                              accum_out=tf[:, j:j + 1]))
                ch.link(dve.tensor_copy(T["tile_of"][:, :], tf[:, :]))
                ch.link(dve.tensor_tensor(bf[:, :], step_f[:, :], tf[:, :], ALU.subtract))
                ch.link(dve.tensor_scalar(T["first_node"][:, :], bf[:, :], float(P), None, ALU.mult))
                dve.sem_inc(s_k, 1)
                for k in range(NT):
                    ch.link(dve.tensor_scalar(wf[:, :], lastB[:, :], T["node"][:, k:k + 1], 0.0, ALU.is_lt, ALU.add,
                                              accum_out=before[:, k:k + 1]))
                ch.link(dve.tensor_scalar(before[:, :], before[:, :], float(ETP - 1), None, ALU.min))
                ch.link(dve.tensor_copy(T["row_tile"][:, :], before[:, :]))
                dve.wait_ge(s_mm, JT + 1)
                ch.link(dve.tensor_copy(brow_i[:, :], pt[0:JT, :]))
                dve.sem_inc(s_br, 1)

            @block.tensor
            def _(pe):
                pe.wait_ge(s_k, 1)
                to_tiles(pe, s_mm, s_rd, 0, pt, ident, wf)
                pe.wait_ge(s_k, 2)
                pe.wait_ge(s_rd, JT)
                pe.transpose(pt[0:JT, :], bf[:, :], ident[:, :]).then_inc(s_mm, 1)

        g = ExitStack()
        with g:
            G = [sb(f"e_g{n}", [P, 2, P], F32, at=g) for n in range(2)]
            pp = pb("e_pp", [P, 2, P], g)
            s_g = [sem(f"e_rows{n}") for n in range(2)]
            s_l, s_m, s_r = sem("e_local"), sem("e_rowT"), sem("e_rowT_read")
            s_dve = sem("e_dve2")
            with nc.Block() as block:
                @block.gpsimd
                def _(pool):
                    for j in range(JT):
                        if j >= 2:
                            pool.wait_ge(s_m, j - 1)
                        off = bass.IndirectOffsetOnAxis(ap=T["tile_of"][:, j:j + 1], axis=0)
                        for a, name in enumerate(("src", "dst")):
                            pool.indirect_dma_start(G[j % 2][:, a, :], None, D[name].rearrange("(t e) -> t e", e=P),
                                                    off).then_inc(s_g[j % 2], 16)

                @block.vector
                def _(dve):
                    for j in range(JT):
                        dve.wait_ge(s_g[j % 2], 32 * (j // 2 + 1))
                        dve.tensor_scalar(G[j % 2][:, 1, :], G[j % 2][:, 1, :], T["first_node"][:, j:j + 1], None,
                                          ALU.subtract).then_inc(s_l, 1)
                        dve.wait_ge(s_m, j + 1)
                        dve.tensor_copy(T["src_of"][:, j * P:j * P + P], pp[:, 0, :]).then_inc(s_r, 1)
                        dve.tensor_copy(T["dst_of"][:, j * P:j * P + P], pp[:, 1, :]).then_inc(s_r, 1)

                @block.tensor
                def _(pe):
                    for j in range(JT):
                        pe.wait_ge(s_l, j + 1)
                        if j:
                            pe.wait_ge(s_r, 2 * j)
                        for a in range(2):
                            mm = pe.transpose(pp[:, a, :], G[j % 2][:, a, :], ident[:, :])
                        mm.then_inc(s_m, 1)

        g = ExitStack()
        with g:
            NS = 5
            G = [sb(f"r_g{n}", [P, P], F32, at=g) for n in range(NS)]
            J = sb("r_j", [P, 2, P], F32, at=g)
            s_g = [sem(f"r_rows{n}") for n in range(NS)]
            s_u, s_dve = sem("r_used"), sem("r_dve")
            with nc.Block() as block:
                @block.gpsimd
                def _(pool):
                    for k in range(NT):
                        if k >= NS:
                            pool.wait_ge(s_u, k - NS + 1)
                        pool.indirect_dma_start(G[k % NS][:, :], None, D["dst"].rearrange("(t e) -> t e", e=P),
                                                bass.IndirectOffsetOnAxis(ap=T["row_tile"][:, k:k + 1], axis=0)
                                                ).then_inc(s_g[k % NS], 16)

                @block.vector
                def _(dve):
                    ch = Count(dve, s_dve)
                    for k in range(NT):
                        dve.wait_ge(s_g[k % NS], 16 * (k // NS + 1))
                        for a, (op, to) in enumerate(((ALU.is_lt, less), (ALU.is_equal, equal))):
                            ch.link(dve.tensor_scalar(J[:, a, :], G[k % NS][:, :], T["node"][:, k:k + 1], 0.0, op, ALU.add,
                                                      accum_out=to[:, k:k + 1]))
                        dve.sem_inc(s_u, 1)
                    ch.link(dve.tensor_scalar(equal[:, :], equal[:, :], 0.5, 1.0e6, ALU.is_lt, ALU.mult))
                    ch.link(dve.scalar_tensor_tensor(out=pos[:, :], in0=before[:, :], scalar=float(P), in1=less[:, :],
                                                     op0=ALU.mult, op1=ALU.add))
                    ch.link(dve.tensor_tensor(pos[:, :], pos[:, :], equal[:, :], ALU.add))
                    ch.link(dve.tensor_copy(T["first_edge"][:, :], pos[:, :]))


def edge_softmax(nc, sb, pb, sem, gated, ident, iota, elr, er_col, D, T, H, L):
    ctx = ExitStack()
    with ctx:
        sem = ctx.enter_context(phase_semaphores(nc))
        t = lambda name, shape, dt=F32: sb(f"{name}{L}", shape, dt, at=ctx)
        S = lambda *names: [sem(f"{n}{L}") for n in names]
        val = t("l_val", [P, ETP, H])
        init = t("l_init", [P, 4])
        erc = t("l_erc", [P, COLS * H])
        er_dram = D["er%d" % H]
        c1 = ExitStack()
        with c1:
            t1 = lambda name, shape, dt=F32: sb(f"{name}{L}", shape, dt, at=c1)
            K = NT
            parts = t1("l_parts", [P, 3, H * K], BF16)
            whole, back = t1("l_whole", [P, H, K]), t1("l_back", [P, H * K])
            bcs = t1("l_lo", [P, 2, UA * P], BF16)
            pick = t1("l_pick", [P, 2, UA * P], BF16)
            own = t1("l_own", [P, 1])
            junk = t1("l_junk", [P, 2, UA, H, K])
            got = t1("l_got", [P, 2, UA, H])
            banks = [pb(f"l_b{n}{L}", [P, 4, H * K], c1) for n in range(8)]
            s_dve, s_lo0, s_lo1, s_pk, s_mm, s_rd, s_er, s_init, s_tab, s_erl = S(
                "l_dve", "l_lo0", "l_lo1", "l_pick", "l_mm", "l_read", "l_er", "l_init", "l_table", "l_er_loaded")
            s_lo = [s_lo0, s_lo1]
            GR = UA // 4
            with nc.Block() as block:
                @block.gpsimd
                def _(pool):
                    for k in range(NT):
                        pool.indirect_dma_start(er_dram, bass.IndirectOffsetOnAxis(ap=T["first_edge"][:, k:k + 1], axis=0),
                                                elr[:, k, er_col:er_col + H], None, bounds_check=P * COLS - 1,
                                                oob_is_err=False).then_inc(s_er, 16)
                    pool.wait_ge(s_tab, 16)
                    pool.indirect_dma_start(init[:, :], None, D["terms"], bass.IndirectOffsetOnAxis(
                        ap=T["first_dst"][:, 0:1], axis=0)).then_inc(s_init, 16)
                    pool.wait_ge(s_er, NT * 16)
                    pool.wait_ge(s_init, 16)

                @block.scalar
                def _(act):
                    act.dma_start(D["terms"].rearrange("(k p) c -> p k c", p=P), elr[:, :, :]).then_inc(s_tab, 16)
                    act.wait_ge(s_er, NT * 16)
                    act.dma_start(erc[:, :], er_dram.rearrange("(p c) h -> p (c h)", c=COLS)).then_inc(s_erl, 16)
                    act.wait_ge(s_erl, 16)
                    act.wait_ge(s_tab, 16)

                @block.sync
                def _(sp):
                    def load(i, u):
                        row = D["src_lo"][bass.ds(i * (2 * UA * P) + u * UA * P, UA * P)]
                        sp.dma_start(bcs[:, u, :], row.partition_broadcast(P)).then_inc(s_lo[u], 16)

                    with sp.Fori(0, AIT) as i:
                        for u in range(2):
                            gated(sp, "sp", s_pk, i * 2 + (u + 1))
                            load(i, u)
                    sp.wait_ge(s_pk, AIT * 2 + 1)
                    load(AIT, 0)

                @block.tensor
                def _(pe):
                    with pe.Fori(0, AIT) as i:
                        for u in range(2):
                            pe.wait_ge(s_pk, i * 2 + (2 + u + 1))
                            for g in range(GR):
                                gated(pe, "pe", s_rd, i * (2 * GR) + (u * GR + g + 1))
                                for q in range(4):
                                    for part in range(3):
                                        mm = pe.matmul(banks[u * GR + g][:, q, :], pick[:, u, (4 * g + q) * P:(4 * g + q + 1) * P],
                                                       parts[:, part, :], start=part == 0, stop=part == 2)
                                mm.then_inc(s_mm, 1)

                @block.vector
                def _(dve):
                    ch = Count(dve, s_dve)
                    for h in range(H):
                        ch.inc(dve.tensor_copy(whole[:, h, :], elr[:, :, h]))
                    ch.link(dve.tensor_copy(own[:, :], T["node"][:, 0:1]))
                    flat = whole[:, :, :].rearrange("p h k -> p (h k)")
                    for part in range(3):
                        ch.link(dve.tensor_copy(parts[:, part, :], flat))
                        if part < 2:
                            ch.link(dve.tensor_copy(back[:, :], parts[:, part, :]))
                            ch.link(dve.tensor_tensor(flat, flat, back[:, :], ALU.subtract))
                    dve.sem_inc(s_rd, 2 * GR)
                    dve.sem_inc(s_pk, 2)

                    def one_hot(u, need):
                        dve.wait_ge(s_lo[u], need)
                        dve.tensor_scalar(pick[:, u, :], bcs[:, u, :], own[:, 0:1], None, ALU.is_equal).then_inc(s_pk, 1)

                    one_hot(0, 16)
                    with dve.Fori(0, AIT) as i:
                        ch.enter(i, 2)
                        for u in range(2):
                            one_hot(1 - u, i * 16 + 16 * (1 + u))
                            for g in range(GR):
                                dve.wait_ge(s_mm, i * (2 * GR) + (u * GR + g + 1))
                                for q in range(4 * g, 4 * g + 4):
                                    for h in range(H):
                                        ins = dve.scalar_tensor_tensor(
                                            out=junk[:, u, q, h, :], in0=iota[:, 0:K],
                                            scalar=T["src_hi"][:, bass.ds(i * (2 * UA) + (u * UA + q), 1)],
                                            in1=banks[u * GR + g][:, q % 4, h * K:h * K + K], op0=ALU.is_equal, op1=ALU.mult,
                                            accum_out=got[:, u, q, h:h + 1])
                                ins.then_inc(s_rd, 1)
                            gated(dve, "dve", s_rd, i * (2 * GR) + (2 * GR + GR * (u + 1)))
                            to = val[:, bass.ds(i * (2 * UA) + u * UA, UA), :].rearrange("p t h -> p (t h)")
                            ch.link(dve.tensor_scalar(to, got[:, u, :, :].rearrange("p t h -> p (t h)"), 1.0, None, ALU.mult))
                        ch.leave(AIT)

        c2 = ExitStack()
        with c2:
            t2 = lambda name, shape, dt=F32: sb(f"{name}{L}", shape, dt, at=c2)
            vP = [[t2(f"l_P{s}{h}", [P, COLS]) for h in range(H)] for s in range(2)]
            F, M, W = t2("m_F", [P, COLS]), t2("m_M", [P, COLS]), t2("m_W", [P, COLS])
            rows_ = t2("m_rows", [1, 4, P + 2])
            carry = t2("m_carry", [P, 2])
            pt = [pb(f"m_pt{n}{L}", [P, P], c2) for n in range(2)]
            pr = pb(f"m_pr{L}", [1, 2, P], c2)
            pc = pb(f"m_pc{L}", [P, 2], c2)
            s_dve, s_mm, s_rd, s_row, s_mr, s_ex, s_exd = S("m_dve", "m_T", "m_T_read", "m_row", "m_mr", "m_e", "m_stored")
            with nc.Block() as block:
                @block.tensor
                def _(pe):
                    for n in range(H * JT):
                        if n >= 2:
                            pe.wait_ge(s_rd, n - 1)
                        pe.transpose(pt[n % 2][:, :], val[:, n % JT:COLS:JT, n // JT], ident[:, :]).then_inc(s_mm, 1)
                    for h in range(H):
                        for d in range(2):
                            r = 2 * (2 * h + d)
                            pe.wait_ge(s_row, r + 1)
                            pe.transpose(pr[:, 0, :], carry[:, 0:1], ident[:, :])
                            pe.transpose(pr[:, 1, :], T["chain"][:, d:d + 1], ident[:, :]).then_inc(s_mr, 1)
                            pe.wait_ge(s_row, r + 2)
                            pe.transpose(pc[:, 0:1], rows_[:, 3, d:d + P], ident[0:1, 0:1]).then_inc(s_mr, 1)

                @block.vector
                def _(dve):
                    ch = Count(dve, s_dve)
                    for h in range(H):
                        ch.link(dve.tensor_tensor_scan(vP[1][h][:, :], T["same"][:, :], erc[:, h:COLS * H:H],
                                                       init[:, er_col + h:er_col + h + 1], ALU.mult, ALU.add))
                    for n in range(H * JT):
                        j = n % JT
                        dve.wait_ge(s_mm, n + 1)
                        dve.tensor_copy(vP[0][n // JT][:, j * P:j * P + P], pt[n % 2][:, :]).then_inc(s_rd, 1)
                    dve.wait_ge(s_rd, H * JT)

                    def turn(ap, d, n):
                        return ap if d == 0 else bass.AP(ap.tensor, ap.offset + n - 1, [list(ap.ap[0]), [-1, n]])

                    for h in range(H):
                        for d, mark, v, o in ((0, T["starts"], vP[0][h], F), (1, T["ends"], F, M)):
                            r = 2 * (2 * h + d)
                            scan = lambda init: dve.tensor_tensor_scan(
                                turn(o[:, :], d, COLS), turn(mark[:, :], d, COLS), turn(v[:, :], d, COLS), init, ALU.add, ALU.max)
                            ch.link(scan(-BIG))
                            last = COLS - 1 if d == 0 else 0
                            ch.link(dve.tensor_copy(carry[:, 0:1], o[:, last:last + 1]))
                            dve.sem_inc(s_row, 1)
                            dve.wait_ge(s_mr, r + 1)
                            ch.inc(dve.tensor_copy(rows_[:, 0, 0:P], pr[:, 0, :]))
                            ch.inc(dve.tensor_copy(rows_[:, 1, 0:P], pr[:, 1, :]))
                            ch.link(dve.memset(rows_[:, 3, :], -BIG))
                            ch.link(dve.tensor_tensor_scan(turn(rows_[:, 3, 1:P + 1], d, P), turn(rows_[:, 1, 0:P], d, P),
                                                           turn(rows_[:, 0, 0:P], d, P), -BIG, ALU.add, ALU.max))
                            if d:
                                ch.link(dve.tensor_copy(rows_[:, 2, 0:P], rows_[:, 3, 1:P + 1]))
                                ch.link(dve.memset(rows_[:, 3, :], -BIG))
                                ch.link(dve.tensor_copy(rows_[:, 3, 1:P], rows_[:, 2, 1:P]))
                            dve.sem_inc(s_row, 1)
                            dve.wait_ge(s_mr, r + 2)
                            ch.link(dve.tensor_copy(carry[:, 1:2], pc[:, 0:1]))
                            ch.link(scan(carry[:, 1:2]))
                        el, er = vP[0][h], vP[1][h]
                        ch.link(dve.tensor_tensor(W[:, :], el[:, :], er[:, :], ALU.add))
                        ch.inc(dve.scalar_tensor_tensor(out=W[:, :], in0=W[:, :], scalar=0.2, in1=W[:, :], op0=ALU.mult, op1=ALU.max))
                        ch.link(dve.tensor_tensor(M[:, :], M[:, :], er[:, :], ALU.add))
                        ch.link(dve.scalar_tensor_tensor(out=M[:, :], in0=M[:, :], scalar=0.2, in1=M[:, :], op0=ALU.mult, op1=ALU.max))
                        ch.link(dve.tensor_tensor(el[:, :], W[:, :], M[:, :], ALU.subtract))
                        dve.sem_inc(s_ex, 1)

                @block.scalar
                def _(act):
                    for h in range(H):
                        act.wait_ge(s_ex, h + 1)
                        act.activation(vP[0][h][:, :], vP[0][h][:, :], ACT.Exp).then_inc(s_exd, 1)
                        act.wait_ge(s_exd, h * 17 + 1)
                        act.dma_start(D["ex"][h].rearrange("(p c) -> p c", c=COLS), vP[0][h][:, :]).then_inc(s_exd, 16)
                        act.wait_ge(s_exd, h * 17 + 17)

        c3 = ExitStack()
        with c3:
            G = [sb(f"x_g{n}{L}", [P, H, P], F32, at=c3) for n in range(2)]
            pp = pb(f"x_p{L}", [P, H, P], c3)
            s_g = S("x_rows0", "x_rows1")
            s_m, s_r = S("x_T", "x_T_read")
            with nc.Block() as block:
                @block.gpsimd
                def _(pool):
                    for j in range(JT):
                        if j >= 2:
                            pool.wait_ge(s_m, j - 1)
                        off = bass.IndirectOffsetOnAxis(ap=T["tile_of"][:, j:j + 1], axis=0)
                        for h in range(H):
                            pool.indirect_dma_start(G[j % 2][:, h, :], None, D["ex"][h].rearrange("(t e) -> t e", e=P),
                                                    off).then_inc(s_g[j % 2], 16)

                @block.tensor
                def _(pe):
                    for j in range(JT):
                        pe.wait_ge(s_g[j % 2], 16 * H * (j // 2 + 1))
                        if j:
                            pe.wait_ge(s_r, j)
                        for h in range(H):
                            mm = pe.transpose(pp[:, h, :], G[j % 2][:, h, :], ident[:, :])
                        mm.then_inc(s_m, 1)

                @block.vector
                def _(dve):
                    for j in range(JT):
                        dve.wait_ge(s_m, j + 1)
                        dve.tensor_copy(T["ex"][:, j * P:j * P + P, 0:H].rearrange("p e h -> p h e"),
                                        pp[:, :, :]).then_inc(s_r, 1)


RING = 16
HALF = RING // 2


def gather_and_sum(nc, sb, pb, sem, gated, iota, ztab, acc, T, H, L):
    ctx = ExitStack()
    with ctx:
        sem = ctx.enter_context(phase_semaphores(nc))
        G = [sb(f"g_row{n}{L}", [P, C], F32, at=ctx) for n in range(RING)]
        GS = sb(f"g_scaled{L}", [P, RING, C], F32, at=ctx)
        OH = sb(f"g_onehot{L}", [P, RING, P], F32, at=ctx)
        idx = sb(f"g_idx{L}", [P, 2, HALF], I32, at=ctx)
        ps = [pb(f"g_ps{n}{L}", [P, C + H], ctx) for n in range(HALF)]
        S = lambda *names: [sem(f"{n}{L}") for n in names]
        s_row = [sem(f"g_landed{n}{L}") for n in range(RING)]
        s_idx, s_gs, s_oh, s_mm, s_add, s_z = S("g_idx", "g_scaled", "g_onehot", "g_mm", "g_added", "g_zero")
        TURNS = (STEPS + RING - 1) // RING
        w = C // H
        with nc.Block() as block:
            @block.gpsimd
            def _(pool):
                with pool.Fori(0, TURNS) as i:
                    for half in range(2):
                        gated(pool, "pool", s_gs, i * RING + HALF * (half + 1))
                        pool.tensor_copy(idx[:, half, :], T["src_of"][:, bass.ds(i * RING + HALF * half, HALF)]).then_inc(s_idx, 1)
                        gated(pool, "pool", s_idx, i * 2 + (half + 1))
                        for q in range(HALF):
                            n = HALF * half + q
                            pool.indirect_dma_start(G[n][:, :], None, ztab, bass.IndirectOffsetOnAxis(
                                ap=idx[:, half, q:q + 1], axis=0)).then_inc(s_row[n], 16)

            @block.scalar
            def _(act):
                act.sem_inc(s_gs, RING)
                with act.Fori(0, TURNS) as i:
                    for n in range(RING):
                        if n % HALF == 0:
                            gated(act, "act", s_mm, i * RING + (n + HALF))
                        gated(act, "act", s_row[n], i * 16 + 16)
                        for h in range(H):
                            ins = act.activation(GS[:, n, h * w:h * w + w], G[n][:, h * w:h * w + w], ACT.Copy,
                                                 scale=T["ex"][:, bass.ds(i * RING + n, 1), h])
                        ins.then_inc(s_gs, 1)

            @block.tensor
            def _(pe):
                pe.sem_inc(s_mm, RING)
                with pe.Fori(0, TURNS) as i:
                    for n in range(RING):
                        gated(pe, "pe", s_oh, i * RING + (n + 1))
                        gated(pe, "pe", s_add, i * RING + (n + 1))
                        pe.wait_ge(s_gs, i * RING + (RING + n + 1))
                        pe.matmul(ps[n % HALF][:, 0:C], OH[:, n, :], GS[:, n, :], start=True, stop=True)
                        pe.matmul(ps[n % HALF][:, C:C + H], OH[:, n, :],
                                  T["ex"][:, bass.ds(i * RING + n, 1), 0:H].rearrange("p a h -> p (a h)"),
                                  start=True, stop=True).then_inc(s_mm, 1)

            @block.vector
            def _(dve):
                dve.memset(acc[:, :, :], 0.0).then_inc(s_z, 1)
                dve.sem_inc(s_add, HALF)

                def one_hot(turn, n):
                    dve.wait_ge(s_mm, turn + (n + 1))
                    dve.tensor_scalar(OH[:, n, :], iota[:, :], T["dst_of"][:, bass.ds(turn + n, 1)], None,
                                      ALU.is_equal).then_inc(s_oh, 1)

                for n in range(HALF):
                    one_hot(0, n)
                dve.wait_ge(s_z, 1)
                with dve.Fori(0, TURNS) as i:
                    for n in range(RING):
                        one_hot(i * RING + RING * ((n + HALF) // RING), (n + HALF) % RING)
                        b = dve.value_load(T["block_of"][0:1, bass.ds(i * RING + n, 1)], min_val=0, max_val=NT - 1)
                        to = acc[:, bass.ds(b, 1), :].rearrange("p a c -> p (a c)")
                        gated(dve, "dve", s_mm, i * RING + (RING + n + 1))
                        dve.wait_ge(s_add, i * RING + (HALF + n))
                        dve.tensor_tensor(to, to, ps[n % HALF][:, :], ALU.add).then_inc(s_add, 1)


def divide_by_sum(nc, sem, acc, small, H, L, bias=None, X=None):
    s_dve = sem(f"d_dve{L}")
    w = C // H
    with nc.Block() as block:
        @block.vector
        def _(dve):
            ch = Count(dve, s_dve)
            ch.link(dve.tensor_scalar(small[:, :, 0:H], acc[:, :, C:C + H], 1.0e-30, None, ALU.max))
            ch.link(dve.reciprocal(small[:, :, 0:H], small[:, :, 0:H]))
            for h in range(H):
                part = acc[:, :, h * w:h * w + w]
                ch.link(dve.tensor_tensor(part, part, bcast(small[:, :, h], w), ALU.mult))
            body = acc[:, :, 0:C]
            if bias is not None:
                b = bias[:, :]
                ch.link(dve.tensor_tensor(body, body, bass.AP(b.tensor, b.offset, [list(b.ap[0]), [0, NT], [1, C]]), ALU.add))
                ch.link(dve.tensor_scalar(body, body, 0.0, None, ALU.max))
            else:
                ch.link(dve.tensor_tensor(X[:, :, :], X[:, :, :], body, ALU.add))


def second_projection(nc, sb, pb, sem, gated, ident, acc, elr, ztab, W2, al2, ar2):
    ctx = ExitStack()
    with ctx:
        sem = ctx.enter_context(phase_semaphores(nc))
        t = lambda name, shape: sb(name, shape, F32, at=ctx)
        wz, avec, prod = t("z_w", [P, 2, C + 2]), t("z_a", [P, 2, C]), t("z_prod", [P, C])
        xs, xT, zs = t("z_xs", [P, 2, C]), t("z_xT", [P, 2, 2, P]), t("z_zs", [P, 2, C])
        pT = [pb(f"z_pT{n}", [P, 2, P], ctx) for n in range(2)]
        pZ = [pb(f"z_pZ{n}", [P, C + 2], ctx) for n in range(2)]
        s_w, s_dve, s_xs, s_t, s_xt, s_z, s_zc, s_e = [sem("z_" + n) for n in (
            "w", "dve", "xs", "T", "xT", "mm", "copied", "elr")]
        s_zd = [sem(f"z_stored{u}") for u in range(2)]
        with nc.Block() as block:
            @block.sync
            def _(sp):
                sp.dma_start(wz[:, :, 0:C], W2.rearrange("(a p) n -> p a n", p=P)).then_inc(s_w, 16)
                sp.dma_start(avec[:, 0, :], al2.rearrange("h d -> (h d)").partition_broadcast(P)).then_inc(s_w, 16)
                sp.dma_start(avec[:, 1, :], ar2.rearrange("h d -> (h d)").partition_broadcast(P)).then_inc(s_w, 16)
                with sp.Fori(0, PAIRS) as i:
                    for u in range(2):
                        sp.wait_ge(s_zc, i * 2 + (u + 1))
                        sp.dma_start(ztab[bass.ds(i * (2 * P) + u * P, P), :], zs[:, u, :]).then_inc(s_zd[u], 16)
                for u in range(2):
                    sp.wait_ge(s_zd[u], 16 + PAIRS * 16)

            @block.vector
            def _(dve):
                ch = Count(dve, s_dve)
                dve.wait_ge(s_w, 48)
                for c in range(2):
                    for side in range(2):
                        ch.link(dve.tensor_tensor(prod[:, :], wz[:, c, 0:C], avec[:, side, :], ALU.mult))
                        ch.link(dve.tensor_reduce(wz[:, c, C + side:C + side + 1], prod[:, :], AX_X, ALU.add))
                with dve.Fori(0, PAIRS) as i:
                    for u in range(2):
                        dve.wait_ge(s_t, i * 2 + (u + 1))
                        dve.tensor_scalar(xs[:, u, :], acc[:, bass.ds(i * 2 + u, 1), 0:C].rearrange("p a c -> p (a c)"),
                                          1.0, None, ALU.mult).then_inc(s_xs, 1)
                    for u in range(2):
                        dve.wait_ge(s_zc, i * 2 + (u + 1))
                        dve.tensor_scalar(elr[:, bass.ds(i * 2 + u, 1), 0:2].rearrange("p a c -> p (a c)"),
                                          pZ[u][:, C:C + 2], 1.0, None, ALU.mult).then_inc(s_e, 1)

            @block.tensor
            def _(pe):
                pe.sem_inc(s_t, 2)
                pe.sem_inc(s_e, 2)
                pe.wait_ge(s_dve, 8)
                with pe.Fori(0, PAIRS) as i:
                    for u in range(2):
                        pe.wait_ge(s_xs, i * 2 + (u + 1))
                        for c in range(2):
                            mm = pe.transpose(pT[u][:, c, :], xs[:, u, c * P:c * P + P], ident[:, :])
                        mm.then_inc(s_t, 1)
                    for u in range(2):
                        pe.wait_ge(s_xt, i * 2 + (u + 1))
                        gated(pe, "pe", s_e, i * 2 + (u + 1))
                        for c in range(2):
                            mm = pe.matmul(pZ[u][:, :], xT[:, u, c, :], wz[:, c, :], start=c == 0, stop=c == 1)
                        mm.then_inc(s_z, 1)

            @block.scalar
            def _(act):
                for u in range(2):
                    act.sem_inc(s_zd[u], 16)
                with act.Fori(0, PAIRS) as i:
                    for u in range(2):
                        act.wait_ge(s_t, i * 2 + (2 + u + 1))
                        act.copy(xT[:, u, :, :], pT[u][:, :, :]).then_inc(s_xt, 1)
                    for u in range(2):
                        act.wait_ge(s_z, i * 2 + (u + 1))
                        gated(act, "act", s_zd[u], i * 16 + 16)
                        act.copy(zs[:, u, :], pZ[u][:, 0:C]).then_inc(s_zc, 1)


def attention_layers(nc, sb, pb, sem, dram, gated, ident, iota, X, elr, ztab, src, dst, b1, W2, al2, ar2):
    ctx = ExitStack()
    with ctx:
        sem = ctx.enter_context(phase_semaphores(nc))
        t = lambda name, shape, dt=F32: sb(name, shape, dt, at=ctx)
        D = {"src_lo": dram("src_lo_d", (P * COLS,), BF16), "er1": dram("er1", (P * COLS, 1), F32),
             "er2": dram("er2", (P * COLS, 2), F32), "terms": dram("terms", (NT * P, 4), F32), "last": dram("last", (COLS,), F32),
             "src": dram("src_f", (P * COLS,), F32), "dst": dram("dst_f", (P * COLS,), F32),
             "window": dram("window", (P * COLS + 2,), F32), "keys": dram("keys", (COLS,), F32),
             "block_of": dram("block_of_d", (COLS,), I32),
             "ex": [dram(f"ex{h}", (P * COLS,), F32) for h in range(2)]}
        T = {"src_hi": t("src_hi", [P, COLS]), "same": t("same", [P, COLS]), "node": t("node", [P, NT]),
             "row_tile": t("row_tile", [P, NT], I32), "first_edge": t("first_edge", [P, NT], I32),
             "first_dst": t("first_dst", [P, 1], I32),
             "starts": t("starts", [P, COLS]), "ends": t("ends", [P, COLS]), "chain": t("chain", [P, 2]),
             "tile_of": t("tile_of", [P, JT], I32), "first_node": t("first_node", [P, JT]),
             "src_of": t("src_of", [P, COLS], I32), "dst_of": t("dst_of", [P, COLS]),
             "block_of": t("block_of", [1, COLS], I32), "ex": t("ex", [P, COLS, 2])}
        bias = t("gat_bias", [P, C])
        small = t("small", [P, NT, 2])
        c0 = ExitStack()
        with c0:
            T["edge_no"] = sb("edge_no", [P, COLS], I32, at=c0)
            node_i = sb("node_i", [P, NT], I32, at=c0)
            s_i, s_b = sem("i_edge"), sem("i_bias")
            with nc.Block() as block:
                @block.gpsimd
                def _(pool):
                    pool.iota(T["edge_no"][:, :], pattern=[[1, COLS]], base=0, channel_multiplier=COLS).then_inc(s_i, 1)
                    pool.iota(node_i[:, :], pattern=[[P, NT]], base=0, channel_multiplier=1).then_inc(s_i, 1)
                    pool.wait_ge(s_i, 2)
                    pool.tensor_copy(T["node"][:, :], node_i[:, :]).then_inc(s_i, 1)

                @block.sync
                def _(sp):
                    sp.dma_start(bias[:, :], b1.rearrange("h d -> (h d)").partition_broadcast(P)).then_inc(s_b, 16)
                    sp.wait_ge(s_b, 16)
            prepare_edges(nc, sb, pb, sem, ident, src, dst, D, T)
        edge_softmax(nc, sb, pb, sem, gated, ident, iota, elr, 2, D, T, 2, "a")
        c1 = ExitStack()
        with c1:
            acc = sb("acc_a", [P, NT, C + 2], F32, at=c1)
            gather_and_sum(nc, sb, pb, sem, gated, iota, ztab, acc, T, 2, "a")
            divide_by_sum(nc, sem, acc, small, 2, "a", bias=bias)
            second_projection(nc, sb, pb, sem, gated, ident, acc, elr, ztab, W2, al2, ar2)
        edge_softmax(nc, sb, pb, sem, gated, ident, iota, elr, 1, D, T, 1, "b")
        c1 = ExitStack()
        with c1:
            acc = sb("acc_b", [P, NT, C + 1], F32, at=c1)
            gather_and_sum(nc, sb, pb, sem, gated, iota, ztab, acc, T, 1, "b")
            divide_by_sum(nc, sem, acc, small, 1, "b", X=X)


def experts(nc, sb, pb, sem, gated, ident, X, out, Wr, br, fW1, fb1, fg1, fbe1, fm1, fv1,
            fW2, fb2, fg2, fbe2, fm2, fv2, fWo, fbo):
    ctx = ExitStack()
    with ctx:
        sem = ctx.enter_context(phase_semaphores(nc))
        t = lambda name, shape, dt=F32: sb(name, shape, dt, at=ctx)
        XN = t("f_xn", [P, NT, C])
        rs = t("f_rs", [P, NT])
        c1 = ExitStack()
        with c1:
            sq, sm = sb("f_sq", [P, 10, C], F32, at=c1), sb("f_sm", [P, NT], F32, at=c1)
            layer_norm(nc, sem, "ln2", X, XN, sq, sm, rs)
        w1, w2, wo = [t(n, [P, NX, 2, C]) for n in ("f_w1", "f_w2", "f_wo")]
        wr = t("f_wr", [P, 2, NX])
        brb = t("f_br", [P, NX])
        bo = t("f_bo", [NX, C])
        pn = t("f_pn", [80, 2, P])
        par = t("f_par", [P, 2, 5, 16])
        root = t("f_root", [P, 2, 16])
        mul, add = t("f_mul", [P, 2, 16]), t("f_add", [P, 2, 16])
        xs = t("f_xs", [P, 2, C])
        xT = t("f_xT", [P, 2, 2 * P])
        h1, h2 = t("f_h1", [P, 2, 2, 2 * P]), t("f_h2", [P, 2, 2, 2 * P])
        lg, wt, m2 = t("f_lg", [P, 2, NX]), t("f_wt", [P, 2, NX]), t("f_m2", [P, 2])
        wT = t("f_wT", [NX, 2, P])
        pH1 = [pb(f"f_pH1{n}", [P, 2, 2 * P], ctx) for n in range(2)]
        pH2 = [pb(f"f_pH2{n}", [P, 2, 2 * P], ctx) for n in range(2)]
        pY = [pb(f"f_pY{n}", [P, 2, C], ctx) for n in range(2)]
        pT = pb("f_pT", [P, 2, 2 * P], ctx)
        pR = pb("f_pR", [P, 512], ctx)
        names = ("loaded par parT par_read dve root bn xs T xT logits wlog exp weights wT wT_copied bo_sum bo_read "
                 "h1 a1 h2 a2 y y_read").split()
        (s_ld, s_par, s_pt, s_pr, s_dve, s_root, s_bn, s_xs, s_t, s_xt, s_lg, s_wl, s_ex, s_w, s_wT, s_wc, s_b, s_br,
         s_h1, s_a1, s_h2, s_a2, s_y, s_yr) = [sem("f_" + n) for n in names]
        s_done, s_out = sem("f_done"), sem("f_out")
        with nc.Block() as block:
            @block.sync
            def _(sp):
                for n, stack in enumerate(((fb1, fg1, fbe1, fm1, fv1), (fb2, fg2, fbe2, fm2, fv2))):
                    for a, p in enumerate(stack):
                        sp.dma_start(pn[16 * a:16 * a + 16, n, :], p.rearrange("e (c p) -> (e c) p", p=P)).then_inc(s_par, 16)
                sp.dma_start(wr[:, :, :], Wr.rearrange("(a p) e -> p a e", p=P)).then_inc(s_ld, 16)
                sp.dma_start(brb[:, :], br.partition_broadcast(P)).then_inc(s_ld, 16)
                sp.dma_start(bo[:, :], fbo).then_inc(s_ld, 16)
                for to, w in ((w1, fW1), (w2, fW2), (wo, fWo)):
                    for e in range(NX):
                        sp.dma_start(to[:, e, :, :], w[e].rearrange("(a p) n -> p a n", p=P)).then_inc(s_ld, 16)
                with sp.Fori(0, PAIRS - 1) as i:
                    sp.wait_ge(s_done, i + 1)
                    rows = out[bass.ds(i * (2 * P), 2 * P), :].rearrange("(k p) c -> p k c", p=P)
                    sp.dma_start(rows, X[:, bass.ds(i * 2, 2), :]).then_inc(s_out, 16)
                sp.wait_ge(s_done, PAIRS)
                sp.dma_start(out[FULL * P:N, :], X[0:REST, FULL, :]).then_inc(s_out, 16)
                sp.wait_ge(s_out, PAIRS * 16)

            @block.vector
            def _(dve):
                ch = Count(dve, s_dve)
                for n in range(2):
                    dve.wait_ge(s_pt, n + 1)
                    dve.tensor_copy(par[:, n, :, :].rearrange("p a b -> p (a b)"), pR[:, 0:80]).then_inc(s_pr, 1)
                dve.wait_ge(s_pr, 2)
                ch.link(dve.tensor_scalar(root[:, :, :], par[:, :, 4, :], EPS_BN, None, ALU.add))
                dve.sem_inc(s_bn, 1)
                dve.wait_ge(s_root, 1)
                ch.link(dve.reciprocal(root[:, :, :], root[:, :, :]))
                ch.link(dve.tensor_tensor(mul[:, :, :], par[:, :, 1, :], root[:, :, :], ALU.mult))
                ch.link(dve.tensor_tensor(add[:, :, :], par[:, :, 0, :], par[:, :, 3, :], ALU.subtract))
                ch.link(dve.tensor_tensor(add[:, :, :], add[:, :, :], mul[:, :, :], ALU.mult))
                ch.link(dve.tensor_tensor(add[:, :, :], add[:, :, :], par[:, :, 2, :], ALU.add))
                dve.sem_inc(s_bn, 1)
                dve.wait_ge(s_ld, 27 * 16)
                with dve.Fori(0, PAIRS) as i:
                    ch.enter(i, 2 + 6 + 1 + 2 * NX)
                    for u in range(2):
                        ch.link(dve.tensor_scalar(xs[:, u, :], XN[:, bass.ds(i * 2 + u, 1), :].rearrange("p a c -> p (a c)"),
                                                  rs[:, bass.ds(i * 2 + u, 1)], None, ALU.mult))
                    dve.sem_inc(s_xs, 1)
                    dve.wait_ge(s_lg, i + 1)
                    b = brb[:, :]
                    ch.link(dve.tensor_tensor(lg[:, :, :], pR[:, 0:2 * NX].rearrange("p (u e) -> p u e", u=2),
                                              bass.AP(b.tensor, b.offset, [list(b.ap[0]), [0, 2], [1, NX]]), ALU.add))
                    ch.link(dve.tensor_reduce(m2[:, :], lg[:, :, :], AX_X, ALU.max))
                    ch.link(dve.tensor_tensor(lg[:, :, :], lg[:, :, :], bcast(m2[:, :], NX), ALU.subtract))
                    dve.sem_inc(s_wl, 1)
                    dve.wait_ge(s_ex, i + 1)
                    ch.link(dve.tensor_reduce(m2[:, :], lg[:, :, :], AX_X, ALU.add))
                    ch.link(dve.reciprocal(m2[:, :], m2[:, :]))
                    ch.link(dve.tensor_tensor(wt[:, :, :], lg[:, :, :], bcast(m2[:, :], NX), ALU.mult))
                    dve.sem_inc(s_w, 1)
                    both = X[:, bass.ds(i * 2, 2), :]
                    dve.wait_ge(s_b, i + 1)
                    ch.link(dve.tensor_tensor(both, both, pT[:, :, :], ALU.add))
                    dve.sem_inc(s_br, 1)
                    for e in range(NX):
                        dve.wait_ge(s_y, i * NX + (e + 3))
                        for u in range(2):
                            xk = X[:, bass.ds(i * 2 + u, 1), :].rearrange("p a c -> p (a c)")
                            ch.inc(dve.scalar_tensor_tensor(out=xk, in0=pY[e % 2][:, u, :], scalar=wt[:, u, e:e + 1], in1=xk,
                                                            op0=ALU.mult, op1=ALU.add))
                        ch.wait()
                        dve.sem_inc(s_yr, 1)
                    dve.sem_inc(s_done, 1)
                ch.leave(PAIRS)

            @block.scalar
            def _(act):
                act.wait_ge(s_bn, 1)
                act.activation(root[:, :, :], root[:, :, :], ACT.Sqrt).then_inc(s_root, 1)
                act.wait_ge(s_bn, 2)
                act.sem_inc(s_a1, 2)
                act.sem_inc(s_a2, 2)

                def relu(i, e, p, h, layer, ready, slot, done):
                    act.wait_ge(ready, i * NX + (e + 1 + 2 * layer))
                    gated(act, "act", slot, i * NX + (e + 1))
                    for c in range(2):
                        k = 2 * e + c
                        ins = act.activation(h[:, e % 2, c, :], p[e % 2][:, c, :], ACT.Relu, bias=add[:, layer, k:k + 1],
                                             scale=mul[:, layer, k:k + 1])
                    ins.then_inc(done, 1)

                with act.Fori(0, PAIRS) as i:
                    act.wait_ge(s_t, i + 1)
                    act.copy(xT[:, :, :], pT[:, :, :]).then_inc(s_xt, 1)
                    act.wait_ge(s_wl, i + 1)
                    act.activation(lg[:, :, :], lg[:, :, :], ACT.Exp).then_inc(s_ex, 1)
                    act.wait_ge(s_wT, i + 1)
                    act.copy(wT[:, :, :].rearrange("p u n -> p (u n)"), pR[0:NX, 256:512]).then_inc(s_wc, 1)
                    for e in range(NX + 1):
                        if e < NX:
                            relu(i, e, pH1, h1, 0, s_h1, s_h2, s_a1)
                        if e:
                            relu(i, e - 1, pH2, h2, 1, s_h2, s_y, s_a2)

            @block.tensor
            def _(pe):
                pe.wait_ge(s_par, 160)
                for n in range(2):
                    if n:
                        pe.wait_ge(s_pr, n)
                    pe.transpose(pR[:, 0:80], pn[:, n, :], ident[0:80, 0:80]).then_inc(s_pt, 1)
                pe.wait_ge(s_ld, 27 * 16)
                pe.wait_ge(s_pr, 2)
                pe.sem_inc(s_h2, 2)
                pe.sem_inc(s_y, 2)
                pe.sem_inc(s_yr, 2)

                def layer(i, e, w, h_of, p, waits, done):
                    for s, v in waits:
                        gated(pe, "pe", s, v)
                    for m in range(2):
                        for c in range(2):
                            mm = pe.matmul(p[e % 2][:, m, :], w[:, e, c, m * P:m * P + P], h_of(c), start=c == 0, stop=c == 1)
                    mm.then_inc(done, 1)

                with pe.Fori(0, PAIRS) as i:
                    gated(pe, "pe", s_xs, i + 1)
                    for c in range(2):
                        for u in range(2):
                            mm = pe.transpose(pT[:, c, u * P:u * P + P], xs[:, u, c * P:c * P + P], ident[:, :])
                    mm.then_inc(s_t, 1)
                    gated(pe, "pe", s_xt, i + 1)
                    for u in range(2):
                        for c in range(2):
                            mm = pe.matmul(pR[:, u * NX:u * NX + NX], xT[:, c, u * P:u * P + P], wr[:, c, :],
                                           start=c == 0, stop=c == 1)
                    mm.then_inc(s_lg, 1)
                    for e in range(NX + 2):
                        if e < NX:
                            layer(i, e, w1, lambda c: xT[:, c, :], pH1, [(s_a1, i * NX + (e + 1))], s_h1)
                        if e == 1:
                            gated(pe, "pe", s_w, i + 1)
                            for u in range(2):
                                mm = pe.transpose(pR[0:NX, 256 + u * P:256 + u * P + P], wt[:, u, :], ident[:, :])
                            mm.then_inc(s_wT, 1)
                        if 1 <= e <= NX:
                            layer(i, e - 1, w2, lambda c: h1[:, (e - 1) % 2, c, :], pH2,
                                  [(s_a1, i * NX + (e + 2)), (s_a2, i * NX + e)], s_h2)
                        if e == 1:
                            gated(pe, "pe", s_wc, i + 1)
                            for u in range(2):
                                mm = pe.matmul(pT[:, u, :], wT[:, u, :], bo[:, :], start=True, stop=True)
                            mm.then_inc(s_b, 1)
                        if e >= 2:
                            f = e - 2
                            gated(pe, "pe", s_a2, i * NX + (f + 3))
                            gated(pe, "pe", s_yr, i * NX + (f + 1))
                            for u in range(2):
                                for c in range(2):
                                    mm = pe.matmul(pY[f % 2][:, u, :], h2[:, f % 2, c, u * P:u * P + P], wo[:, f, c, :],
                                                   start=c == 0, stop=c == 1)
                            mm.then_inc(s_y, 1)
                    gated(pe, "pe", s_br, i + 1)


_INS = ['x', 'src', 'dst', 'L0_gnn_W1', 'L0_gnn_al1', 'L0_gnn_ar1', 'L0_gnn_b1', 'L0_gnn_W2', 'L0_gnn_al2', 'L0_gnn_ar2', 'L0_gnn_b2', 'L0_mix_Wqkv', 'L0_mix_bqkv', 'L0_mix_Wproj', 'L0_mix_bproj', 'L0_mix_temperature', 'L0_ffn_Wr', 'L0_ffn_br', 'L0_ffn_W1', 'L0_ffn_b1', 'L0_ffn_g1', 'L0_ffn_be1', 'L0_ffn_m1', 'L0_ffn_v1', 'L0_ffn_W2', 'L0_ffn_b2', 'L0_ffn_g2', 'L0_ffn_be2', 'L0_ffn_m2', 'L0_ffn_v2', 'L0_ffn_Wo', 'L0_ffn_bo']


def kernel(**inputs):
    import numpy as _np
    import concourse.bacc as _bacc
    from concourse import mybir as _mybir
    from concourse.bass_utils import run_bass_kernel_spmd as _run

    nc = _bacc.Bacc("TRN2", target_bir_lowering=False, num_devices=1)
    arrays, args = {}, []
    for name in _INS:
        a = _np.ascontiguousarray(inputs[name])
        arrays[f"in_{name}_dram"] = a
        args.append(nc.dram_tensor(f"in_{name}_dram", a.shape, _mybir.dt.from_np(a.dtype), kind="ExternalInput").ap())
    args.append(nc.dram_tensor("out_dram", (N, C), F32, kind="ExternalOutput").ap())
    build(nc, *args)
    r = _run(nc, [arrays], core_ids=[0])
    return r.results[0]["out_dram"]
```

```python
from contextlib import ExitStack, contextmanager

import concourse.bass as bass
from concourse import mybir

ALU = mybir.AluOpType
ACT = mybir.ActivationFunctionType
F32 = mybir.dt.float32
BF16 = mybir.dt.bfloat16
I32 = mybir.dt.int32
AX_X = mybir.AxisListType.X

P = 128
N, C = 6250, 256
E = 200000
NT = 50
FULL = N // P
REST = N - FULL * P
PAIRS = NT // 2
HM, DM = 8, 32
MAIN = 16 * DM
QUADS = HM * MAIN // P
FEAT = HM * MAIN + 2 * HM * DM
CH = FEAT // P
V1 = DM + 1
COLS = 1664
JT = COLS // P
ET = (E + P - 1) // P
ETP = COLS
NBLK = (N + P - 1) // P
STEPS = ET + NBLK
ROUND = 32
ROUNDS = (STEPS + ROUND - 1) // ROUND
UA = 16
AIT = (ET + 2 * UA - 1) // (2 * UA)
NX = 8
EPS_LN, EPS_BN, EPS_NORM = 1e-5, 1e-3, 1e-12
SC = float(DM) ** 0.25
BIG = 1.0e30


class Count:

    def __init__(self, eng, sem):
        self.eng, self.sem, self.total, self.n, self.reg = eng, sem, 0, 0, 0

    def inc(self, ins):
        ins.then_inc(self.sem, 1)
        self.n += 1

    def wait(self):
        self.eng.wait_ge(self.sem, self.reg + (self.total + self.n))

    def link(self, ins):
        self.inc(ins)
        self.wait()

    def enter(self, i, per_round):
        self.total, self.n, self.per, self.reg = self.total + self.n, 0, per_round, i * per_round

    def leave(self, rounds):
        assert self.n == self.per, (self.n, self.per)
        self.total, self.n, self.reg = self.total + rounds * self.per, 0, 0


@contextmanager
def phase_semaphores(nc):
    held = []

    def sem(name):
        held.append(nc.alloc_semaphore(name))
        return held[-1]

    yield sem
    nc.clear_and_free_semaphores(held)
    nc.all_engine_barrier()


def bcast(ap, count):
    return bass.AP(ap.tensor, ap.offset, [list(d) for d in ap.ap] + [[0, count]])



def build(nc, x, src, dst, W1, al1, ar1, b1, W2, al2, ar2, b2, Wqkv, bqkv, Wproj, bproj, temp,
          Wr, br, fW1, fb1, fg1, fbe1, fm1, fv1, fW2, fb2, fg2, fbe2, fm2, fv2, fWo, fbo, out):
    ctx = ExitStack()
    with ctx:
        def sb(name, shape, dt=F32, at=None):
            return (at or ctx).enter_context(nc.sbuf_tensor(name, shape, dt))

        def pb(name, shape, at, dt=F32):
            return at.enter_context(nc.psum_tensor(name, shape, dt))

        def sem(name):
            return ctx.enter_context(nc.semaphore(name))

        def dram(name, shape, dt):
            return nc.dram_tensor(name, shape, dt, kind="Internal").ap()

        s_gate = {e: sem(f"gate_{e}") for e in ("pool", "act", "dve", "pe", "sp")}

        def gated(eng, name, s, value):
            eng.wait_ge(s, value)
            eng.sem_inc(s_gate[name], 1)

        ztab = dram("ztab", (NT * P, C), F32)

        qtab = dram("qtab", ((ROUNDS + 1) * P, C), F32)
        xtab = dram("xtab", (ROUNDS * P, C), F32)

        ident = sb("ident", [P, P])
        iota = sb("iota", [P, P])
        elr = sb("elr", [P, NT, 4])
        mix = {"KVS": sb("KVS", [P, QUADS, V1]),
               "KV4": sb("KV4", [P, 4, 4 * V1]), "VS": sb("VS", [P, HM * V1]),
               "wproj": sb("wproj", [P, 2, C]), "bsum": sb("bsum", [P, C])}

        head = ExitStack()
        with head:
            X = sb("X", [P, NT, C], at=head)
            st = sb("x_stats", [P, NT, 6], at=head)
            constants(nc, head, sb, pb, sem, ident, iota, X, x, st)
            project_and_mix(nc, sb, pb, sem, gated, ident, X, st, elr, ztab, qtab, xtab, mix,
                            W1, al1, ar1, b2, Wqkv, bqkv, Wproj, bproj, temp)
        acc = sb("acc", [P, NT, C + 2])
        attention_layers(nc, sb, pb, sem, dram, gated, ident, iota, acc, elr, ztab, qtab, xtab, mix, src, dst, b1, W2, al2, ar2)
        X = acc[:, :, 0:C]
        experts(nc, sb, pb, sem, gated, ident, X, out, Wr, br, fW1, fb1, fg1, fbe1, fm1, fv1,
                fW2, fb2, fg2, fbe2, fm2, fv2, fWo, fbo)


def constants(nc, ctx, sb, pb, sem, ident, iota, X, x, st):
    parts = 5
    K = NT // parts
    s_pad, s_id, s_st = sem("s_pad"), sem("s_id"), sem("s_statistics")
    s_x = [sem(f"s_x{n}") for n in range(parts)]
    tmp = ctx.enter_context(nc.sbuf_tensor("iota_i", [P, P], I32))
    with nc.Block() as block:
        @block.sync
        def _(sp):
            for n in range(parts):
                a, b = n * K, min(n * K + K, FULL)
                sp.dma_start(X[:, a:b, :], x[a * P:b * P, :].rearrange("(k p) c -> p k c", p=P)).then_inc(s_x[n], 16)
            sp.wait_ge(s_pad, 1)
            sp.dma_start(X[0:REST, FULL, :], x[FULL * P:N, :]).then_inc(s_x[parts - 1], 16)

        @block.gpsimd
        def _(pool):
            pool.memset(X[:, FULL:NT, :], 0.0).then_inc(s_pad, 1)
            pool.memset(ident[:, :], 0.0).then_inc(s_id, 1)
            pool.iota(tmp[:, :], pattern=[[1, P]], base=0, channel_multiplier=0).then_inc(s_id, 1)
            pool.wait_ge(s_id, 2)
            pool.affine_select(out=ident[:, :], in_=ident[:, :], compare_op=ALU.not_equal, fill=1.0,
                               base=0, pattern=[[-1, P]], channel_multiplier=1).then_inc(s_id, 1)
            pool.tensor_copy(iota[:, :], tmp[:, :]).then_inc(s_id, 1)
            pool.wait_ge(s_id, 4)

        @block.vector
        def _(dve):
            for n in range(parts):
                dve.wait_ge(s_x[n], 32 if n == parts - 1 else 16)
                tile_statistics(dve, X, st, n * K, n * K + K, s_st)
            dve.wait_ge(s_st, NT)


def tile_statistics(dve, X, st, first, last, count):
    with dve.Fori(first, last) as k:
        dve.bn_stats(st[:, bass.ds(k, 1), :].rearrange("p a c -> p (a c)"),
                     X[:, bass.ds(k, 1), :].rearrange("p a c -> p (a c)")).then_inc(count, 1)


def mean_and_variance(dve, ch, st, mean, var):
    ch.link(dve.tensor_tensor(var[:, :], st[:, :, 1], st[:, :, 4], ALU.subtract))
    ch.link(dve.tensor_tensor(var[:, :], var[:, :], var[:, :], ALU.mult))
    ch.link(dve.tensor_tensor(mean[:, :], st[:, :, 2], st[:, :, 5], ALU.add))
    ch.link(dve.tensor_scalar(var[:, :], var[:, :], 0.25, EPS_LN, ALU.mult, ALU.add))
    ch.link(dve.scalar_tensor_tensor(out=var[:, :], in0=mean[:, :], scalar=1.0 / C, in1=var[:, :], op0=ALU.mult, op1=ALU.add))
    ch.link(dve.tensor_tensor(mean[:, :], st[:, :, 1], st[:, :, 4], ALU.add))
    ch.link(dve.tensor_scalar(mean[:, :], mean[:, :], 0.5, None, ALU.mult))


def project_and_mix(nc, sb, pb, sem, gated, ident, X, st, elr, ztab, qtab, xtab, mix, W1, al1, ar1, b2, Wqkv, bqkv, Wproj, bproj, temp):
    ctx = ExitStack()
    with ctx:
        sem = ctx.enter_context(phase_semaphores(nc))
        t = lambda name, shape, dt=F32: sb(name, shape, dt, at=ctx)
        QN = t("QN", [P, NT, C])
        KVS, KV4, VS, wproj, bsum = [mix[n] for n in ("KVS", "KV4", "VS", "wproj", "bsum")]
        w8 = t("w8", [P, 2])
        head_of = t("head_of", [P, 4])
        c1 = ExitStack()
        with c1:
            t = lambda name, shape, dt=F32: sb(name, shape, dt, at=c1)
            wz = t("wz", [P, 2, C + 4])
            wqkv = t("wqkv", [P, 2, 3 * C])
            wnat = t("wnat", [P, 8, C])
            avec = t("avec", [P, 2, C])
            prod = t("prod", [P, C])
            bq = t("bq", [P, 3 * C])
            tmpb = t("tmpb", [P, 2, C])
            tempb = t("tempb", [P, HM])
            fac = t("fac", [P, 2, HM])
            sq2 = t("sq2", [P, 2, HM])
            mask = t("mask", [P, NT])
            mean, root_ = t("mean", [P, NT]), t("root", [P, NT])
            rs, shift = t("rs", [P, NT]), t("shift", [P, NT])
            xs = t("xs", [P, 2, C])
            xT = t("xT", [P, 2, 2, P])
            zs = t("zs", [P, 2, C])
            qkv = t("qkv", [P, 3 * C])
            sqk = t("sqk", [P, 2 * C])
            nrm = t("nrm", [P, 2, HM])
            rt = t("rt", [P, 2 * HM])
            kn = t("kn", [P, 2, HM, 2 * DM])
            v1 = t("v1", [P, 2, HM, V1])
            KF = t("KF", [P, 2, FEAT])
            ones = t("ones", [P, P])
            zero = t("zero", [P, 512])
            pKV = [pb(f"pKV{n}", [P, 512], c1) for n in range(4)]
            pE = pb("pE", [P, 512], c1)
            pE2 = pb("pE2", [P, 512], c1)
            pQ = pb("pQ", [P, 1024], c1)
            pZ = pQ[:, 2 * C:3 * C + 4]
            pT = pQ[:, 3 * C:4 * C].rearrange("p (a n) -> p a n", a=2)
            vpad = t("vpad", [P, 2, 4, 64 + V1])
            vacc = t("vacc", [P, HM * V1])
            kvT = t("kvT", [P, 4, 512])
            s_w, s_nw, s_cst = sem("p_w"), sem("p_natural"), sem("p_const")
            s_wt, s_wc = sem("p_wT"), sem("p_wT_copied")
            s_dve, s_xs, s_t, s_xt = sem("p_dve"), sem("p_xs"), sem("p_T"), sem("p_xT")
            s_kl, s_sq, s_kn, s_kn2, s_v, s_n2, s_rt, s_z, s_q, s_zc, s_elr, s_qv, s_kf, s_kv, s_init = [sem("p_" + n) for n in (
                "linear", "squares", "keys", "keys_doubled", "values", "norm2", "norm", "z", "qkv", "z_copied", "elr", "qkv_read", "features", "kv", "init")]
            s_vz, s_vp, s_va, s_kc, s_kt = [sem("p_" + n) for n in (
                "padding", "values_padded", "values_summed", "key_sums_copied", "key_sums_T")]
            s_zd = [sem(f"p_z_stored{u}") for u in range(2)]
            s_var, s_root, s_norm = sem("p_var"), sem("p_root"), sem("p_layer_norm")
            s_qn, s_qs, s_xs0 = sem("p_query"), sem("p_query_stored"), sem("p_x_stored")

            def extra(g):
                return pE[:, g * 4 * V1:(g + 1) * 4 * V1] if g < 3 else pE2[:, 0:4 * V1]

            with nc.Block() as block:
                @block.sync
                def _(sp):
                    sp.dma_start(wz[:, :, 0:C], W1.rearrange("(a p) n -> p a n", p=P)).then_inc(s_w, 16)
                    sp.dma_start(avec[:, 0, :], al1.rearrange("h d -> (h d)").partition_broadcast(P)).then_inc(s_w, 16)
                    sp.dma_start(avec[:, 1, :], ar1.rearrange("h d -> (h d)").partition_broadcast(P)).then_inc(s_w, 16)
                    sp.dma_start(bq[:, :], bqkv.partition_broadcast(P)).then_inc(s_w, 16)
                    sp.dma_start(tmpb[:, 0, :], bproj.partition_broadcast(P)).then_inc(s_w, 16)
                    sp.dma_start(tmpb[:, 1, :], b2.rearrange("h d -> (h d)").partition_broadcast(P)).then_inc(s_w, 16)
                    sp.dma_start(tempb[:, :], temp.rearrange("a h b c -> (a h b c)").partition_broadcast(P)).then_inc(s_w, 16)
                    sp.dma_start(wnat[:, 0:6, :], Wqkv.rearrange("(a p) c -> p a c", p=P)).then_inc(s_nw, 16)
                    sp.dma_start(wnat[:, 6:8, :], Wproj.rearrange("(a p) c -> p a c", p=P)).then_inc(s_nw, 16)
                    sp.wait_ge(s_w, 7 * 16)
                    sp.wait_ge(s_nw, 32)
                    sp.dma_start(xtab[0:NT * P, :].rearrange("(k p) c -> p k c", p=P), X[:, :, :]).then_inc(s_xs0, 16)
                    for k in range(NT, ROUNDS):
                        sp.dma_start(xtab[k * P:(k + 1) * P, :], X[:, NT - 1, :]).then_inc(s_xs0, 16)

                    with sp.Fori(0, PAIRS) as i:
                        for u in range(2):
                            sp.wait_ge(s_zc, i * 2 + (u + 1))
                            sp.dma_start(ztab[bass.ds(i * (2 * P) + u * P, P), :], zs[:, u, :]).then_inc(s_zd[u], 16)
                        for u in range(2):
                            sp.wait_ge(s_qn, i * 2 + (u + 1))
                            sp.dma_start(qtab[bass.ds(i * (2 * P) + u * P, P), :],
                                         QN[:, bass.ds(i * 2 + u, 1), :].rearrange("p a c -> p (a c)")).then_inc(s_qs, 16)
                    for k in range(NT, ROUNDS + 1):
                        sp.dma_start(qtab[k * P:(k + 1) * P, :], QN[:, NT - 1, :]).then_inc(s_qs, 16)
                    sp.wait_ge(s_qs, (ROUNDS + 1) * 16)
                    sp.wait_ge(s_xs0, (1 + ROUNDS - NT) * 16)
                    for u in range(2):
                        sp.wait_ge(s_zd[u], 16 + PAIRS * 16)

                @block.gpsimd
                def _(pool):
                    pool.memset(vpad[:, :, :, :], 0.0).then_inc(s_vz, 1)
                    pool.memset(vacc[:, :], 0.0).then_inc(s_va, 1)
                    pool.memset(ones[:, :], 1.0).then_inc(s_cst, 1)
                    pool.memset(zero[:, :], 0.0).then_inc(s_cst, 1)
                    pool.memset(mask[:, :], 1.0 / N).then_inc(s_cst, 1)
                    pool.memset(w8[:, 0:1], 1.0).then_inc(s_cst, 1)
                    pool.wait_ge(s_cst, 4)
                    pool.memset(w8[0:DM, 0:1], 0.5).then_inc(s_cst, 1)
                    pool.wait_ge(s_cst, 5)
                    pool.affine_select(out=mask[:, :], in_=mask[:, :], compare_op=ALU.is_gt, fill=0.0,
                                       base=N, pattern=[[-P, NT]], channel_multiplier=-1).then_inc(s_cst, 1)
                    pool.memset(head_of[:, :], 0.0).then_inc(s_cst, 1)
                    pool.wait_ge(s_cst, 7)
                    for h in range(4):
                        pool.memset(head_of[DM * h:DM * h + DM, h:h + 1], 1.0).then_inc(s_cst, 1)
                    pool.wait_ge(s_cst, 11)
                    pool.sem_inc(s_va, 2)
                    with pool.Fori(0, PAIRS) as i:
                        for u in range(2):
                            gated(pool, "pool", s_v, i * 2 + (u + 1))
                            pool.wait_ge(s_va, i * 2 + (u + 3))
                            pool.tensor_tensor(vacc[:, :], vacc[:, :], v1[:, u, :, :].rearrange("p h e -> p (h e)"),
                                               ALU.add).then_inc(s_va, 1)

                @block.vector
                def _(dve):
                    ch = Count(dve, s_dve)
                    mean_and_variance(dve, ch, st, mean, rs)
                    dve.sem_inc(s_var, 1)
                    dve.wait_ge(s_root, 1)
                    ch.link(dve.reciprocal(rs[:, :], root_[:, :]))
                    ch.link(dve.scalar_tensor_tensor(out=shift[:, :], in0=mean[:, :], scalar=-1.0, in1=rs[:, :],
                                                     op0=ALU.mult, op1=ALU.mult))
                    dve.sem_inc(s_norm, 1)
                    dve.wait_ge(s_w, 7 * 16)
                    for c in range(2):
                        for side in range(2):
                            ch.link(dve.tensor_tensor(prod[:, :], wz[:, c, 0:C], avec[:, side, :], ALU.mult))
                            ch.link(dve.tensor_reduce(wz[:, c, C + 2 * side:C + 2 * side + 2],
                                                      prod[:, :].rearrange("p (h d) -> p h d", h=2), AX_X, ALU.add))
                    ch.link(dve.tensor_tensor(bsum[:, :], tmpb[:, 0, :], tmpb[:, 1, :], ALU.add))
                    ch.link(dve.tensor_scalar(fac[:, 0, :], tempb[:, :], SC * SC, None, ALU.mult))
                    ch.link(dve.memset(fac[:, 1, :], SC))
                    ch.link(dve.memset(sq2[:, 0, :], SC * SC))
                    ch.link(dve.memset(sq2[:, 1, :], 1.0))
                    for n in range(8):
                        dve.wait_ge(s_wt, n + 1)
                        to = wqkv[:, :, n * P:n * P + P] if n < 6 else wproj[:, :, (n - 6) * P:(n - 5) * P]
                        dve.tensor_copy(to, pT[:, :, :]).then_inc(s_wc, 1)
                    dve.wait_ge(s_cst, 11)


                    def products(j, u):
                        dve.wait_ge(s_kn2, j + 1)
                        gated(dve, "dve", s_kv, j + 1)
                        features(dve, KF[:, u, :], kn[:, u, :, :]).then_inc(s_kf, 1)

                    def front(j, u):
                        dve.wait_ge(s_zc, j + 1)
                        dve.tensor_scalar(elr[:, bass.ds(j, 1), :].rearrange("p a c -> p (a c)"),
                                          pZ[:, C:C + 4], 1.0, None, ALU.mult).then_inc(s_elr, 1)
                        dve.wait_ge(s_q, j + 1)
                        dve.tensor_tensor(qkv[:, :], pQ[:, 0:3 * C], bq[:, :], ALU.add).then_inc(s_qv, 1)

                    def norms(j):
                        flat = nrm[:, :, :].rearrange("p a h -> p (a h)")
                        dve.wait_ge(s_sq, j + 1)
                        ch.link(dve.tensor_reduce(flat, sqk[:, :].rearrange("p (g d) -> p g d", d=DM), AX_X, ALU.add))
                        ch.link(dve.tensor_tensor(nrm[:, :, :], nrm[:, :, :], sq2[:, :, :], ALU.mult))
                        dve.tensor_scalar(flat, flat, EPS_NORM ** 2, None, ALU.max).then_inc(s_n2, 1)

                    def rest(j, u):
                        dve.tensor_tensor(KF[:, u, HM * MAIN:HM * MAIN + HM * DM].rearrange("p (h i) -> p h i", h=HM),
                                          kn[:, u, :, 0:DM], kn[:, u, :, 16:16 + DM], ALU.mult).then_inc(s_kf, 1)

                    def scaled(j, u):
                        flat = nrm[:, :, :].rearrange("p a h -> p (a h)")
                        dve.wait_ge(s_rt, j + 1)
                        ch.link(dve.reciprocal(flat, rt[:, :]))
                        ch.link(dve.tensor_tensor(nrm[:, :, :], nrm[:, :, :], fac[:, :, :], ALU.mult))
                        gated(dve, "dve", s_kf, j * 2 + 2)
                        gated(dve, "dve", s_kl, j + 1)
                        dve.tensor_tensor(kn[:, u, :, 0:DM], qkv[:, C:2 * C].rearrange("p (h d) -> p h d", h=HM),
                                          bcast(nrm[:, 1, :], DM), ALU.mult).then_inc(s_kn, 1)
                        dve.tensor_tensor(QN[:, bass.ds(j, 1), :].rearrange("p a (h d) -> p (a h) d", h=HM),
                                          qkv[:, 0:C].rearrange("p (h d) -> p h d", h=HM),
                                          bcast(nrm[:, 0, :], DM), ALU.mult).then_inc(s_qn, 1)
                        gated(dve, "dve", s_kv, j + 1)
                        gated(dve, "dve", s_va, j + 2)
                        ch.inc(dve.tensor_scalar(v1[:, u, :, 1:V1], qkv[:, 2 * C:3 * C].rearrange("p (h d) -> p h d", h=HM),
                                                 mask[:, bass.ds(j, 1)], None, ALU.mult))
                        ch.link(dve.tensor_scalar(v1[:, u, :, 0:1], bcast(ones[:, 0:HM], 1),
                                                  mask[:, bass.ds(j, 1)], None, ALU.mult))
                        dve.sem_inc(s_v, 1)

                    with dve.Fori(0, PAIRS) as i:
                        ch.enter(i, 2 * 6)
                        for u in range(2):
                            front(i * 2 + u, u)
                            norms(i * 2 + u)
                            scaled(i * 2 + u, u)
                            products(i * 2 + u, u)
                            rest(i * 2 + u, u)
                        ch.leave(PAIRS)
                    dve.wait_ge(s_kv, NT + 2)
                    for n in range(4):
                        dve.tensor_copy(kvT[0:64 + V1, n, :], pKV[n][0:64 + V1, :]).then_inc(s_kc, 1)
                    for n in range(4):
                        dve.wait_ge(s_kt, n + 1)
                        for c in range(4):
                            for h, at in ((n, 0), (n + 4, 64)):
                                w = w8[:, 0:1] if c == 0 else 1.0
                                ch.inc(dve.tensor_scalar(KVS[:, 4 * h + c, :], pKV[n][:, c * P + at:c * P + at + V1], w, None,
                                                         ALU.mult))
                    for g in range(4):
                        w = 0.5 if g < 2 else SC * SC
                        ch.inc(dve.scalar_tensor_tensor(out=KV4[:, g, :].rearrange("p (h e) -> p h e", h=4),
                                                        in0=extra(g).rearrange("p (h e) -> p h e", h=4),
                                                        scalar=w, in1=bcast(head_of[:, :], V1),
                                                        op0=ALU.mult, op1=ALU.mult))
                    dve.wait_ge(s_kt, 5)
                    ch.inc(dve.tensor_scalar(VS[:, :], pQ[:, 0:HM * V1], SC ** 4, None, ALU.mult))
                    gated(dve, "dve", s_dve, ch.total + ch.n)

                @block.tensor
                def _(pe):
                    pe.wait_ge(s_nw, 32)
                    for n in range(8):
                        if n:
                            pe.wait_ge(s_wc, n)
                        for c in range(2):
                            mm = pe.transpose(pT[:, c, :], wnat[:, n, c * P:c * P + P], ident[:, :])
                        mm.then_inc(s_wt, 1)
                    pe.wait_ge(s_wc, 8)
                    pe.wait_ge(s_cst, 5)
                    for bank in pKV + [pE, pE2]:
                        mm = pe.matmul(bank[:, :], zero[:, 0:P], zero[:, :], start=True, stop=False,
                                       skip_group_check=True)
                    mm.then_inc(s_init, 1)
                    pe.wait_ge(s_init, 1)
                    pe.sem_inc(s_kv, 2)
                    pe.sem_inc(s_t, 2)

                    def key_side(j, u, half):
                        if half == 0:
                            gated(pe, "pe", s_kf, j * 2 + 6)
                            gated(pe, "pe", s_kl, j + 3)
                            gated(pe, "pe", s_v, j + 1)
                            gated(pe, "pe", s_vp, j + 1)
                        for h in range(4 * half, 4 * half + 4):
                            rows, values = (V1, v1[:, u, h, :]) if h < 4 else (64 + V1, vpad[:, u, h - 4, :])
                            pe.matmul(pKV[h % 4][0:rows, :], values, KF[:, u, h * MAIN:(h + 1) * MAIN], start=False, stop=False,
                                      skip_group_check=True)
                        if half == 1:
                            for g in range(4):
                                c = QUADS + g
                                mm = pe.matmul(extra(g), KF[:, u, c * P:(c + 1) * P],
                                               v1[:, u, 4 * (c % 2):4 * (c % 2) + 4, :].rearrange("p h e -> p (h e)"),
                                               start=False, stop=False, skip_group_check=True)
                            mm.then_inc(s_kv, 1)

                    def turn(j, u):
                        pe.wait_ge(s_xs, j + 1)
                        for c in range(2):
                            mm = pe.transpose(pT[:, c, :], xs[:, u, c * P:c * P + P], ident[:, :])
                        mm.then_inc(s_t, 1)

                    def project(j, u):
                        gated(pe, "pe", s_xt, j + 1)
                        for c in range(2):
                            mm = pe.matmul(pZ, xT[:, u, c, :], wz[:, c, :], start=c == 0, stop=c == 1)
                        mm.then_inc(s_z, 1)
                        for a, b in ((0, 2 * C), (2 * C, 3 * C)):
                            if a == 0:
                                gated(pe, "pe", s_qv, j + 1)
                            else:
                                gated(pe, "pe", s_elr, j + 2)
                            for c in range(2):
                                mm = pe.matmul(pQ[:, a:b], xT[:, u, c, :], wqkv[:, c, a:b], start=c == 0, stop=c == 1)
                        mm.then_inc(s_q, 1)

                    def tile(j, u, back=True, ahead=True):
                        project(j, u)
                        if back:
                            key_side(j + (-1), 1 - u, 0)
                        if ahead:
                            gated(pe, "pe", s_qv, j + 2)
                            turn(j + 1, 1 - u)
                        if back:
                            key_side(j + (-1), 1 - u, 1)

                    pe.sem_inc(s_elr, 1)
                    pe.sem_inc(s_qv, 1)
                    pe.sem_inc(s_kf, 4)
                    pe.sem_inc(s_kl, 2)
                    turn(0, 0)
                    tile(0, 0, back=False)
                    tile(1, 1)
                    with pe.Fori(0, PAIRS - 2) as i:
                        for u in range(2):
                            tile(i * 2 + (2 + u), u)
                    tile(NT - 2, 0)
                    tile(NT - 1, 1, ahead=False)
                    for half in range(2):
                        key_side(NT - 1, 1, half)
                    for n in range(4):
                        pe.wait_ge(s_kc, n + 1)
                        for c in range(4):
                            mm = pe.transpose(pKV[n][:, c * P:c * P + 64 + V1], kvT[0:64 + V1, n, c * P:(c + 1) * P],
                                              ident[0:64 + V1, 0:64 + V1])
                        mm.then_inc(s_kt, 1)
                    pe.wait_ge(s_va, NT + 3)
                    pe.wait_ge(s_qv, NT + 1)
                    pe.matmul(pQ[:, 0:HM * V1], ones[:, :], vacc[:, :], start=True, stop=True).then_inc(s_kt, 1)

                @block.scalar
                def _(act):
                    act.wait_ge(s_var, 1)
                    act.activation(root_[:, :], rs[:, :], ACT.Sqrt).then_inc(s_root, 1)
                    act.wait_ge(s_norm, 1)
                    act.wait_ge(s_vz, 1)
                    for u in range(2):
                        act.sem_inc(s_zd[u], 16)

                    def normalised(j, u):
                        gated(act, "act", s_t, j + 1)
                        act.activation(xs[:, u, :], X[:, bass.ds(j, 1), :].rearrange("p a c -> p (a c)"), ACT.Identity,
                                       scale=rs[:, bass.ds(j, 1)], bias=shift[:, bass.ds(j, 1)]).then_inc(s_xs, 1)

                    def transposed(j, u):
                        act.wait_ge(s_t, j + 3)
                        act.copy(xT[:, u, :, :], pT[:, :, :]).then_inc(s_xt, 1)

                    def z_out(j, pair, u):
                        act.wait_ge(s_z, j + 1)
                        gated(act, "act", s_zd[u], pair * 16 + 16)
                        act.copy(zs[:, u, :], pZ[:, 0:C]).then_inc(s_zc, 1)

                    def squares(j):
                        act.wait_ge(s_qv, j + 2)
                        act.activation(sqk[:, :], qkv[:, 0:2 * C], ACT.Square).then_inc(s_sq, 1)

                    def root(j):
                        act.wait_ge(s_n2, j + 1)
                        act.activation(rt[:, :], nrm[:, :, :].rearrange("p a h -> p (a h)"), ACT.Sqrt).then_inc(s_rt, 1)

                    def copies(j, u):
                        act.wait_ge(s_kn, j + 1)
                        act.copy(kn[:, u, :, DM:2 * DM], kn[:, u, :, 0:DM]).then_inc(s_kn2, 1)
                        gated(act, "act", s_kv, j + 1)
                        act.copy(KF[:, u, HM * MAIN + HM * DM:FEAT].rearrange("p (h i) -> p h i", h=HM),
                                 kn[:, u, :, 0:DM]).then_inc(s_kl, 1)
                        gated(act, "act", s_v, j + 1)
                        act.copy(vpad[:, u, :, 64:64 + V1], v1[:, u, 4:8, :]).then_inc(s_vp, 1)

                    def tile(j, pair, u, ahead=2):
                        z_out(j, pair, u)
                        squares(j)
                        root(j)
                        copies(j, u)
                        if ahead >= 1:
                            transposed(j + 1, 1 - u)
                        if ahead >= 2:
                            normalised(j + 2, u)

                    normalised(0, 0)
                    transposed(0, 0)
                    normalised(1, 1)
                    with act.Fori(0, PAIRS - 1) as i:
                        for u in range(2):
                            tile(i * 2 + u, i, u)
                    tile(NT - 2, PAIRS - 1, 0, ahead=1)
                    tile(NT - 1, PAIRS - 1, 1, ahead=0)
        c1.close()


def features(eng, out, kn, heads=HM):
    part = list(kn.ap[0])
    same = bass.AP(kn.tensor, kn.offset, [part, [2 * DM, heads], [0, 16], [1, DM]])
    window = bass.AP(kn.tensor, kn.offset, [part, [2 * DM, heads], [1, 16], [1, DM]])
    main = out[:, 0:heads * MAIN].rearrange("p (h d i) -> p h d i", h=heads, d=16)
    return eng.tensor_tensor(main, same, window, ALU.mult)


def to_tiles(pe, mm_sem, rd_sem, base, pt, ident, src):
    for j in range(JT):
        if base + j:
            pe.wait_ge(rd_sem, base + j)
        pe.transpose(pt[:, :], src[:, j * P:j * P + P], ident[:, :]).then_inc(mm_sem, 1)


def prepare_edges(nc, sb, pb, sem, ident, src, dst, D, T):
    ctx = ExitStack()
    with ctx:
        sem = ctx.enter_context(phase_semaphores(nc))
        t = lambda name, shape, dt=F32: sb(name, shape, dt, at=ctx)
        si, di = t("e_src", [P, COLS], I32), t("e_dst", [P, COLS], I32)
        wi, wf, wb = t("e_int", [P, COLS], I32), t("e_f32", [P, COLS]), t("e_b16", [P, COLS], BF16)
        sf, df = t("e_srcf", [P, COLS]), t("e_dstf", [P, COLS])
        zero = t("e_zero", [P, COLS])
        last = t("e_last", [P, JT])
        lastB = t("e_lastB", [P, COLS])
        dx = t("e_dx", [P, COLS + 2])
        keyB = t("e_keyB", [P, COLS])
        ends = t("e_ends", [1, 2])
        tile_i, tile_f = t("e_ti", [P, JT], I32), t("e_tf", [P, JT])
        step_i, step_f = t("e_si", [P, JT], I32), t("e_sf", [P, JT])
        before = t("e_before", [P, NT])
        less, equal, pos = t("e_less", [P, NT]), t("e_equal", [P, NT]), t("e_pos", [P, NT])
        key, tf, bf, b128 = t("e_key", [P, JT]), t("e_t", [P, JT]), t("e_b", [P, JT]), t("e_b128", [P, JT])
        brow_f, brow_i = t("e_brf", [JT, P]), t("e_bri", [JT, P], I32)
        pt = pb("e_pt", [P, P], ctx)
        s_pad, s_ld, s_w, s_b, s_dve, s_io, s_k, s_kb, s_mm, s_rd, s_br = [sem("e_" + n) for n in (
            "pad", "loaded", "written", "windowed", "dve", "iota", "keys_ready", "keys", "T", "T_read", "brow")]
        rows = E // COLS
        left = E - rows * COLS
        with nc.Block() as block:
            @block.gpsimd
            def _(pool):
                pool.memset(si[:, :], 0).then_inc(s_pad, 1)
                pool.memset(di[:, :], N - 1).then_inc(s_pad, 1)
                pool.iota(tile_i[:, :], pattern=[[1, JT]], base=0, channel_multiplier=JT).then_inc(s_io, 1)
                pool.iota(step_i[:, :], pattern=[[P, JT]], base=0, channel_multiplier=1).then_inc(s_io, 1)
                pool.wait_ge(s_io, 2)

            @block.sync
            def _(sp):
                sp.wait_ge(s_pad, 2)
                for a, b in ((src, si), (dst, di)):
                    sp.dma_start(b[0:rows, :], a[0:rows * COLS].rearrange("(p c) -> p c", c=COLS)).then_inc(s_ld, 16)
                    sp.dma_start(b[rows:rows + 1, 0:left], a[rows * COLS:E].rearrange("(a c) -> a c", a=1)).then_inc(s_ld, 16)
                sp.wait_ge(s_k, 1)
                for a, b in ((D["src_lo"], wb), (D["src"], sf), (D["dst"], df)):
                    sp.dma_start(a.rearrange("(p c) -> p c", c=COLS), b[:, :]).then_inc(s_w, 16)
                sp.dma_start(D["window"][1:1 + P * COLS].rearrange("(p c) -> p c", c=COLS), df[:, :]).then_inc(s_w, 16)
                sp.dma_start(D["window"][0:1].rearrange("(a c) -> a c", a=1), ends[:, 0:1]).then_inc(s_w, 16)
                sp.dma_start(D["window"][1 + P * COLS:2 + P * COLS].rearrange("(a c) -> a c", a=1), ends[:, 1:2]).then_inc(s_w, 16)
                sp.dma_start(D["keys"].rearrange("(p c) -> p c", c=JT), key[:, :]).then_inc(s_w, 16)
                sp.dma_start(D["last"].rearrange("(p c) -> p c", c=JT), last[:, :]).then_inc(s_w, 16)
                sp.dma_start(D["er1"].rearrange("(p c) h -> p (c h)", c=COLS), zero[:, :]).then_inc(s_w, 16)
                for h in range(2):
                    half = D["er2"][h * P * COLS // 2:(h + 1) * P * COLS // 2, :]
                    sp.dma_start(half.rearrange("(p c) h -> p (c h)", c=COLS // 2), zero[:, :]).then_inc(s_w, 16)
                sp.wait_ge(s_w, 11 * 16)
                w = D["window"]
                sp.dma_start(dx[:, :], bass.AP(w.tensor, 0, [[COLS, P], [1, COLS + 2]])).then_inc(s_b, 16)
                sp.dma_start(keyB[:, :], D["keys"].partition_broadcast(P)).then_inc(s_kb, 16)
                sp.dma_start(lastB[:, :], D["last"].partition_broadcast(P)).then_inc(s_kb, 16)
                sp.wait_ge(s_br, 1)
                sp.dma_start(D["block_of"].rearrange("(p c) -> p c", c=P), brow_i[:, :]).then_inc(s_b, 16)
                sp.wait_ge(s_b, 32)
                sp.dma_start(T["block_of"][:, :], D["block_of"].rearrange("(a c) -> a c", a=1)).then_inc(s_b, 16)
                sp.wait_ge(s_b, 48)
                sp.wait_ge(s_kb, 32)

            @block.vector
            def _(dve):
                ch = Count(dve, s_dve)
                dve.wait_ge(s_ld, 64)
                dve.wait_ge(s_io, 2)
                ch.inc(dve.tensor_copy(sf[:, :], si[:, :]))
                ch.inc(dve.tensor_copy(df[:, :], di[:, :]))
                ch.inc(dve.tensor_copy(tile_f[:, :], tile_i[:, :]))
                ch.inc(dve.tensor_copy(step_f[:, :], step_i[:, :]))
                ch.inc(dve.memset(ends[:, 0:1], -1.0))
                ch.inc(dve.memset(ends[:, 1:2], 2.0e6))
                ch.link(dve.tensor_scalar(wi[:, :], si[:, :], P - 1, None, ALU.bitwise_and))
                ch.inc(dve.tensor_copy(wb[:, :], wi[:, :]))
                ch.link(dve.tensor_scalar(si[:, :], si[:, :], 7, None, ALU.arith_shift_right))
                ch.link(dve.tensor_copy(wf[:, :], si[:, :]))
                ch.inc(dve.memset(zero[:, :], 0.0))
                ch.inc(dve.tensor_copy(last[:, :], di[:, P - 1:COLS:P]))
                ch.link(dve.tensor_copy(T["first_dst"][:, :], di[:, 0:1]))
                ch.link(dve.tensor_scalar(di[:, :], di[:, :], 7, None, ALU.arith_shift_right))
                ch.link(dve.tensor_copy(key[:, :], di[:, P - 1:COLS:P]))
                ch.link(dve.tensor_tensor(key[:, :], key[:, :], tile_f[:, :], ALU.add))
                ch.link(dve.tensor_copy(wi[:, :], T["edge_no"][:, :]))
                ch.link(dve.tensor_copy(keyB[:, :], wi[:, :]))
                ch.link(dve.tensor_scalar(keyB[:, :], keyB[:, :], E - 0.5, 1.0e6, ALU.is_gt, ALU.mult))
                ch.link(dve.tensor_tensor(df[:, :], df[:, :], keyB[:, :], ALU.add))
                dve.sem_inc(s_k, 1)
                for j in range(JT):
                    dve.wait_ge(s_mm, j + 1)
                    dve.tensor_copy(T["src_hi"][:, j:COLS:JT], pt[:, :]).then_inc(s_rd, 1)
                dve.wait_ge(s_b, 16)
                ch.link(dve.tensor_tensor(T["same"][:, :], dx[:, 0:COLS], dx[:, 1:1 + COLS], ALU.is_equal))
                for a, b, c in ((T["starts"], 0, 1), (T["ends"], 2, 1)):
                    ch.link(dve.tensor_tensor(a[:, :], dx[:, b:b + COLS], dx[:, c:c + COLS], ALU.not_equal))
                    ch.link(dve.tensor_scalar(a[:, :], a[:, :], -BIG, None, ALU.mult))
                for a, n in ((T["starts"], 0), (T["ends"], 1)):
                    ch.link(dve.tensor_reduce(T["chain"][:, n:n + 1], a[:, :], AX_X, ALU.add))
                dve.wait_ge(s_kb, 32)
                for j in range(JT):
                    ch.link(dve.tensor_scalar(wf[:, :], keyB[:, :], step_f[:, j:j + 1], 0.0, ALU.is_lt, ALU.add,
                                              accum_out=tf[:, j:j + 1]))
                ch.link(dve.tensor_copy(T["tile_of"][:, :], tf[:, :]))
                ch.link(dve.tensor_tensor(bf[:, :], step_f[:, :], tf[:, :], ALU.subtract))
                ch.link(dve.tensor_scalar(T["first_node"][:, :], bf[:, :], float(P), None, ALU.mult))
                ch.link(dve.tensor_scalar(bf[:, :], bf[:, :], 0.0, float(NT - 1), ALU.max, ALU.min))
                dve.sem_inc(s_k, 1)
                for k in range(NT):
                    ch.link(dve.tensor_scalar(wf[:, :], lastB[:, :], T["node"][:, k:k + 1], 0.0, ALU.is_lt, ALU.add,
                                              accum_out=before[:, k:k + 1]))
                ch.link(dve.tensor_scalar(before[:, :], before[:, :], float(ETP - 1), None, ALU.min))
                ch.link(dve.tensor_copy(T["row_tile"][:, :], before[:, :]))
                dve.wait_ge(s_mm, JT + 1)
                ch.link(dve.tensor_copy(brow_i[:, :], pt[0:JT, :]))
                dve.sem_inc(s_br, 1)

            @block.tensor
            def _(pe):
                pe.wait_ge(s_k, 1)
                to_tiles(pe, s_mm, s_rd, 0, pt, ident, wf)
                pe.wait_ge(s_k, 2)
                pe.wait_ge(s_rd, JT)
                pe.transpose(pt[0:JT, :], bf[:, :], ident[:, :]).then_inc(s_mm, 1)

        g = ExitStack()
        with g:
            G = [sb(f"e_g{n}", [P, 2, P], F32, at=g) for n in range(2)]
            pp = pb("e_pp", [P, 2, P], g)
            s_g = [sem(f"e_rows{n}") for n in range(2)]
            s_l, s_m, s_r = sem("e_local"), sem("e_rowT"), sem("e_rowT_read")
            s_dve = sem("e_dve2")
            with nc.Block() as block:
                @block.gpsimd
                def _(pool):
                    for j in range(JT):
                        if j >= 2:
                            pool.wait_ge(s_m, j - 1)
                        off = bass.IndirectOffsetOnAxis(ap=T["tile_of"][:, j:j + 1], axis=0)
                        for a, name in enumerate(("src", "dst")):
                            pool.indirect_dma_start(G[j % 2][:, a, :], None, D[name].rearrange("(t e) -> t e", e=P),
                                                    off).then_inc(s_g[j % 2], 16)

                @block.vector
                def _(dve):
                    for j in range(JT):
                        dve.wait_ge(s_g[j % 2], 32 * (j // 2 + 1))
                        dve.tensor_scalar(G[j % 2][:, 1, :], G[j % 2][:, 1, :], T["first_node"][:, j:j + 1], None,
                                          ALU.subtract).then_inc(s_l, 1)
                        dve.wait_ge(s_m, j + 1)
                        dve.tensor_copy(T["src_of"][:, j * P:j * P + P], pp[:, 0, :]).then_inc(s_r, 1)
                        dve.tensor_copy(T["dst_of"][:, j * P:j * P + P], pp[:, 1, :]).then_inc(s_r, 1)

                @block.tensor
                def _(pe):
                    for j in range(JT):
                        pe.wait_ge(s_l, j + 1)
                        if j:
                            pe.wait_ge(s_r, 2 * j)
                        for a in range(2):
                            mm = pe.transpose(pp[:, a, :], G[j % 2][:, a, :], ident[:, :])
                        mm.then_inc(s_m, 1)

        g = ExitStack()
        with g:
            NS = 5
            G = [sb(f"r_g{n}", [P, P], F32, at=g) for n in range(NS)]
            J = sb("r_j", [P, 2, P], F32, at=g)
            s_g = [sem(f"r_rows{n}") for n in range(NS)]
            s_u, s_dve = sem("r_used"), sem("r_dve")
            with nc.Block() as block:
                @block.gpsimd
                def _(pool):
                    for k in range(NT):
                        if k >= NS:
                            pool.wait_ge(s_u, k - NS + 1)
                        pool.indirect_dma_start(G[k % NS][:, :], None, D["dst"].rearrange("(t e) -> t e", e=P),
                                                bass.IndirectOffsetOnAxis(ap=T["row_tile"][:, k:k + 1], axis=0)
                                                ).then_inc(s_g[k % NS], 16)

                @block.vector
                def _(dve):
                    ch = Count(dve, s_dve)
                    for k in range(NT):
                        dve.wait_ge(s_g[k % NS], 16 * (k // NS + 1))
                        for a, (op, to) in enumerate(((ALU.is_lt, less), (ALU.is_equal, equal))):
                            ch.link(dve.tensor_scalar(J[:, a, :], G[k % NS][:, :], T["node"][:, k:k + 1], 0.0, op, ALU.add,
                                                      accum_out=to[:, k:k + 1]))
                        dve.sem_inc(s_u, 1)
                    ch.link(dve.tensor_scalar(equal[:, :], equal[:, :], 0.5, 1.0e6, ALU.is_lt, ALU.mult))
                    ch.link(dve.scalar_tensor_tensor(out=pos[:, :], in0=before[:, :], scalar=float(P), in1=less[:, :],
                                                     op0=ALU.mult, op1=ALU.add))
                    ch.link(dve.tensor_tensor(pos[:, :], pos[:, :], equal[:, :], ALU.add))
                    ch.link(dve.tensor_copy(T["first_edge"][:, :], pos[:, :]))


def edge_softmax(nc, sb, pb, sem, gated, ident, iota, elr, er_col, D, T, H, L):
    ctx = ExitStack()
    with ctx:
        sem = ctx.enter_context(phase_semaphores(nc))
        t = lambda name, shape, dt=F32: sb(f"{name}{L}", shape, dt, at=ctx)
        S = lambda *names: [sem(f"{n}{L}") for n in names]
        val = t("l_val", [P, ETP, H])
        init = t("l_init", [P, 4])
        erc = t("l_erc", [P, COLS * H])
        er_dram = D["er%d" % H]
        c1 = ExitStack()
        with c1:
            t1 = lambda name, shape, dt=F32: sb(f"{name}{L}", shape, dt, at=c1)
            K = NT
            parts = t1("l_parts", [P, 3, H * K], BF16)
            whole, back = t1("l_whole", [P, H, K]), t1("l_back", [P, H * K])
            bcs = t1("l_lo", [P, 2, UA * P], BF16)
            pick = t1("l_pick", [P, 2, UA * P], BF16)
            own = t1("l_own", [P, 1])
            mask = t1("l_mask", [P, 2, UA, K])
            one = t1("l_one", [P, 1])
            picked = t1("l_picked", [P, 2, UA, H, K])
            banks = [pb(f"l_b{n}{L}", [P, UA, P], c1) for n in range(2)]
            s_dve, s_lo0, s_lo1, s_pk, s_mm, s_rd, s_er, s_init, s_tab, s_erl, s_mask, s_diff, s_sq, s_one = S(
                "l_dve", "l_lo0", "l_lo1", "l_pick", "l_mm", "l_read", "l_er", "l_init", "l_table", "l_er_loaded", "l_masks", "l_differences",
                "l_squares", "l_one")
            s_lo = [s_lo0, s_lo1]
            with nc.Block() as block:
                @block.gpsimd
                def _(pool):
                    tiles = list(iota[:, 0:K].ap)
                    numbers = bass.AP(iota[:, :].tensor, iota[:, :].offset, [list(tiles[0]), [0, UA], [1, K]])
                    for part in range(5):
                        for k in range(NT // 5 * part, NT // 5 * (part + 1)):
                            pool.indirect_dma_start(er_dram, bass.IndirectOffsetOnAxis(ap=T["first_edge"][:, k:k + 1], axis=0),
                                                    elr[:, k, er_col:er_col + H], None, bounds_check=P * COLS - 1,
                                                    oob_is_err=False).then_inc(s_er, 16)
                        with pool.Fori(10 * part, min(10 * part + 10, AIT)) as i:
                            for u in range(2):
                                gated(pool, "pool", s_rd, i * 2 + (u + 1))
                                at = T["src_hi"][:, bass.ds(i * (2 * UA) + u * UA, UA)]
                                pool.tensor_tensor(mask[:, u, :, :], numbers, bcast(at, K), ALU.subtract).then_inc(s_diff, 1)
                    pool.wait_ge(s_tab, 16)
                    pool.indirect_dma_start(init[:, :], None, D["terms"], bass.IndirectOffsetOnAxis(
                        ap=T["first_dst"][:, 0:1], axis=0)).then_inc(s_init, 16)
                    pool.wait_ge(s_er, NT * 16)
                    pool.wait_ge(s_init, 16)

                @block.scalar
                def _(act):
                    act.dma_start(D["terms"].rearrange("(k p) c -> p k c", p=P), elr[:, :, :]).then_inc(s_tab, 16)
                    act.wait_ge(s_one, 1)
                    with act.Fori(0, AIT) as i:
                        for u in range(2):
                            gated(act, "act", s_diff, i * 2 + (u + 1))
                            act.activation(mask[:, u, :, :], mask[:, u, :, :], ACT.Square).then_inc(s_sq, 1)
                            act.wait_ge(s_sq, i * 2 + (u + 1))
                            act.activation(mask[:, u, :, :], mask[:, u, :, :], ACT.Relu, bias=one[:, :], scale=-1.0).then_inc(s_mask, 1)
                    act.wait_ge(s_tab, 16)

                @block.sync
                def _(sp):
                    def load(i, u):
                        row = D["src_lo"][bass.ds(i * (2 * UA * P) + u * UA * P, UA * P)]
                        sp.dma_start(bcs[:, u, :], row.partition_broadcast(P)).then_inc(s_lo[u], 16)

                    with sp.Fori(0, AIT) as i:
                        for u in range(2):
                            gated(sp, "sp", s_pk, i * 2 + (u + 1))
                            load(i, u)
                    sp.wait_ge(s_pk, AIT * 2 + 1)
                    load(AIT, 0)
                    sp.wait_ge(s_pk, AIT * 2 + 2)
                    load(AIT, 1)
                    sp.wait_ge(s_er, NT * 16)
                    sp.dma_start(erc[:, :], er_dram.rearrange("(p c) h -> p (c h)", c=COLS)).then_inc(s_erl, 16)
                    sp.wait_ge(s_erl, 16)

                @block.tensor
                def _(pe):
                    with pe.Fori(0, AIT) as i:
                        for u in range(2):
                            pe.wait_ge(s_pk, i * 2 + (2 + u + 1))
                            gated(pe, "pe", s_rd, i * 2 + (u + 1))
                            for q in range(UA):
                                for part in range(3):
                                    mm = pe.matmul(banks[u][:, q, 0:H * K], pick[:, u, q * P:(q + 1) * P],
                                                   parts[:, part, :], start=part == 0, stop=part == 2)
                            mm.then_inc(s_mm, 1)

                @block.vector
                def _(dve):
                    ch = Count(dve, s_dve)
                    dve.memset(one[:, :], 1.0).then_inc(s_one, 1)
                    for h in range(H):
                        ch.inc(dve.tensor_copy(whole[:, h, :], elr[:, :, h]))
                    ch.link(dve.tensor_copy(own[:, :], T["node"][:, 0:1]))
                    flat = whole[:, :, :].rearrange("p h k -> p (h k)")
                    for part in range(3):
                        ch.link(dve.tensor_copy(parts[:, part, :], flat))
                        if part < 2:
                            ch.link(dve.tensor_copy(back[:, :], parts[:, part, :]))
                            ch.link(dve.tensor_tensor(flat, flat, back[:, :], ALU.subtract))
                    dve.sem_inc(s_rd, 2)
                    dve.sem_inc(s_pk, 2)

                    def one_hot(u, need):
                        dve.wait_ge(s_lo[u], need)
                        dve.tensor_scalar(pick[:, u, :], bcs[:, u, :], own[:, 0:1], None, ALU.is_equal).then_inc(s_pk, 1)

                    one_hot(0, 16)
                    one_hot(1, 16)
                    with dve.Fori(0, AIT) as i:
                        ch.enter(i, 4)
                        for u in range(2):
                            m = mask[:, u, :, :]
                            gated(dve, "dve", s_mask, i * 2 + (u + 1))
                            dve.wait_ge(s_mm, i * 2 + (u + 1))
                            ch.inc(dve.tensor_tensor(
                                picked[:, u, :, :, :], banks[u][:, :, 0:H * K].rearrange("p t (h k) -> p t h k", h=H),
                                bass.AP(m.tensor, m.offset, [list(m.ap[0]), [K, UA], [0, H], [1, K]]), ALU.mult))
                            ch.wait()
                            dve.sem_inc(s_rd, 1)
                            one_hot(u, i * 16 + 32)
                            ch.inc(dve.tensor_reduce(val[:, bass.ds(i * (2 * UA) + u * UA, UA), :],
                                                     picked[:, u, :, :, :], AX_X, ALU.add))
                        ch.leave(AIT)
                    ch.wait()

        c2 = ExitStack()
        with c2:
            t2 = lambda name, shape, dt=F32: sb(f"{name}{L}", shape, dt, at=c2)
            vP = [[t2(f"l_P{s}{h}", [P, COLS]) for h in range(H)] for s in range(2)]
            F, M, W = t2("m_F", [P, COLS]), t2("m_M", [P, COLS]), t2("m_W", [P, COLS])
            rows_ = t2("m_rows", [1, 4, P + 2])
            carry = t2("m_carry", [P, 2])
            pt = [pb(f"m_pt{n}{L}", [P, P], c2) for n in range(2)]
            pr = pb(f"m_pr{L}", [1, 2, P], c2)
            pc = pb(f"m_pc{L}", [P, 2], c2)
            s_dve, s_mm, s_rd, s_row, s_mr, s_ex, s_exd = S("m_dve", "m_T", "m_T_read", "m_row", "m_mr", "m_e", "m_stored")
            with nc.Block() as block:
                @block.tensor
                def _(pe):
                    for n in range(H * JT):
                        if n >= 2:
                            pe.wait_ge(s_rd, n - 1)
                        pe.transpose(pt[n % 2][:, :], val[:, n % JT:COLS:JT, n // JT], ident[:, :]).then_inc(s_mm, 1)
                    for h in range(H):
                        for d in range(2):
                            r = 2 * (2 * h + d)
                            pe.wait_ge(s_row, r + 1)
                            pe.transpose(pr[:, 0, :], carry[:, 0:1], ident[:, :])
                            pe.transpose(pr[:, 1, :], T["chain"][:, d:d + 1], ident[:, :]).then_inc(s_mr, 1)
                            pe.wait_ge(s_row, r + 2)
                            pe.transpose(pc[:, 0:1], rows_[:, 3, d:d + P], ident[0:1, 0:1]).then_inc(s_mr, 1)

                @block.vector
                def _(dve):
                    ch = Count(dve, s_dve)
                    for h in range(H):
                        ch.link(dve.tensor_tensor_scan(vP[1][h][:, :], T["same"][:, :], erc[:, h:COLS * H:H],
                                                       init[:, er_col + h:er_col + h + 1], ALU.mult, ALU.add))
                    for n in range(H * JT):
                        j = n % JT
                        dve.wait_ge(s_mm, n + 1)
                        dve.tensor_copy(vP[0][n // JT][:, j * P:j * P + P], pt[n % 2][:, :]).then_inc(s_rd, 1)
                    dve.wait_ge(s_rd, H * JT)

                    def turn(ap, d, n):
                        return ap if d == 0 else bass.AP(ap.tensor, ap.offset + n - 1, [list(ap.ap[0]), [-1, n]])

                    for h in range(H):
                        for d, mark, v, o in ((0, T["starts"], vP[0][h], F), (1, T["ends"], F, M)):
                            r = 2 * (2 * h + d)
                            scan = lambda init: dve.tensor_tensor_scan(
                                turn(o[:, :], d, COLS), turn(mark[:, :], d, COLS), turn(v[:, :], d, COLS), init, ALU.add, ALU.max)
                            ch.link(scan(-BIG))
                            last = COLS - 1 if d == 0 else 0
                            ch.link(dve.tensor_copy(carry[:, 0:1], o[:, last:last + 1]))
                            dve.sem_inc(s_row, 1)
                            dve.wait_ge(s_mr, r + 1)
                            ch.inc(dve.tensor_copy(rows_[:, 0, 0:P], pr[:, 0, :]))
                            ch.inc(dve.tensor_copy(rows_[:, 1, 0:P], pr[:, 1, :]))
                            ch.link(dve.memset(rows_[:, 3, :], -BIG))
                            ch.link(dve.tensor_tensor_scan(turn(rows_[:, 3, 1:P + 1], d, P), turn(rows_[:, 1, 0:P], d, P),
                                                           turn(rows_[:, 0, 0:P], d, P), -BIG, ALU.add, ALU.max))
                            if d:
                                ch.link(dve.tensor_copy(rows_[:, 2, 0:P], rows_[:, 3, 1:P + 1]))
                                ch.link(dve.memset(rows_[:, 3, :], -BIG))
                                ch.link(dve.tensor_copy(rows_[:, 3, 1:P], rows_[:, 2, 1:P]))
                            dve.sem_inc(s_row, 1)
                            dve.wait_ge(s_mr, r + 2)
                            ch.link(dve.tensor_copy(carry[:, 1:2], pc[:, 0:1]))
                            ch.link(scan(carry[:, 1:2]))
                        el, er = vP[0][h], vP[1][h]
                        ch.link(dve.tensor_tensor(W[:, :], el[:, :], er[:, :], ALU.add))
                        ch.inc(dve.scalar_tensor_tensor(out=W[:, :], in0=W[:, :], scalar=0.2, in1=W[:, :], op0=ALU.mult, op1=ALU.max))
                        ch.link(dve.tensor_tensor(M[:, :], M[:, :], er[:, :], ALU.add))
                        ch.link(dve.scalar_tensor_tensor(out=M[:, :], in0=M[:, :], scalar=0.2, in1=M[:, :], op0=ALU.mult, op1=ALU.max))
                        ch.link(dve.tensor_tensor(el[:, :], W[:, :], M[:, :], ALU.subtract))
                        dve.sem_inc(s_ex, 1)

                @block.scalar
                def _(act):
                    for h in range(H):
                        act.wait_ge(s_ex, h + 1)
                        act.activation(vP[0][h][:, :], vP[0][h][:, :], ACT.Exp).then_inc(s_exd, 1)
                        act.wait_ge(s_exd, h * 17 + 1)
                        act.dma_start(D["ex"][h].rearrange("(p c) -> p c", c=COLS), vP[0][h][:, :]).then_inc(s_exd, 16)
                        act.wait_ge(s_exd, h * 17 + 17)

        c3 = ExitStack()
        with c3:
            G = [sb(f"x_g{n}{L}", [P, H, P], F32, at=c3) for n in range(2)]
            pp = pb(f"x_p{L}", [P, H, P], c3)
            s_g = S("x_rows0", "x_rows1")
            s_m, s_r = S("x_T", "x_T_read")
            with nc.Block() as block:
                @block.gpsimd
                def _(pool):
                    for j in range(JT):
                        if j >= 2:
                            pool.wait_ge(s_m, j - 1)
                        off = bass.IndirectOffsetOnAxis(ap=T["tile_of"][:, j:j + 1], axis=0)
                        for h in range(H):
                            pool.indirect_dma_start(G[j % 2][:, h, :], None, D["ex"][h].rearrange("(t e) -> t e", e=P),
                                                    off).then_inc(s_g[j % 2], 16)

                @block.tensor
                def _(pe):
                    for j in range(JT):
                        pe.wait_ge(s_g[j % 2], 16 * H * (j // 2 + 1))
                        if j:
                            pe.wait_ge(s_r, j)
                        for h in range(H):
                            mm = pe.transpose(pp[:, h, :], G[j % 2][:, h, :], ident[:, :])
                        mm.then_inc(s_m, 1)

                @block.vector
                def _(dve):
                    for j in range(JT):
                        dve.wait_ge(s_m, j + 1)
                        dve.tensor_copy(T["ex"][:, j * P:j * P + P, 0:H].rearrange("p e h -> p h e"),
                                        pp[:, :, :]).then_inc(s_r, 1)


RING = 16
HALF = RING // 2


def block_at(nc, T, step):
    return nc.values_load(T["block_of"][0:1, bass.ds(step, 1)], engines=(mybir.EngineType.DVE,), min_val=0, max_val=NT - 1,
                          skip_runtime_bounds_check_because="prepare_edges clamps it to 0..NT - 1")


def match_half(dve, s_mm, s_oh, OH, GS, iota, T, H, at, half):
    at, slots = at + HALF * half, slice(HALF * (half % 2), HALF * (half % 2) + HALF)
    dve.wait_ge(s_mm, at + HALF)
    numbers = bass.AP(iota.tensor, iota.offset, [list(iota.ap[0]), [0, HALF], [1, P]])
    dve.tensor_tensor(OH[:, slots, :], numbers, bcast(T["dst_of"][:, bass.ds(at, HALF)], P), ALU.is_equal).then_inc(s_oh, 1)
    dve.tensor_scalar(GS[:, slots, C:C + H], T["ex"][:, bass.ds(at, HALF), 0:H], 1.0, None, ALU.mult).then_inc(s_oh, 1)


def gather_and_sum(nc, sb, pb, sem, gated, iota, ztab, acc, T, H, L):
    ctx = ExitStack()
    with ctx:
        sem = ctx.enter_context(phase_semaphores(nc))
        G = [sb(f"g_row{n}{L}", [P, C], F32, at=ctx) for n in range(RING)]
        GS = sb(f"g_scaled{L}", [P, RING, C + H], F32, at=ctx)
        OH = sb(f"g_onehot{L}", [P, RING, P], F32, at=ctx)
        idx = sb(f"g_idx{L}", [P, 2, HALF], I32, at=ctx)
        ps = [pb(f"g_ps{n}{L}", [P, C + H], ctx) for n in range(HALF)]
        S = lambda *names: [sem(f"{n}{L}") for n in names]
        s_row = [sem(f"g_landed{n}{L}") for n in range(RING)]
        s_idx, s_gs, s_oh, s_mm, s_add, s_z = S("g_idx", "g_scaled", "g_onehot", "g_mm", "g_added", "g_zero")
        TURNS = (STEPS + RING - 1) // RING
        w = C // H
        with nc.Block() as block:
            @block.gpsimd
            def _(pool):
                with pool.Fori(0, TURNS) as i:
                    for half in range(2):
                        gated(pool, "pool", s_gs, i * RING + HALF * (half + 1))
                        pool.tensor_copy(idx[:, half, :], T["src_of"][:, bass.ds(i * RING + HALF * half, HALF)]).then_inc(s_idx, 1)
                        gated(pool, "pool", s_idx, i * 2 + (half + 1))
                        for q in range(HALF):
                            n = HALF * half + q
                            pool.indirect_dma_start(G[n][:, :], None, ztab, bass.IndirectOffsetOnAxis(
                                ap=idx[:, half, q:q + 1], axis=0)).then_inc(s_row[n], 16)

            @block.scalar
            def _(act):
                act.sem_inc(s_gs, RING)
                with act.Fori(0, TURNS) as i:
                    for n in range(RING):
                        if n % HALF == 0:
                            gated(act, "act", s_mm, i * RING + (n + HALF))
                        gated(act, "act", s_row[n], i * 16 + 16)
                        for h in range(H):
                            ins = act.activation(GS[:, n, h * w:h * w + w], G[n][:, h * w:h * w + w], ACT.Copy,
                                                 scale=T["ex"][:, bass.ds(i * RING + n, 1), h])
                        ins.then_inc(s_gs, 1)

            @block.tensor
            def _(pe):
                pe.sem_inc(s_mm, RING)
                with pe.Fori(0, TURNS) as i:
                    for n in range(RING):
                        if n % HALF == 0:
                            gated(pe, "pe", s_oh, i * 4 + (2 * (n // HALF) + 2))
                        gated(pe, "pe", s_add, i * RING + (n + 1))
                        pe.wait_ge(s_gs, i * RING + (RING + n + 1))
                        pe.matmul(ps[n % HALF][:, :], OH[:, n, :], GS[:, n, :], start=True, stop=True).then_inc(s_mm, 1)

            @block.vector
            def _(dve):
                dve.memset(acc[:, :, :], 0.0).then_inc(s_z, 1)
                dve.sem_inc(s_add, HALF)

                match = lambda at, half: match_half(dve, s_mm, s_oh, OH, GS, iota[:, :], T, H, at, half)
                match(0, 0)
                dve.wait_ge(s_z, 1)
                with dve.Fori(0, TURNS) as i:
                    for n in range(RING):
                        if n % HALF == 0:
                            match(i * RING, n // HALF + 1)
                        if n % 4 == 0:
                            gated(dve, "dve", s_mm, i * RING + (RING + n + 4))
                        b = block_at(nc, T, i * RING + n)
                        to = acc[:, bass.ds(b, 1), :].rearrange("p a c -> p (a c)")
                        dve.wait_ge(s_add, i * RING + (HALF + n))
                        dve.tensor_tensor(to, to, ps[n % HALF][:, :], ALU.add).then_inc(s_add, 1)


def gather_and_mix(nc, sb, pb, sem, gated, ident, iota, ztab, qtab, xtab, mix, acc, T):
    ctx = ExitStack()
    with ctx:
        sem = ctx.enter_context(phase_semaphores(nc))
        t = lambda name, shape, dt=F32: sb("w_" + name, shape, dt, at=ctx)
        H = 1
        NB = 4
        G = [t(f"row{n}", [P, C]) for n in range(RING)]
        GS = t("scaled", [P, RING, C + H])
        OH = t("onehot", [P, RING, P])
        idx = t("idx", [P, 2, HALF], I32)
        ps = [pb(f"w_ps{n}", [P, C + H], ctx) for n in range(NB)]
        s_row = [sem(f"w_landed{n}") for n in range(RING)]
        s_idx, s_gs, s_oh, s_mm, s_add, s_z = [sem("w_" + n) for n in ("idx", "scaled", "onehot", "mm", "added", "zero")]
        KVS, KV4, VS, wproj, bsum = [mix[n] for n in ("KVS", "KV4", "VS", "wproj", "bsum")]
        q, xt, res = t("q", [P, C]), t("x", [P, C]), t("res", [P, C])
        q2 = t("q2", [P, HM, 2 * DM])
        QF = t("QF", [P, FEAT])
        QT = t("QT", [P, 3, 4, P])
        rec = t("rec", [P, HM])
        yo, ot = t("yo", [P, C]), t("ot", [P, C])
        yT = t("yT", [P, 2, P])
        pT = [pb(f"w_qT{n}", [P, 4, P], ctx) for n in range(2)]
        pY = pb("w_qY", [P, HM, V1], ctx)
        pO = pb("w_qO", [P, C], ctx)
        s_dve, s_ql, s_xl, s_q2, s_f, s_l, s_t, s_tc, s_y, s_yo, s_yt, s_yc, s_o, s_or, s_res, s_st, s_f16 = [sem("q_" + n) for n in (
            "dve", "loaded", "x_loaded", "doubled", "products", "linear", "T", "T_copied", "y", "y_divided", "yT",
            "yT_copied", "projected", "projection_read", "result", "stored", "products_16")]
        GR = CH // 4
        TURN = [3, 6, 8, 11, 13, 16, 18, 20, 22]
        LAG = 4
        with nc.Block() as block:
            @block.sync
            def _(sp):
                sp.sem_inc(s_q2, 1)
                sp.sem_inc(s_res, 1)
                sp.sem_inc(s_st, 16)
                sp.dma_start(q[:, :], qtab[0:P, :]).then_inc(s_ql, 16)
                with sp.Fori(0, ROUNDS) as i:
                    sp.wait_ge(s_res, i + 1)
                    sp.dma_start(xt[:, :], xtab[bass.ds(i * P, P), :]).then_inc(s_xl, 16)
                    sp.wait_ge(s_q2, i + 2)
                    sp.dma_start(q[:, :], qtab[bass.ds(i * P + P, P), :]).then_inc(s_ql, 16)
                    sp.wait_ge(s_res, i + 2)
                    sp.dma_start(xtab[bass.ds(i * P, P), :], res[:, :]).then_inc(s_st, 16)
                sp.wait_ge(s_st, 16 + ROUNDS * 16)
                sp.wait_ge(s_ql, 16 + ROUNDS * 16)

            @block.gpsimd
            def _(pool):
                with pool.Fori(0, ROUNDS * ROUND // RING) as i:
                    for half in range(2):
                        gated(pool, "pool", s_gs, i * RING + HALF * (half + 1))
                        pool.tensor_copy(idx[:, half, :], T["src_of"][:, bass.ds(i * RING + HALF * half, HALF)]).then_inc(s_idx, 1)
                        gated(pool, "pool", s_idx, i * 2 + (half + 1))
                        for k in range(HALF):
                            n = HALF * half + k
                            pool.indirect_dma_start(G[n][:, :], None, ztab, bass.IndirectOffsetOnAxis(
                                ap=idx[:, half, k:k + 1], axis=0)).then_inc(s_row[n], 16)

            @block.scalar
            def _(act):
                act.sem_inc(s_gs, RING)
                act.sem_inc(s_f, 4)
                act.sem_inc(s_f16, 1)
                with act.Fori(0, ROUNDS) as i:
                    for n in range(ROUND):
                        if n == 0:
                            act.wait_ge(s_ql, i * 16 + 16)
                            gated(act, "act", s_f, i * 4 + 4)
                            gated(act, "act", s_f16, i + 1)
                            for half in range(2):
                                ins = act.copy(q2[:, :, DM * half:DM * half + DM], q[:, :].rearrange("p (h d) -> p h d", h=HM))
                            ins.then_inc(s_q2, 1)
                            gated(act, "act", s_q2, i + 2)
                            gated(act, "act", s_t, i * GR + GR)
                            act.copy(QF[:, HM * MAIN + HM * DM:FEAT].rearrange("p (h i) -> p h i", h=HM),
                                     q2[:, :, 0:DM]).then_inc(s_l, 1)
                        m = n % RING
                        if n % HALF == 0:
                            gated(act, "act", s_mm, i * ROUND + (n + HALF))
                        gated(act, "act", s_row[m], i * 32 + (n // RING * 16 + 16))
                        act.activation(GS[:, m, 0:C], G[m][:, :], ACT.Copy,
                                       scale=T["ex"][:, bass.ds(i * ROUND + n, 1), 0]).then_inc(s_gs, 1)
                        if n - LAG in TURN:
                            g = TURN.index(n - LAG)
                            act.wait_ge(s_t, i * GR + (GR + g + 1))
                            act.copy(QT[:, g % 3, :, :], pT[g % 2][:, :, :]).then_inc(s_tc, 1)
                        if n == ROUND - 2:
                            act.wait_ge(s_yt, i + 2)
                            act.copy(yT[:, :, :].rearrange("p a c -> p (a c)"), pO[:, :]).then_inc(s_yc, 1)

            @block.tensor
            def _(pe):
                pe.sem_inc(s_mm, RING)
                pe.sem_inc(s_t, GR)
                pe.sem_inc(s_tc, 2)
                pe.sem_inc(s_yo, 1)
                pe.sem_inc(s_yt, 1)
                pe.sem_inc(s_or, 1)

                def turn(i, g):
                    pe.wait_ge(s_tc, i * GR + (2 if g == 0 else g + 1))
                    for c in range(4 * g, 4 * g + 4):
                        mm = pe.transpose(pT[g % 2][:, c % 4, :], QF[:, c * P:(c + 1) * P], ident[:, :])
                    mm.then_inc(s_t, 1)

                def y_chunk(i, g):
                    flat = pY[:, :, :].rearrange("p h e -> p (h e)")
                    if g == 0:
                        pe.wait_ge(s_yo, i + 1)
                        pe.matmul(flat, ident[:, :], VS[:, :], start=True, stop=False, skip_group_check=True)
                    pe.wait_ge(s_tc, i * GR + (g + 3))
                    for c in range(4 * g, 4 * g + 4):
                        if c < QUADS:
                            h, nh, rhs = c // 4, 1, KVS[:, c, :]
                        else:
                            h, nh, rhs = 4 * (c % 2), 4, KV4[:, c - QUADS, :]
                        mm = pe.matmul(flat[:, h * V1:(h + nh) * V1], QT[:, g % 3, c % 4, :], rhs, start=False,
                                       stop=c == CH - 1, skip_group_check=True)
                    if g == GR - 1:
                        mm.then_inc(s_y, 1)

                with pe.Fori(0, ROUNDS) as i:
                    for n in range(ROUND):
                        m = n % RING
                        if n % HALF == 0:
                            gated(pe, "pe", s_oh, i * (2 * ROUND // HALF) + (2 * (n // HALF) + 2))
                        gated(pe, "pe", s_add, i * ROUND + (n + 1))
                        pe.wait_ge(s_gs, i * ROUND + (RING + n + 1))
                        pe.matmul(ps[n % NB][:, :], OH[:, m, :], GS[:, m, :], start=True, stop=True).then_inc(s_mm, 1)
                        if n in TURN:
                            g = TURN.index(n)
                            if g % 2 == 0 and g < 8:
                                gated(pe, "pe", s_f, i * 4 + (g // 2 + 5))
                            if g == 8:
                                gated(pe, "pe", s_f16, i + 2)
                                gated(pe, "pe", s_l, i + 1)
                            turn(i, g)
                        if n - LAG in TURN:
                            y_chunk(i, TURN.index(n - LAG))
                        if n == ROUND - 3:
                            pe.wait_ge(s_yo, i + 2)
                            gated(pe, "pe", s_or, i + 1)
                            for c in range(2):
                                mm = pe.transpose(pO[:, c * P:c * P + P], yo[:, c * P:c * P + P], ident[:, :])
                            mm.then_inc(s_yt, 1)
                        if n == ROUND - 1:
                            pe.wait_ge(s_yc, i + 1)
                            for c in range(2):
                                mm = pe.matmul(pO[:, :], yT[:, c, :], wproj[:, c, :], start=c == 0, stop=c == 1)
                            mm.then_inc(s_o, 1)

            @block.vector
            def _(dve):
                ch = Count(dve, s_dve)
                body = acc[:, :, 0:C + H]
                dve.memset(body, 0.0).then_inc(s_z, 1)
                dve.sem_inc(s_add, NB)

                match = lambda at, half: match_half(dve, s_mm, s_oh, OH, GS, iota[:, :], T, H, at, half)
                def query_features(i, part):
                    if part == 0:
                        dve.wait_ge(s_q2, i + 2)
                        gated(dve, "dve", s_t, i * GR + GR)
                    features(dve, QF[:, 2 * part * MAIN:], q2[:, 2 * part:2 * part + 2, :], heads=2).then_inc(s_f, 1)
                    if part == 3:
                        dve.tensor_tensor(QF[:, HM * MAIN:HM * MAIN + HM * DM].rearrange("p (h i) -> p h i", h=HM),
                                          q2[:, :, 0:DM], q2[:, :, 16:16 + DM], ALU.mult).then_inc(s_f16, 1)

                def divide(i):
                    dve.wait_ge(s_y, i + 1)
                    gated(dve, "dve", s_yt, i + 1)
                    ch.link(dve.reciprocal(rec[:, :], pY[:, :, 0:1].rearrange("p h e -> p (h e)")))
                    dve.tensor_tensor(yo[:, :].rearrange("p (h d) -> p h d", h=HM), pY[:, :, 1:V1],
                                      bcast(rec[:, :], DM), ALU.mult).then_inc(s_yo, 1)

                def add_to_stream(i):
                    dve.wait_ge(s_o, i + 1)
                    dve.tensor_tensor(ot[:, :], pO[:, :], bsum[:, :], ALU.add).then_inc(s_or, 1)
                    gated(dve, "dve", s_or, i + 2)
                    gated(dve, "dve", s_xl, i * 16 + 16)
                    gated(dve, "dve", s_st, i * 16 + 16)
                    dve.tensor_tensor(res[:, :], xt[:, :], ot[:, :], ALU.add).then_inc(s_res, 1)

                match(0, 0)
                dve.wait_ge(s_z, 1)
                with dve.Fori(0, ROUNDS) as i:
                    ch.enter(i, 1)
                    for n in range(ROUND):
                        if n % HALF == 0:
                            match(i * ROUND, n // HALF + 1)
                        b = block_at(nc, T, i * ROUND + n)
                        gated(dve, "dve", s_mm, i * ROUND + (RING + n + 1))
                        to = acc[:, bass.ds(b, 1), 0:C + H].rearrange("p a c -> p (a c)")
                        dve.wait_ge(s_add, i * ROUND + (NB + n))
                        dve.tensor_tensor(to, to, ps[n % NB][:, :], ALU.add).then_inc(s_add, 1)
                        if n in (1, 4, 8, 12):
                            query_features(i, n // 4)
                        if n == ROUND - 5:
                            divide(i)
                        if n == ROUND - 1:
                            add_to_stream(i)
                    ch.leave(ROUNDS)


def divide_and_add(nc, sb, sem, acc, small, xtab):
    ctx = ExitStack()
    with ctx:
        parts = 5
        K = NT // parts
        xm = [sb(f"d_x{n}", [P, K, C], F32, at=ctx) for n in range(parts)]
        s_x = [sem(f"d_x_loaded{n}") for n in range(parts)]
        s_dve = sem("d_dve_b")
        with nc.Block() as block:
            @block.sync
            def _(sp):
                for n in range(parts):
                    sp.dma_start(xm[n][:, :, :], xtab[n * K * P:(n + 1) * K * P, :].rearrange(
                        "(k p) c -> p k c", p=P)).then_inc(s_x[n], 16)

            @block.vector
            def _(dve):
                ch = Count(dve, s_dve)
                ch.link(dve.tensor_scalar(small[:, :, 0:1], acc[:, :, C:C + 1], 1.0e-30, None, ALU.max))
                ch.link(dve.reciprocal(small[:, :, 0:1], small[:, :, 0:1]))
                for n in range(parts):
                    part = acc[:, n * K:(n + 1) * K, 0:C]
                    ch.link(dve.tensor_tensor(part, part, bcast(small[:, n * K:(n + 1) * K, 0], C), ALU.mult))
                    dve.wait_ge(s_x[n], 16)
                    ch.link(dve.tensor_tensor(part, part, xm[n][:, :, :], ALU.add))


def second_projection(nc, sb, pb, sem, gated, ident, acc, small, bias, elr, ztab, W2, al2, ar2):
    ctx = ExitStack()
    with ctx:
        sem = ctx.enter_context(phase_semaphores(nc))
        t = lambda name, shape: sb(name, shape, F32, at=ctx)
        wz, avec, prod = t("z_w", [P, 2, C + 2]), t("z_a", [P, 2, C]), t("z_prod", [P, C])
        xs, xT, zs = t("z_xs", [P, 2, C]), t("z_xT", [P, 2, 2, P]), t("z_zs", [P, 2, C])
        pT = [pb(f"z_pT{n}", [P, 2, P], ctx) for n in range(2)]
        pZ = [pb(f"z_pZ{n}", [P, C + 2], ctx) for n in range(2)]
        s_w, s_dve, s_xs, s_t, s_xt, s_z, s_zc, s_e = [sem("z_" + n) for n in (
            "w", "dve", "xs", "T", "xT", "mm", "copied", "elr")]
        s_h = sem("z_hidden")
        s_zd = [sem(f"z_stored{u}") for u in range(2)]
        with nc.Block() as block:
            @block.sync
            def _(sp):
                sp.dma_start(wz[:, :, 0:C], W2.rearrange("(a p) n -> p a n", p=P)).then_inc(s_w, 16)
                sp.dma_start(avec[:, 0, :], al2.rearrange("h d -> (h d)").partition_broadcast(P)).then_inc(s_w, 16)
                sp.dma_start(avec[:, 1, :], ar2.rearrange("h d -> (h d)").partition_broadcast(P)).then_inc(s_w, 16)
                with sp.Fori(0, PAIRS) as i:
                    for u in range(2):
                        sp.wait_ge(s_zc, i * 2 + (u + 1))
                        sp.dma_start(ztab[bass.ds(i * (2 * P) + u * P, P), :], zs[:, u, :]).then_inc(s_zd[u], 16)
                for u in range(2):
                    sp.wait_ge(s_zd[u], 16 + PAIRS * 16)

            @block.vector
            def _(dve):
                ch = Count(dve, s_dve)
                dve.wait_ge(s_w, 48)
                for c in range(2):
                    for side in range(2):
                        ch.link(dve.tensor_tensor(prod[:, :], wz[:, c, 0:C], avec[:, side, :], ALU.mult))
                        ch.link(dve.tensor_reduce(wz[:, c, C + side:C + side + 1], prod[:, :], AX_X, ALU.add))
                ch.link(dve.tensor_scalar(small[:, :, :], acc[:, :, C:C + 2], 1.0e-30, None, ALU.max))
                ch.link(dve.reciprocal(small[:, :, :], small[:, :, :]))

                def hidden(j, u):
                    gated(dve, "dve", s_t, j + 1)
                    for h in range(2):
                        part = slice(h * (C // 2), (h + 1) * (C // 2))
                        dve.scalar_tensor_tensor(out=xs[:, u, part], in0=acc[:, bass.ds(j, 1), part].rearrange("p a c -> p (a c)"),
                                                 scalar=small[:, bass.ds(j, 1), h], in1=bias[:, part],
                                                 op0=ALU.mult, op1=ALU.add).then_inc(s_h, 1)
                    dve.wait_ge(s_h, j * 2 + 2)
                    dve.tensor_scalar(xs[:, u, :], xs[:, u, :], 0.0, None, ALU.max).then_inc(s_xs, 1)

                def terms(j, u):
                    dve.wait_ge(s_zc, j + 1)
                    dve.tensor_scalar(elr[:, bass.ds(j, 1), 0:2].rearrange("p a c -> p (a c)"),
                                      pZ[u][:, C:C + 2], 1.0, None, ALU.mult).then_inc(s_e, 1)

                hidden(0, 0)
                hidden(1, 1)
                with dve.Fori(0, PAIRS - 1) as i:
                    for u in range(2):
                        hidden(i * 2 + (2 + u), u)
                        terms(i * 2 + u, u)
                terms(NT - 2, 0)
                terms(NT - 1, 1)

            @block.tensor
            def _(pe):
                pe.sem_inc(s_t, 2)
                pe.sem_inc(s_e, 2)
                pe.wait_ge(s_dve, 8)

                def turn(j, u):
                    pe.wait_ge(s_xs, j + 1)
                    for c in range(2):
                        mm = pe.transpose(pT[u][:, c, :], xs[:, u, c * P:c * P + P], ident[:, :])
                    mm.then_inc(s_t, 1)

                def project(j, u):
                    pe.wait_ge(s_xt, j + 1)
                    gated(pe, "pe", s_e, j + 1)
                    for c in range(2):
                        mm = pe.matmul(pZ[u][:, :], xT[:, u, c, :], wz[:, c, :], start=c == 0, stop=c == 1)
                    mm.then_inc(s_z, 1)

                turn(0, 0)
                with pe.Fori(0, PAIRS - 1) as i:
                    for u in range(2):
                        turn(i * 2 + (u + 1), 1 - u)
                        project(i * 2 + u, u)
                turn(NT - 1, 1)
                project(NT - 2, 0)
                project(NT - 1, 1)

            @block.scalar
            def _(act):
                for u in range(2):
                    act.sem_inc(s_zd[u], 16)

                def transposed(j, u):
                    act.wait_ge(s_t, j + 3)
                    act.copy(xT[:, u, :, :], pT[u][:, :, :]).then_inc(s_xt, 1)

                def z_out(j, pair, u):
                    act.wait_ge(s_z, j + 1)
                    gated(act, "act", s_zd[u], pair * 16 + 16)
                    act.copy(zs[:, u, :], pZ[u][:, 0:C]).then_inc(s_zc, 1)

                transposed(0, 0)
                with act.Fori(0, PAIRS - 1) as i:
                    for u in range(2):
                        transposed(i * 2 + (u + 1), 1 - u)
                        z_out(i * 2 + u, i, u)
                transposed(NT - 1, 1)
                z_out(NT - 2, PAIRS - 1, 0)
                z_out(NT - 1, PAIRS - 1, 1)


def attention_layers(nc, sb, pb, sem, dram, gated, ident, iota, acc, elr, ztab, qtab, xtab, mix, src, dst, b1, W2, al2, ar2):
    ctx = ExitStack()
    with ctx:
        sem = ctx.enter_context(phase_semaphores(nc))
        t = lambda name, shape, dt=F32: sb(name, shape, dt, at=ctx)
        D = {"src_lo": dram("src_lo_d", (P * COLS,), BF16), "er1": dram("er1", (P * COLS, 1), F32),
             "er2": dram("er2", (P * COLS, 2), F32), "terms": dram("terms", (NT * P, 4), F32), "last": dram("last", (COLS,), F32),
             "src": dram("src_f", (P * COLS,), F32), "dst": dram("dst_f", (P * COLS,), F32),
             "window": dram("window", (P * COLS + 2,), F32), "keys": dram("keys", (COLS,), F32),
             "block_of": dram("block_of_d", (COLS,), I32),
             "ex": [dram(f"ex{h}", (P * COLS,), F32) for h in range(2)]}
        T = {"node": t("node", [P, NT]), "row_tile": t("row_tile", [P, NT], I32), "first_edge": t("first_edge", [P, NT], I32),
             "first_dst": t("first_dst", [P, 1], I32), "chain": t("chain", [P, 2]),
             "tile_of": t("tile_of", [P, JT], I32), "first_node": t("first_node", [P, JT]),
             "src_of": t("src_of", [P, COLS], I32), "dst_of": t("dst_of", [P, COLS]),
             "block_of": t("block_of", [1, COLS], I32), "ex": t("ex", [P, COLS, 2])}
        bias = t("gat_bias", [P, C])
        small = t("small", [P, NT, 2])
        scans = ctx.enter_context(ExitStack())
        for name in ("src_hi", "same", "starts", "ends"):
            T[name] = sb(name, [P, COLS], F32, at=scans)
        c0 = ExitStack()
        with c0:
            T["edge_no"] = sb("edge_no", [P, COLS], I32, at=c0)
            node_i = sb("node_i", [P, NT], I32, at=c0)
            s_i, s_b = sem("i_edge"), sem("i_bias")
            with nc.Block() as block:
                @block.gpsimd
                def _(pool):
                    pool.iota(T["edge_no"][:, :], pattern=[[1, COLS]], base=0, channel_multiplier=COLS).then_inc(s_i, 1)
                    pool.iota(node_i[:, :], pattern=[[P, NT]], base=0, channel_multiplier=1).then_inc(s_i, 1)
                    pool.wait_ge(s_i, 2)
                    pool.tensor_copy(T["node"][:, :], node_i[:, :]).then_inc(s_i, 1)

                @block.sync
                def _(sp):
                    sp.dma_start(bias[:, :], b1.rearrange("h d -> (h d)").partition_broadcast(P)).then_inc(s_b, 16)
                    sp.wait_ge(s_b, 16)
            prepare_edges(nc, sb, pb, sem, ident, src, dst, D, T)
        edge_softmax(nc, sb, pb, sem, gated, ident, iota, elr, 2, D, T, 2, "a")
        gather_and_sum(nc, sb, pb, sem, gated, iota, ztab, acc, T, 2, "a")
        second_projection(nc, sb, pb, sem, gated, ident, acc, small, bias, elr, ztab, W2, al2, ar2)
        edge_softmax(nc, sb, pb, sem, gated, ident, iota, elr, 1, D, T, 1, "b")
        scans.close()
        gather_and_mix(nc, sb, pb, sem, gated, ident, iota, ztab, qtab, xtab, mix, acc, T)
        divide_and_add(nc, sb, sem, acc, small, xtab)


def experts(nc, sb, pb, sem, gated, ident, X, out, Wr, br, fW1, fb1, fg1, fbe1, fm1, fv1,
            fW2, fb2, fg2, fbe2, fm2, fv2, fWo, fbo):
    ctx = ExitStack()
    with ctx:
        sem = ctx.enter_context(phase_semaphores(nc))
        t = lambda name, shape, dt=F32: sb(name, shape, dt, at=ctx)
        st = t("f_stats", [P, NT, 6])
        mean, var, rs = t("f_mean", [P, NT]), t("f_var", [P, NT]), t("f_rs", [P, NT])
        w1, w2, wo = [t(n, [P, NX, 2, C]) for n in ("f_w1", "f_w2", "f_wo")]
        wr = t("f_wr", [P, 2, NX])
        brb = t("f_br", [P, NX])
        bo = t("f_bo", [NX, C])
        pn = t("f_pn", [80, 2, P])
        par = t("f_par", [P, 2, 5, 16])
        root = t("f_root", [P, 2, 16])
        mul, add = t("f_mul", [P, 2, 16]), t("f_add", [P, 2, 16])
        xs = t("f_xs", [P, 2, C])
        xT = t("f_xT", [P, 2, 2 * P])
        h1, h2 = t("f_h1", [P, 2, 2, 2 * P]), t("f_h2", [P, 2, 2, 2 * P])
        lg, wt, m2 = t("f_lg", [P, 2, NX]), t("f_wt", [P, 2, NX]), t("f_m2", [P, 2])
        wT = t("f_wT", [NX, 2, P])
        pH1 = [pb(f"f_pH1{n}", [P, 2, 2 * P], ctx) for n in range(2)]
        pH2 = [pb(f"f_pH2{n}", [P, 2, 2 * P], ctx) for n in range(2)]
        pY = [pb(f"f_pY{n}", [P, 2, C], ctx) for n in range(2)]
        pT = pb("f_pT", [P, 2, 2 * P], ctx)
        pR = pb("f_pR", [P, 512], ctx)
        names = ("loaded par parT par_read dve root bn xs T xT logits wlog exp weights wT wT_copied bo_sum bo_read "
                 "h1 a1 h2 a2 y y_read").split()
        (s_ld, s_par, s_pt, s_pr, s_dve, s_root, s_bn, s_xs, s_t, s_xt, s_lg, s_wl, s_ex, s_w, s_wT, s_wc, s_b, s_br,
         s_h1, s_a1, s_h2, s_a2, s_y, s_yr) = [sem("f_" + n) for n in names]
        s_done, s_out, s_st, s_var, s_vroot = sem("f_done"), sem("f_out"), sem("f_statistics"), sem("f_var"), sem("f_var_root")
        with nc.Block() as block:
            @block.sync
            def _(sp):
                for n, stack in enumerate(((fb1, fg1, fbe1, fm1, fv1), (fb2, fg2, fbe2, fm2, fv2))):
                    for a, p in enumerate(stack):
                        sp.dma_start(pn[16 * a:16 * a + 16, n, :], p.rearrange("e (c p) -> (e c) p", p=P)).then_inc(s_par, 16)
                sp.dma_start(wr[:, :, :], Wr.rearrange("(a p) e -> p a e", p=P)).then_inc(s_ld, 16)
                sp.dma_start(brb[:, :], br.partition_broadcast(P)).then_inc(s_ld, 16)
                sp.dma_start(bo[:, :], fbo).then_inc(s_ld, 16)
                for to, w in ((w1, fW1), (w2, fW2), (wo, fWo)):
                    for e in range(NX):
                        sp.dma_start(to[:, e, :, :], w[e].rearrange("(a p) n -> p a n", p=P)).then_inc(s_ld, 16)
                with sp.Fori(0, PAIRS - 1) as i:
                    sp.wait_ge(s_done, i + 1)
                    rows = out[bass.ds(i * (2 * P), 2 * P), :].rearrange("(k p) c -> p k c", p=P)
                    sp.dma_start(rows, X[:, bass.ds(i * 2, 2), :]).then_inc(s_out, 16)
                sp.wait_ge(s_done, PAIRS)
                sp.dma_start(out[FULL * P:N, :], X[0:REST, FULL, :]).then_inc(s_out, 16)
                sp.wait_ge(s_out, PAIRS * 16)

            @block.vector
            def _(dve):
                ch = Count(dve, s_dve)
                tile_statistics(dve, X, st, 0, NT, s_st)
                dve.wait_ge(s_st, NT)
                mean_and_variance(dve, ch, st, mean, rs)
                dve.sem_inc(s_var, 1)
                dve.wait_ge(s_vroot, 1)
                ch.link(dve.reciprocal(rs[:, :], var[:, :]))
                for n in range(2):
                    dve.wait_ge(s_pt, n + 1)
                    dve.tensor_copy(par[:, n, :, :].rearrange("p a b -> p (a b)"), pR[:, 0:80]).then_inc(s_pr, 1)
                dve.wait_ge(s_pr, 2)
                ch.link(dve.tensor_scalar(root[:, :, :], par[:, :, 4, :], EPS_BN, None, ALU.add))
                dve.sem_inc(s_bn, 1)
                dve.wait_ge(s_root, 1)
                ch.link(dve.reciprocal(root[:, :, :], root[:, :, :]))
                ch.link(dve.tensor_tensor(mul[:, :, :], par[:, :, 1, :], root[:, :, :], ALU.mult))
                ch.link(dve.tensor_tensor(add[:, :, :], par[:, :, 0, :], par[:, :, 3, :], ALU.subtract))
                ch.link(dve.tensor_tensor(add[:, :, :], add[:, :, :], mul[:, :, :], ALU.mult))
                ch.link(dve.tensor_tensor(add[:, :, :], add[:, :, :], par[:, :, 2, :], ALU.add))
                dve.sem_inc(s_bn, 1)
                dve.wait_ge(s_ld, 27 * 16)

                def normalised(i):
                    gated(dve, "dve", s_xt, i + 1)
                    for u in range(2):
                        ch.link(dve.tensor_scalar(xs[:, u, :], X[:, bass.ds(i * 2 + u, 1), :].rearrange("p a c -> p (a c)"),
                                                  mean[:, bass.ds(i * 2 + u, 1)], rs[:, bass.ds(i * 2 + u, 1)],
                                                  ALU.subtract, ALU.mult))
                    dve.sem_inc(s_xs, 1)

                def add_output(i, e):
                    dve.wait_ge(s_y, i * NX + (e + 3))
                    for u in range(2):
                        xk = X[:, bass.ds(i * 2 + u, 1), :].rearrange("p a c -> p (a c)")
                        ch.inc(dve.scalar_tensor_tensor(out=xk, in0=pY[e % 2][:, u, :], scalar=wt[:, u, e:e + 1], in1=xk,
                                                        op0=ALU.mult, op1=ALU.add))
                    ch.wait()
                    dve.sem_inc(s_yr, 1)

                def pair(i, first=False, last=False):
                    if not first:
                        add_output(i + (-1), NX - 2)
                    dve.wait_ge(s_lg, i + 1)
                    b = brb[:, :]
                    ch.link(dve.tensor_tensor(lg[:, :, :], pR[:, 0:2 * NX].rearrange("p (u e) -> p u e", u=2),
                                              bass.AP(b.tensor, b.offset, [list(b.ap[0]), [0, 2], [1, NX]]), ALU.add))
                    ch.link(dve.tensor_reduce(m2[:, :], lg[:, :, :], AX_X, ALU.max))
                    ch.link(dve.tensor_tensor(lg[:, :, :], lg[:, :, :], bcast(m2[:, :], NX), ALU.subtract))
                    dve.sem_inc(s_wl, 1)
                    if not first:
                        add_output(i + (-1), NX - 1)
                        dve.sem_inc(s_done, 1)
                    dve.wait_ge(s_ex, i + 1)
                    ch.link(dve.tensor_reduce(m2[:, :], lg[:, :, :], AX_X, ALU.add))
                    ch.link(dve.reciprocal(m2[:, :], m2[:, :]))
                    ch.link(dve.tensor_tensor(wt[:, :, :], lg[:, :, :], bcast(m2[:, :], NX), ALU.mult))
                    dve.sem_inc(s_w, 1)
                    for e in range(NX - 2):
                        add_output(i, e)
                        if e == 1:
                            both = X[:, bass.ds(i * 2, 2), :]
                            dve.wait_ge(s_b, i + 1)
                            ch.link(dve.tensor_tensor(both, both, pT[:, :, :], ALU.add))
                            dve.sem_inc(s_br, 1)
                        if e == 2 and not last:
                            normalised(i + 1)

                dve.sem_inc(s_xt, 1)
                normalised(0)
                pair(0, first=True)
                with dve.Fori(1, PAIRS - 1) as i:
                    ch.enter(i + (-1), 2 + 6 + 1 + 2 * NX)
                    pair(i)
                ch.leave(PAIRS - 2)
                pair(PAIRS - 1, last=True)
                add_output(PAIRS - 1, NX - 2)
                add_output(PAIRS - 1, NX - 1)
                dve.sem_inc(s_done, 1)

            @block.scalar
            def _(act):
                act.wait_ge(s_var, 1)
                act.activation(var[:, :], rs[:, :], ACT.Sqrt).then_inc(s_vroot, 1)
                act.wait_ge(s_bn, 1)
                act.activation(root[:, :, :], root[:, :, :], ACT.Sqrt).then_inc(s_root, 1)
                act.wait_ge(s_bn, 2)
                act.sem_inc(s_a1, 2)
                act.sem_inc(s_a2, 2)

                def relu(i, e, p, h, layer, ready, slot, done):
                    act.wait_ge(ready, i * NX + (e + 1 + 2 * layer))
                    gated(act, "act", slot, i * NX + (e + 1))
                    for c in range(2):
                        k = 2 * e + c
                        ins = act.activation(h[:, e % 2, c, :], p[e % 2][:, c, :], ACT.Relu, bias=add[:, layer, k:k + 1],
                                             scale=mul[:, layer, k:k + 1])
                    ins.then_inc(done, 1)

                def transposed(i):
                    act.wait_ge(s_t, i + 1)
                    act.copy(xT[:, :, :], pT[:, :, :]).then_inc(s_xt, 1)

                def pair(i, first=False, last=False):
                    for e in range(NX):
                        if e == NX - 1 and not last:
                            gated(act, "act", s_h1, i * NX + NX)
                            transposed(i + 1)
                        relu(i, e, pH1, h1, 0, s_h1, s_h2, s_a1)
                        if e:
                            relu(i, e - 1, pH2, h2, 1, s_h2, s_y, s_a2)
                        elif not first:
                            relu(i + (-1), NX - 1, pH2, h2, 1, s_h2, s_y, s_a2)
                        if e == 0:
                            act.wait_ge(s_wl, i + 1)
                            act.activation(lg[:, :, :], lg[:, :, :], ACT.Exp).then_inc(s_ex, 1)
                        if e == 2:
                            act.wait_ge(s_wT, i + 1)
                            act.copy(wT[:, :, :].rearrange("p u n -> p (u n)"), pR[0:NX, 256:512]).then_inc(s_wc, 1)

                transposed(0)
                pair(0, first=True)
                with act.Fori(1, PAIRS - 1) as i:
                    pair(i)
                pair(PAIRS - 1, last=True)
                relu(PAIRS - 1, NX - 1, pH2, h2, 1, s_h2, s_y, s_a2)

            @block.tensor
            def _(pe):
                pe.wait_ge(s_par, 160)
                for n in range(2):
                    if n:
                        pe.wait_ge(s_pr, n)
                    pe.transpose(pR[:, 0:80], pn[:, n, :], ident[0:80, 0:80]).then_inc(s_pt, 1)
                pe.wait_ge(s_ld, 27 * 16)
                pe.wait_ge(s_pr, 2)
                pe.sem_inc(s_h2, 2)
                pe.sem_inc(s_y, 2)
                pe.sem_inc(s_yr, 2)

                def layer(i, e, w, h_of, p, waits, done):
                    for s, v in waits:
                        gated(pe, "pe", s, v)
                    for m in range(2):
                        for c in range(2):
                            mm = pe.matmul(p[e % 2][:, m, :], w[:, e, c, m * P:m * P + P], h_of(c), start=c == 0, stop=c == 1)
                    mm.then_inc(done, 1)

                def turn(i):
                    gated(pe, "pe", s_xs, i + 1)
                    for c in range(2):
                        for u in range(2):
                            mm = pe.transpose(pT[:, c, u * P:u * P + P], xs[:, u, c * P:c * P + P], ident[:, :])
                    mm.then_inc(s_t, 1)

                def first_layer(i, e):
                    layer(i, e, w1, lambda c: xT[:, c, :], pH1, [(s_a1, i * NX + (e + 1))], s_h1)

                def second_layer(i, e):
                    layer(i, e, w2, lambda c: h1[:, e % 2, c, :], pH2, [(s_a1, i * NX + (e + 3)), (s_a2, i * NX + (e + 1))], s_h2)

                def output(i, e):
                    gated(pe, "pe", s_a2, i * NX + (e + 3))
                    gated(pe, "pe", s_yr, i * NX + (e + 1))
                    for u in range(2):
                        for c in range(2):
                            mm = pe.matmul(pY[e % 2][:, u, :], h2[:, e % 2, c, u * P:u * P + P], wo[:, e, c, :],
                                           start=c == 0, stop=c == 1)
                    mm.then_inc(s_y, 1)

                def pair(i, first=False, last=False):
                    for e in range(NX):
                        if e == 0:
                            gated(pe, "pe", s_xt, i + 2)
                        first_layer(i, e)
                        if e == 0:
                            for u in range(2):
                                for c in range(2):
                                    mm = pe.matmul(pR[:, u * NX:u * NX + NX], xT[:, c, u * P:u * P + P], wr[:, c, :],
                                                   start=c == 0, stop=c == 1)
                            mm.then_inc(s_lg, 1)
                        if e == 2:
                            gated(pe, "pe", s_w, i + 1)
                            for u in range(2):
                                mm = pe.transpose(pR[0:NX, 256 + u * P:256 + u * P + P], wt[:, u, :], ident[:, :])
                            mm.then_inc(s_wT, 1)
                        if e >= 1:
                            second_layer(i, e - 1)
                        elif not first:
                            second_layer(i + (-1), NX - 1)
                        if e == 3:
                            gated(pe, "pe", s_wc, i + 1)
                            for u in range(2):
                                mm = pe.matmul(pT[:, u, :], wT[:, u, :], bo[:, :], start=True, stop=True)
                            mm.then_inc(s_b, 1)
                        if e == 6 and not last:
                            gated(pe, "pe", s_br, i + 1)
                            turn(i + 1)
                        if e >= 2:
                            output(i, e - 2)
                        elif not first:
                            output(i + (-1), NX - 2 + e)

                turn(0)
                pair(0, first=True)
                with pe.Fori(1, PAIRS - 1) as i:
                    pair(i)
                pair(PAIRS - 1, last=True)
                second_layer(PAIRS - 1, NX - 1)
                output(PAIRS - 1, NX - 2)
                output(PAIRS - 1, NX - 1)


_INS = ['x', 'src', 'dst', 'L0_gnn_W1', 'L0_gnn_al1', 'L0_gnn_ar1', 'L0_gnn_b1', 'L0_gnn_W2', 'L0_gnn_al2', 'L0_gnn_ar2', 'L0_gnn_b2', 'L0_mix_Wqkv', 'L0_mix_bqkv', 'L0_mix_Wproj', 'L0_mix_bproj', 'L0_mix_temperature', 'L0_ffn_Wr', 'L0_ffn_br', 'L0_ffn_W1', 'L0_ffn_b1', 'L0_ffn_g1', 'L0_ffn_be1', 'L0_ffn_m1', 'L0_ffn_v1', 'L0_ffn_W2', 'L0_ffn_b2', 'L0_ffn_g2', 'L0_ffn_be2', 'L0_ffn_m2', 'L0_ffn_v2', 'L0_ffn_Wo', 'L0_ffn_bo']


def kernel(**inputs):
    import numpy as _np
    import concourse.bacc as _bacc
    from concourse import mybir as _mybir
    from concourse.bass_utils import run_bass_kernel_spmd as _run

    nc = _bacc.Bacc("TRN2", target_bir_lowering=False, num_devices=1)
    arrays, args = {}, []
    for name in _INS:
        a = _np.ascontiguousarray(inputs[name])
        arrays[f"in_{name}_dram"] = a
        args.append(nc.dram_tensor(f"in_{name}_dram", a.shape, _mybir.dt.from_np(a.dtype), kind="ExternalInput").ap())
    args.append(nc.dram_tensor("out_dram", (N, C), F32, kind="ExternalOutput").ap())
    build(nc, *args)
    r = _run(nc, [arrays], core_ids=[0])
    return r.results[0]["out_dram"]
```
